# Optimizing a Trainium2 kernel written in Bass

```python
import numpy as np
import jax
import jax.numpy as jnp

def _softmax(x, axis=-1):
    return jax.nn.softmax(x, axis=axis)

def _gelu(x):
    return jax.nn.gelu(x, approximate=True)

def _silu(x):
    return jax.nn.silu(x)

def _sigmoid(x):
    return jax.nn.sigmoid(x)

def _layernorm(x, axis=-1, eps=1e-05):
    m = jnp.mean(x, axis=axis, keepdims=True)
    v = jnp.var(x, axis=axis, keepdims=True)
    return (x - m) / jnp.sqrt(v + eps)

def _scatter_add(tgt, idx, src, axis=0):
    return tgt.at[idx].add(src)

def _segment_sum(src, seg, n):
    return jax.ops.segment_sum(src, seg, n)
kernel_name = 'mk_metaformer_d2_conv_nhwc1024_r4_0cff22'

def setup_inputs(seed: int=0):
    np.random.seed(seed)
    _w = jnp.asarray

    def _rec_inputs():
        import jax
        import jax.numpy as jnp
        _gk = jax.random.key(seed)
        x = -0.0002221 + 1 * jax.random.normal(jax.random.fold_in(_gk, 1), (4, 24, 16, 256), jnp.float32)
        return x
    x = _rec_inputs()

    def _L0_conv_setup():
        import jax, jax.numpy as jnp
        import numpy as np
        DIM = 256
        NUM_HEADS = 16
        HEAD_DIM = DIM // NUM_HEADS
        key = jax.random.key(seed)
        k_x, k_qkv, k_proj, k_b = jax.random.split(key, 4)
        B, N, P, C = (4, 24, 16, DIM)
        x = jax.random.normal(k_x, (B, N, P, C), dtype=jnp.float32)
        s = 1.0 / np.sqrt(C)
        W_qkv = jax.random.uniform(k_qkv, (C, 3 * C), minval=-s, maxval=s, dtype=jnp.float32)
        W_proj = jax.random.uniform(k_proj, (C, C), minval=-s, maxval=s, dtype=jnp.float32)
        b_proj = jax.random.uniform(k_b, (C,), minval=-s, maxval=s, dtype=jnp.float32)
        return {'x': x, 'W_qkv': W_qkv, 'W_proj': W_proj, 'b_proj': b_proj}
    _L0_conv_all = _L0_conv_setup()
    _L0_conv_in = {k: v for k, v in _L0_conv_all.items() if k in ('W_qkv', 'W_proj', 'b_proj')}
    del _L0_conv_all

    def _L0_ffn_setup():
        import jax, jax.numpy as jnp
        import numpy as np
        B, S, D, F, E, K = (4, 512, 256, 1024, 8, 2)
        key = jax.random.key(seed)
        ks = jax.random.split(key, 6)
        sc = 0.02
        return {'x': jax.random.normal(ks[0], (B, S, D), jnp.float32), 'gate_w': jax.random.normal(ks[1], (D, E), jnp.float32) * sc, 'gate_b': jnp.zeros((E,), jnp.float32), 'w1': jax.random.normal(ks[2], (E, D, F), jnp.float32) * sc, 'b1': jnp.zeros((E, F), jnp.float32), 'w2': jax.random.normal(ks[3], (E, F, D), jnp.float32) * sc, 'b2': jnp.zeros((E, D), jnp.float32)}
    _L0_ffn_all = _L0_ffn_setup()
    _L0_ffn_in = {k: v for k, v in _L0_ffn_all.items() if k in ('gate_w', 'gate_b', 'w1', 'b1', 'w2', 'b2')}
    del _L0_ffn_all

    def _L1_conv_setup():
        import jax, jax.numpy as jnp
        import numpy as np
        DIM = 256
        NUM_HEADS = 16
        HEAD_DIM = DIM // NUM_HEADS
        key = jax.random.key(seed)
        k_x, k_qkv, k_proj, k_b = jax.random.split(key, 4)
        B, N, P, C = (4, 24, 16, DIM)
        x = jax.random.normal(k_x, (B, N, P, C), dtype=jnp.float32)
        s = 1.0 / np.sqrt(C)
        W_qkv = jax.random.uniform(k_qkv, (C, 3 * C), minval=-s, maxval=s, dtype=jnp.float32)
        W_proj = jax.random.uniform(k_proj, (C, C), minval=-s, maxval=s, dtype=jnp.float32)
        b_proj = jax.random.uniform(k_b, (C,), minval=-s, maxval=s, dtype=jnp.float32)
        return {'x': x, 'W_qkv': W_qkv, 'W_proj': W_proj, 'b_proj': b_proj}
    _L1_conv_all = _L1_conv_setup()
    _L1_conv_in = {k: v for k, v in _L1_conv_all.items() if k in ('W_qkv', 'W_proj', 'b_proj')}
    del _L1_conv_all

    def _L1_ffn_setup():
        import jax, jax.numpy as jnp
        import numpy as np
        S, B, H = (512, 4, 256)
        I = 672
        E = 8
        TOP_K = 2
        key = jax.random.key(seed)
        ks = jax.random.split(key, 6)
        scale = 0.02
        return {'hidden_states': jax.random.normal(ks[0], (S, B, H), jnp.float32), 'router_w': jax.random.normal(ks[1], (H, E), jnp.float32) * scale, 'W1': jax.random.normal(ks[2], (E, H, 2 * I), jnp.float32) * scale, 'b1': jax.random.normal(ks[3], (E, 2 * I), jnp.float32) * scale, 'W2': jax.random.normal(ks[4], (E, I, H), jnp.float32) * scale, 'b2': jax.random.normal(ks[5], (E, H), jnp.float32) * scale}
    _L1_ffn_all = _L1_ffn_setup()
    _L1_ffn_in = {k: v for k, v in _L1_ffn_all.items() if k in ('router_w', 'W1', 'b1', 'W2', 'b2')}
    del _L1_ffn_all
    return {'x': x, 'L0_conv_W_qkv': _L0_conv_in['W_qkv'], 'L0_conv_W_proj': _L0_conv_in['W_proj'], 'L0_conv_b_proj': _L0_conv_in['b_proj'], 'L0_ffn_gate_w': _L0_ffn_in['gate_w'], 'L0_ffn_gate_b': _L0_ffn_in['gate_b'], 'L0_ffn_w1': _L0_ffn_in['w1'], 'L0_ffn_b1': _L0_ffn_in['b1'], 'L0_ffn_w2': _L0_ffn_in['w2'], 'L0_ffn_b2': _L0_ffn_in['b2'], 'L1_conv_W_qkv': _L1_conv_in['W_qkv'], 'L1_conv_W_proj': _L1_conv_in['W_proj'], 'L1_conv_b_proj': _L1_conv_in['b_proj'], 'L1_ffn_router_w': _L1_ffn_in['router_w'], 'L1_ffn_W1': _L1_ffn_in['W1'], 'L1_ffn_b1': _L1_ffn_in['b1'], 'L1_ffn_W2': _L1_ffn_in['W2'], 'L1_ffn_b2': _L1_ffn_in['b2']}

def reference(x, L0_conv_W_qkv, L0_conv_W_proj, L0_conv_b_proj, L0_ffn_gate_w, L0_ffn_gate_b, L0_ffn_w1, L0_ffn_b1, L0_ffn_w2, L0_ffn_b2, L1_conv_W_qkv, L1_conv_W_proj, L1_conv_b_proj, L1_ffn_router_w, L1_ffn_W1, L1_ffn_b1, L1_ffn_W2, L1_ffn_b2):
    import jax
    import jax.numpy as jnp

    def _L0_conv_ref(x, W_qkv, W_proj, b_proj):
        import jax, jax.numpy as jnp
        import numpy as np
        DIM = 256
        NUM_HEADS = 16
        HEAD_DIM = DIM // NUM_HEADS
        B, N, P, C = x.shape
        H, hd = (NUM_HEADS, C // NUM_HEADS)
        qkv = (x @ W_qkv).reshape(B, N, P, 3, H, hd)
        q = qkv[..., 0, :, :].mean(axis=2).transpose(0, 2, 1, 3)
        k = qkv[..., 1, :, :].mean(axis=2).transpose(0, 2, 1, 3)
        v = qkv[..., 2, :, :].transpose(0, 3, 1, 4, 2).reshape(B, H, N, hd * P)
        scores = jnp.einsum('bhnd,bhmd->bhnm', q, k) * hd ** (-0.5)
        attn = jax.nn.softmax(scores, axis=-1)
        out = jnp.einsum('bhnm,bhme->bhne', attn, v)
        out = out.reshape(B, H, N, hd, P).transpose(0, 2, 4, 1, 3).reshape(B, N, P, C)
        return out @ W_proj + b_proj

    def _L0_ffn_ref(x, gate_w, gate_b, w1, b1, w2, b2):
        import jax, jax.numpy as jnp
        import numpy as np
        B, S, D, F, E, K = (4, 512, 256, 1024, 8, 2)
        b, s, d = x.shape
        e = gate_w.shape[1]
        xf = x.reshape(-1, d)
        t = xf.shape[0]
        router = jax.nn.softmax(xf @ gate_w + gate_b, axis=-1)
        k_scores, k_idx = jax.lax.top_k(router, K)
        comb = jnp.zeros((t, e), x.dtype).at[jnp.arange(t)[:, None], k_idx].add(k_scores)
        out = jnp.zeros_like(xf)
        for i in range(e):
            h = jax.nn.silu(xf @ w1[i] + b1[i])
            y = h @ w2[i] + b2[i]
            out = out + y * comb[:, i:i + 1]
        return out.reshape(b, s, d)

    def _L1_conv_ref(x, W_qkv, W_proj, b_proj):
        import jax, jax.numpy as jnp
        import numpy as np
        DIM = 256
        NUM_HEADS = 16
        HEAD_DIM = DIM // NUM_HEADS
        B, N, P, C = x.shape
        H, hd = (NUM_HEADS, C // NUM_HEADS)
        qkv = (x @ W_qkv).reshape(B, N, P, 3, H, hd)
        q = qkv[..., 0, :, :].mean(axis=2).transpose(0, 2, 1, 3)
        k = qkv[..., 1, :, :].mean(axis=2).transpose(0, 2, 1, 3)
        v = qkv[..., 2, :, :].transpose(0, 3, 1, 4, 2).reshape(B, H, N, hd * P)
        scores = jnp.einsum('bhnd,bhmd->bhnm', q, k) * hd ** (-0.5)
        attn = jax.nn.softmax(scores, axis=-1)
        out = jnp.einsum('bhnm,bhme->bhne', attn, v)
        out = out.reshape(B, H, N, hd, P).transpose(0, 2, 4, 1, 3).reshape(B, N, P, C)
        return out @ W_proj + b_proj

    def _L1_ffn_ref(hidden_states, router_w, W1, b1, W2, b2):
        import jax, jax.numpy as jnp
        import numpy as np
        S, B, H = (512, 4, 256)
        I = 672
        E = 8
        TOP_K = 2
        s, b, n = hidden_states.shape
        x = hidden_states.reshape(-1, n)
        T = x.shape[0]
        route = (x.astype(jnp.float32) @ router_w).astype(x.dtype)
        w, sel = jax.lax.top_k(route, TOP_K)
        w = jax.nn.softmax(w.astype(jnp.float32), axis=-1).astype(x.dtype)
        cw = jnp.zeros((T, E), x.dtype).at[jnp.arange(T)[:, None], sel].add(w)
        out = jnp.zeros_like(x)
        for e in range(E):
            h = x @ W1[e] + b1[e]
            a, g = jnp.split(h, 2, axis=-1)
            act = a * jax.nn.silu(g)
            out = out + cw[:, e:e + 1] * (act @ W2[e] + b2[e])
        return out.reshape(s, b, n)

    def _gn(v, G=32, eps=1e-05):
        B_, H_, W_, C_ = v.shape
        g = v.reshape(B_, H_, W_, G, C_ // G)
        m = jnp.mean(g, axis=(1, 2, 4), keepdims=True)
        s = jnp.var(g, axis=(1, 2, 4), keepdims=True)
        return ((g - m) / jnp.sqrt(s + eps)).reshape(v.shape)

    def _ln_c(v, eps=1e-06):
        m = jnp.mean(v, axis=-1, keepdims=True)
        s = jnp.var(v, axis=-1, keepdims=True)
        return (v - m) / jnp.sqrt(s + eps)

    def _ln_t(v, eps=1e-05):
        m = jnp.mean(v, axis=-1, keepdims=True)
        s = jnp.var(v, axis=-1, keepdims=True)
        return (v - m) / jnp.sqrt(s + eps)

    def _to_tokens(v):
        B_, H_, W_, C_ = v.shape
        return v.reshape(B_, H_ * W_, C_)

    def _from_tokens(t, like):
        return t.reshape(like.shape)
    x = x + _L0_conv_ref(_ln_c(x), L0_conv_W_qkv, L0_conv_W_proj, L0_conv_b_proj)
    t = _to_tokens(x)
    t = t + _L0_ffn_ref(_ln_t(t), L0_ffn_gate_w, L0_ffn_gate_b, L0_ffn_w1, L0_ffn_b1, L0_ffn_w2, L0_ffn_b2)
    x = _from_tokens(t, x)
    x = x + _L1_conv_ref(_ln_c(x), L1_conv_W_qkv, L1_conv_W_proj, L1_conv_b_proj)
    t = _to_tokens(x)
    t = t + _L1_ffn_ref(_ln_t(t), L1_ffn_router_w, L1_ffn_W1, L1_ffn_b1, L1_ffn_W2, L1_ffn_b2)
    x = _from_tokens(t, x)
    return x

_drawn_inputs = setup_inputs


def setup_inputs(seed=0):
    import zlib

    import numpy as np

    out = dict(_drawn_inputs(seed))
    spreads = {'L0_ffn_gate_b': (0.0, 0.355), 'L0_ffn_b1': (0.0, 0.8), 'L0_ffn_b2': (0.0, 0.308)}
    factors = {'L1_ffn_router_w': 2.743,
     'L1_ffn_W1': 2.911,
     'L1_ffn_b1': 8.0,
     'L1_ffn_W2': 2.91,
     'L1_ffn_b2': 3.914}
    for name, (base, spread) in spreads.items():
        noise = np.random.default_rng([zlib.crc32(name.encode()), seed]).standard_normal(out[name].shape)
        drawn = base * np.exp(spread * noise) if base else spread * noise
        out[name] = jnp.asarray(drawn.astype(out[name].dtype))
    for name, factor in factors.items():
        out[name] = (out[name] * factor).astype(out[name].dtype)
    return out
```

```python
from contextlib import ExitStack

import concourse.bass as bass
from concourse import mybir

F32 = mybir.dt.float32
BF16 = mybir.dt.bfloat16
I32 = mybir.dt.int32
ALU = mybir.AluOpType
ACT = mybir.ActivationFunctionType
AX = mybir.AxisListType

P = 128
B, N, PIX, C = 4, 24, 16, 256
BN = B * N
TOKENS = B * N * PIX
TILES = TOKENS // P
KC = C // P
HEADS, HD = 16, 16
HPH = P // HD
GROUP = 4
HGROUPS = HEADS // GROUP
NPT = P // PIX
E, TOPK = 8, 2
PAIRS = TILES * TOPK
MAX_BLOCKS = (TOKENS * TOPK + E * (P - 1)) // P
NB = MAX_BLOCKS
TABLE = 32
assert NB <= TABLE
SLOTS = 7
NEG = -1.0e30
BIG_ROW = 4096

class Ffn:
    def __init__(self, wide, kt, kh, chunk):
        self.wide, self.kt, self.kh, self.chunk, self.chunks = wide, kt, kh, chunk, wide // chunk


FFN = [Ffn(wide=1024, kt=8, kh=128, chunk=512), Ffn(wide=1344, kt=6, kh=112, chunk=336)]
SLOT_WORDS = max(KC * f.wide + f.kt * C for f in FFN)
BIAS_WIDE = max(f.wide for f in FFN) + C
LN_EPS = (1e-6, 1e-5)


class LayerSems:

    def __init__(self, sem, L):
        self.x_in0 = sem(f"x_in0_{L}")
        self.x_in1 = sem(f"x_in1_{L}")
        self.x_in2 = sem(f"x_in2_{L}")
        self.conv_in = sem(f"conv_in_{L}")
        self.bias_in = sem(f"bias_in_{L}")
        self.route_in = sem(f"route_in_{L}")
        self.stat = sem(f"stat_{L}")
        self.var = sem(f"var_{L}")
        self.std = sem(f"std_{L}")
        self.xn = sem(f"xn_{L}")
        self.xnT_mm = sem(f"xnT_mm_{L}")
        self.xnT = sem(f"xnT_{L}")
        self.pool_mm = sem(f"pool_mm_{L}")
        self.xm = sem(f"xm_{L}")
        self.qk_mm = sem(f"qk_mm_{L}")
        self.k_sb = sem(f"k_sb_{L}")
        self.qm = sem(f"qm_{L}")
        self.s_mm = sem(f"s_mm_{L}")
        self.sub = sem(f"sub_{L}")
        self.expd = sem(f"expd_{L}")
        self.attn = sem(f"attn_{L}")
        self.bias_added = sem(f"bias_added_{L}")
        self.v_mm = sem(f"v_mm_{L}")
        self.v = sem(f"v_{L}")
        self.aT_mm = sem(f"aT_mm_{L}")
        self.aT = sem(f"aT_{L}")
        self.av_mm = sem(f"av_mm_{L}")
        self.o_act = sem(f"o_act_{L}")
        self.o_dve = sem(f"o_dve_{L}")
        self.oT_mm = sem(f"oT_mm_{L}")
        self.oT_act = sem(f"oT_act_{L}")
        self.oT_dve = sem(f"oT_dve_{L}")
        self.y_mm = sem(f"y_mm_{L}")
        self.x1 = sem(f"x1_{L}")
        self.var2 = sem(f"var2_{L}")
        self.std2 = sem(f"std2_{L}")
        self.xn2 = sem(f"xn2_{L}")
        self.xn2T_mm = sem(f"xn2T_mm_{L}")
        self.xn2T = sem(f"xn2T_{L}")
        self.lg_mm = sem(f"lg_mm_{L}")
        self.lg = sem(f"lg_{L}")
        self.chain = sem(f"chain_{L}")
        self.mtop = sem(f"mtop_{L}")
        self.exp8 = sem(f"exp8_{L}")
        self.picked = sem(f"picked_{L}")
        self.cnt_mm = sem(f"cnt_mm_{L}")
        self.hot = sem(f"hot_{L}")
        self.tab_mm = sem(f"tab_mm_{L}")
        self.tab = sem(f"tab_{L}")
        self.bias_ready = sem(f"bias_ready_{L}")
        self.bch = sem(f"bch_{L}")
        self.store = sem(f"store_{L}")
        self.gathered0 = sem(f"gathered0_{L}")
        self.gathered1 = sem(f"gathered1_{L}")
        self.gcol = sem(f"gcol_{L}")
        self.scol = sem(f"scol_{L}")
        self.xT_mm = sem(f"xT_mm_{L}")
        self.xT = sem(f"xT_{L}")
        self.h_mm = sem(f"h_mm_{L}")
        self.silu = sem(f"silu_{L}")
        self.h = sem(f"h_{L}")
        self.hT_mm = sem(f"hT_mm_{L}")
        self.hTa = sem(f"hTa_{L}")
        self.hTb = sem(f"hTb_{L}")
        self.e_mm = sem(f"e_mm_{L}")
        self.e_sb = sem(f"e_sb_{L}")
        self.added = sem(f"added_{L}")
        self.gather_go = sem(f"gather_go_{L}")
        self.scatter_go = sem(f"scatter_go_{L}")


def metaformer(nc, x, conv_w, ffn_w, out):
    with ExitStack() as ctx:
        def sb(name, shape, dt=F32):
            return ctx.enter_context(nc.sbuf_tensor(name, shape, dt))

        def sem(name):
            return ctx.enter_context(nc.semaphore(name))

        bank = [ctx.enter_context(nc.psum_tensor(f"bank{i}", [P, 512], F32)) for i in range(8)]

        weights = sb("weights", [P, SLOTS, SLOT_WORDS])
        xres = sb("xres", [P, TILES, C])
        region_a = sb("region_a", [P, 4096])
        region_b = sb("region_b", [P, KC * TOKENS])
        region_c = sb("region_c", [P, 4096])
        region_d = sb("region_d", [P, BIAS_WIDE])
        wqkv = sb("wqkv", [P, KC, 3 * C])
        wproj = sb("wproj", [P, KC, C])
        bproj = sb("bproj", [P, C])
        bias_rows = sb("bias_rows", [96, BIAS_WIDE], BF16)
        expert_sel = sb("expert_sel", [96, E, P], BF16)
        wroute = sb("wroute", [P, KC, E])
        broute = sb("broute", [P, E])

        xn = region_a[:, 0:TILES * C].rearrange("p (i c) -> p i c", i=TILES)
        probs = region_a[0:BN, 0:HEADS * BN].rearrange("p (h m) -> p h m", h=HEADS)
        qmask = region_a[:, 1536:1536 + HEADS * BN].rearrange("p (h n) -> p h n", h=HEADS)
        o_sb = region_a[0:BN, :].rearrange("p (q c) -> p q c", q=PIX)
        xnT = region_b[:, :].rearrange("p (k t) -> p k t", k=KC)
        outT = region_b[:, :].rearrange("p (k n q) -> p k n q", k=KC, q=PIX)
        v_sb = region_c[0:BN, :].rearrange("p (q c) -> p q c", q=PIX)
        attnT = region_d[0:BN, 0:HEADS * BN].rearrange("p (h n) -> p h n", h=HEADS)
        bias_raw = region_d[0:96, :]
        kT = sb("kT", [P, KC, BN])
        xm = sb("xm", [P, KC, BN])
        row_max = sb("row_max", [BN, HEADS])
        row_sum = sb("row_sum", [BN, HEADS])
        stats = sb("stats", [P, TILES, 6])
        mean_var = sb("mean_var", [P, TILES, 2])
        std = sb("std", [P, TILES])
        rstd = sb("rstd", [P, TILES])
        xn2 = region_c[:, 0:TILES * C].rearrange("p (i c) -> p i c", i=TILES)
        xn2T = region_a[:, 0:4 * 512].rearrange("p (r i k t) -> p r i k t", r=4, i=2, k=KC)
        onehot_row = region_b[:, :].rearrange("p (j r) -> p j r", j=PAIRS)
        onehot_blk = region_a[:, 2048:2048 + PAIRS * 2 * TABLE].rearrange("p (j v b) -> p j v b", j=PAIRS, v=2)
        logits = sb("logits", [P, TILES, E])
        lg2 = sb("lg2", [P, TILES, E])
        prob8 = sb("prob8", [P, TILES, E])
        cand = sb("cand", [P, TILES, E])
        m_top = sb("m_top", [P, TOPK, TILES])
        i_top = sb("i_top", [P, TOPK, TILES])
        pick = sb("pick", [P, TOPK, E, TILES])
        picked = sb("picked", [P, E, TILES], BF16)
        gate = sb("gate", [P, TOPK, TILES])
        small = sb("small", [P, 4, TILES])
        incl = sb("incl", [P, E, TILES])
        place = sb("place", [P, E, TILES])
        term = sb("term", [P, E, TILES])
        cnt_i = sb("cnt_i", [P, 2, E], I32)
        nblk = sb("nblk", [P, E])
        endblk = sb("endblk", [P, E])
        base = sb("base", [P, E])
        slot_f = sb("slot_f", [P, TOPK, TILES])
        slot_i = sb("slot_i", [P, 3, TOPK, TILES], I32)
        rowblk = sb("rowblk", [P, 2, PAIRS])
        blk_cmp = sb("blk_cmp", [1, TABLE, E])
        blk_e = sb("blk_e", [1, 3, TABLE])
        tab_e = sb("tab_e", [1, 2, TABLE], I32)
        tab_end = [sb(f"tab_end{L}", [1, E], I32) for L in range(2)]
        id_sb = sb("id_sb", [P, 2, TABLE])
        gather_tab = sb("gather_tab", [P, TABLE], I32)
        scatter_tab = sb("scatter_tab", [P, TABLE], I32)
        gate_tab = sb("gate_tab", [P, TABLE])
        h_sb = region_a[:, 0:1024]
        hT = region_a[:, 1024:2048].rearrange("p (k s) -> p k s", s=P)
        silu_g = region_a[:, 2048:2048 + 672]
        xT = region_a[:, 2720:2720 + 512].rearrange("p (a k s) -> p a k s", a=2, k=KC)
        xg = region_b[:, 0:512].rearrange("p (a c) -> p a c", a=2)
        y_sb = region_b[:, 512:1024].rearrange("p (a c) -> p a c", a=2)
        gcol = [sb(f"gcol{a}", [P, 1], I32) for a in range(2)]
        scol = [sb(f"scol{a}", [P, 1], I32) for a in range(2)]
        ident = sb("ident", [P, P])
        head_mask = sb("head_mask", [P, HPH])
        q_mask = sb("q_mask", [P, HPH])
        batch_mask = sb("batch_mask", [BN, B, N])
        tri = sb("tri", [P, P], BF16)
        ones = sb("ones", [P, P], BF16)
        iota_i = sb("iota_i", [P, P], I32)
        iota = sb("iota", [P, P])
        expert_m8 = sb("expert_m8", [P, E])
        token_i = sb("token_i", [P, TILES], I32)
        token_id = sb("token_id", [P, TILES])
        scan_keep = sb("scan_keep", [P, E, TILES])

        xn_dram = nc.dram_tensor("xn_dram", [TOKENS, C], F32).ap()
        mid_dram = nc.dram_tensor("mid_dram", [TOKENS, C], F32).ap()
        x_rows = x.rearrange("b n p c -> (b n p) c")
        out_rows = out.rearrange("b n p c -> (b n p) c")

        lay = [LayerSems(sem, L) for L in range(2)]
        const = sem("const")
        const_done = sem("const_done")
        w_dma = [sem(f"w_dma{i}") for i in range(2)]
        w_ready = sem("w_ready")

        block = ctx.enter_context(nc.Block())

        def register(b):
            return not isinstance(b, int)

        def col(tab, b):
            return tab[:, bass.ds(b, 1)] if register(b) else tab[:, b:b + 1]

        def block_loop(eng, step):
            for b in range(3):
                step(b, b % 2)
            with eng.Fori(0, (NB - 5) // 2) as i:
                step(i * 2 + 3, 1)
                step(i * 2 + 4, 0)
            for b in range(3 + (NB - 5) // 2 * 2, NB + 1):
                step(b, b % 2)

        def weight_views(L, slot):
            f = FFN[L]
            w1 = weights[:, slot, 0:KC * f.wide].rearrange("p (k n) -> p k n", k=KC)
            w2 = weights[0:f.kh, slot, KC * f.wide:KC * f.wide + f.kt * C].rearrange("p (k n) -> p k n", k=f.kt)
            return w1, w2

        @block.sync
        def _(sp):
            def load_x(L, src):
                v = src.rearrange("(i p) c -> p i c", p=P)
                for g, done in enumerate((lay[L].x_in0, lay[L].x_in1, lay[L].x_in2)):
                    sp.dma_start(xres[:, 4 * g:4 * g + 4, :], v[:, 4 * g:4 * g + 4, :]).then_inc(done, 16)

            def load_conv(L):
                w_qkv, w_proj, b_proj = conv_w[L]
                sp.dma_start(wqkv[:, :, :], w_qkv.rearrange("(k p) n -> p k n", p=P)).then_inc(lay[L].conv_in, 16)
                sp.dma_start(wproj[:, :, :], w_proj.rearrange("(k p) n -> p k n", p=P)).then_inc(lay[L].conv_in, 16)
                sp.dma_start(bproj[:, :], b_proj.partition_broadcast(P)).then_inc(lay[L].conv_in, 16)

            def load_route(L):
                router, router_b = ffn_w[L][0:2]
                sp.dma_start(wroute[:, :, :], router.rearrange("(k p) n -> p k n", p=P)).then_inc(lay[L].route_in, 16)
                if router_b is not None:
                    sp.dma_start(broute[:, :], router_b.partition_broadcast(P)).then_inc(lay[L].route_in, 16)

            def load_expert(g):
                L, e = g // E, g % E
                w1, w2 = weight_views(L, g % SLOTS)
                sp.dma_start(w1, ffn_w[L][2][e].rearrange("(k p) n -> p k n", p=P)).then_inc(w_dma[g % 2], 16)
                sp.dma_start(w2, ffn_w[L][4][e].rearrange("(k p) n -> p k n", p=FFN[L].kh)).then_inc(w_dma[g % 2], 16)

            def expert_loaded(g):
                sp.wait_ge(w_dma[g % 2], 32 * (g // 2 + 1))
                sp.sem_inc(w_ready, 1)

            def expert_free(g):
                L, e = (g - SLOTS) // E, (g - SLOTS) % E
                last = sp.value_load(tab_end[L][0:1, e:e + 1], min_val=1, max_val=NB)
                sp.wait_ge(lay[L].e_mm, last)

            load_x(0, x_rows)
            load_conv(0)
            load_route(0)
            for g in range(SLOTS):
                load_expert(g)
                if g:
                    expert_loaded(g - 1)
            sp.wait_ge(lay[0].y_mm, 6)
            sp.wait_ge(lay[0].bias_added, 1)
            load_conv(1)
            sp.wait_ge(lay[0].lg_mm, 1)
            sp.wait_ge(lay[0].lg, 1)
            load_route(1)
            sp.wait_ge(lay[0].tab, 1)
            for g in range(SLOTS, 2 * E - 1):
                expert_free(g)
                load_expert(g)
                expert_loaded(g - 1)
            sp.wait_ge(lay[0].added, 16 * NB)
            load_x(1, mid_dram)
            expert_loaded(2 * E - 2)
            sp.wait_ge(lay[1].tab, 1)
            expert_free(2 * E - 1)
            load_expert(2 * E - 1)
            expert_loaded(2 * E - 1)
            sp.wait_ge(lay[1].added, 16 * NB)

        @block.gpsimd
        def _(pool):
            cc = [0]

            def made(ins):
                cc[0] += 1
                ins.then_inc(const, 1)
                pool.wait_ge(const, cc[0])

            made(pool.memset(ident[:, :], 0.0))
            made(pool.affine_select(out=ident[:, :], in_=ident[:, :], compare_op=ALU.not_equal, fill=1.0, base=0,
                                    pattern=[[-1, P]], channel_multiplier=1))
            for tile, value in ((head_mask, 1.0 / PIX), (q_mask, float(HD) ** -0.5)):
                made(pool.memset(tile[:, :], value))
                made(pool.affine_select(out=tile[:, :], in_=tile[:, :], compare_op=ALU.is_ge, fill=0.0, base=0,
                                        pattern=[[-HD, HPH]], channel_multiplier=1))
                made(pool.affine_select(out=tile[:, :], in_=tile[:, :], compare_op=ALU.is_ge, fill=0.0, base=HD - 1,
                                        pattern=[[HD, HPH]], channel_multiplier=-1))
            made(pool.memset(batch_mask[:, :, :], 0.0))
            made(pool.affine_select(out=batch_mask[:, :, :], in_=batch_mask[:, :, :], compare_op=ALU.is_ge, fill=NEG,
                                    base=0, pattern=[[-N, B], [0, N]], channel_multiplier=1))
            made(pool.affine_select(out=batch_mask[:, :, :], in_=batch_mask[:, :, :], compare_op=ALU.is_ge, fill=NEG,
                                    base=N - 1, pattern=[[N, B], [0, N]], channel_multiplier=-1))
            pool.sem_inc(const_done, 1)

            def load_biases(L):
                s, f = lay[L], FFN[L]
                b1, b2 = ffn_w[L][3], ffn_w[L][5]
                if L == 1:
                    pool.wait_ge(lay[0].av_mm, HEADS // 2)
                made2(L, pool.memset(bias_raw[:, :], 0.0))
                for q in range(3):
                    pool.dma_start(bias_raw[32 * q:32 * q + E, 0:f.wide], b1).then_inc(s.bias_in, 16)
                    pool.dma_start(bias_raw[32 * q:32 * q + E, f.wide:f.wide + C], b2).then_inc(s.bias_in, 16)

            nb = [0, 0]

            def made2(L, ins):
                nb[L] += 1
                ins.then_inc(lay[L].bch, 1)
                pool.wait_ge(lay[L].bch, nb[L])

            def split_biases(L):
                s = lay[L]
                pool.wait_ge(s.bias_in, 6 * 16)
                if L == 1:
                    pool.wait_ge(lay[0].e_mm, NB)
                made2(L, pool.tensor_copy(bias_rows[:, :], bias_raw[:, :]))
                made2(L, pool.tensor_tensor(bias_raw[:, :], bias_raw[:, :], bias_rows[:, :], ALU.subtract))
                made2(L, pool.tensor_copy(bias_rows[32:64, :], bias_raw[32:64, :]))
                made2(L, pool.tensor_copy(bias_rows[64:96, :], bias_raw[64:96, :]))
                made2(L, pool.tensor_tensor(bias_raw[64:96, :], bias_raw[64:96, :], bias_rows[64:96, :], ALU.subtract))
                pool.tensor_copy(bias_rows[64:96, :], bias_raw[64:96, :]).then_inc(s.bias_ready, 1)
                pool.wait_ge(s.bias_ready, 1)

            load_biases(0)
            made(pool.memset(tri[:, :], 1.0))
            made(pool.affine_select(out=tri[:, :], in_=tri[:, :], compare_op=ALU.is_ge, fill=0.0, base=-1,
                                    pattern=[[1, P]], channel_multiplier=-1))
            made(pool.memset(ones[:, :], 1.0))
            made(pool.iota(iota_i[:, :], pattern=[[1, P]], base=0, channel_multiplier=0))
            made(pool.tensor_copy(iota[:, :], iota_i[:, :]))
            made(pool.tensor_scalar(expert_m8[:, :], iota[:, 0:E], float(E), None, ALU.subtract))
            made(pool.iota(token_i[:, :], pattern=[[P, TILES]], base=1, channel_multiplier=1))
            made(pool.tensor_copy(token_id[:, :], token_i[:, :]))
            made(pool.memset(scan_keep[:, :, :], 1.0))
            made(pool.memset(scan_keep[:, :, 0:1], 0.0))
            made(pool.memset(expert_sel[:, :, :], 0.0))
            for q in range(3):
                made(pool.affine_select(out=expert_sel[:, :, :], in_=expert_sel[:, :, :], compare_op=ALU.not_equal,
                                        fill=1.0, base=-32 * q, pattern=[[-1, E], [0, P]], channel_multiplier=1))
            pool.sem_inc(const_done, 1)

            for L in range(2):
                s = lay[L]
                dst = (mid_dram, out_rows)[L].rearrange("(i p) c -> p i c", p=P)
                xn_v = xn_dram.rearrange("(i p) c -> p i c", p=P)
                pool.wait_ge(s.conv_in, 48)
                pool.wait_ge(s.xn, TILES)
                pool.tensor_tensor(xres[:, :, :], xres[:, :, :], bproj[:, :].unsqueeze(1).to_broadcast([P, TILES, C]),
                                   ALU.add).then_inc(s.bias_added, 1)
                if L == 0:
                    split_biases(0)
                for g in range(3):
                    pool.wait_ge(s.xn2, 4 * (g + 1))
                    pool.dma_start(xn_v[:, 4 * g:4 * g + 4, :], xn2[:, 4 * g:4 * g + 4, :]).then_inc(s.store, 16)
                    pool.dma_start(dst[:, 4 * g:4 * g + 4, :], xres[:, 4 * g:4 * g + 4, :]).then_inc(s.store, 16)
                if L == 1:
                    load_biases(1)
                    split_biases(1)
                acc = (mid_dram, out_rows)[L]
                pool.wait_ge(s.store, 6 * 16)
                pool.wait_ge(s.tab, 1)

                def gather(b, par):
                    if register(b) or b >= 2:
                        pool.wait_ge(s.xT_mm, b - 1)
                        pool.wait_ge((s.gathered0, s.gathered1)[par], 16 * (b // 2))
                    pool.tensor_copy(gcol[par][:, :], col(gather_tab, b)).then_inc(s.gcol, 1)
                    pool.wait_ge(s.gcol, b + 1)
                    pool.sem_inc(s.gather_go, 1)
                    pool.indirect_dma_start(out=xg[:, par, :], out_offset=None, in_=xn_dram,
                                            in_offset=bass.IndirectOffsetOnAxis(ap=gcol[par][:, :], axis=0)
                                            ).then_inc((s.gathered0, s.gathered1)[par], 16)

                def scatter(b, par):
                    if register(b) or b >= 1:
                        pool.wait_ge(s.added, 16 * b)
                    pool.tensor_copy(scol[par][:, :], col(scatter_tab, b)).then_inc(s.scol, 1)
                    pool.wait_ge(s.scol, b + 1)
                    pool.wait_ge(s.e_sb, b + 1)
                    pool.sem_inc(s.scatter_go, 1)
                    pool.indirect_dma_start(out=acc, out_offset=bass.IndirectOffsetOnAxis(ap=scol[par][:, :], axis=0),
                                            in_=y_sb[:, par, :], in_offset=None, bounds_check=TOKENS - 1,
                                            oob_is_err=False, compute_op=ALU.add).then_inc(s.added, 16)

                gather(0, 0)
                gather(1, 1)

                def step(b, par):
                    if register(b) or b + 2 < NB:
                        gather(b + 2, par)
                    if register(b) or b >= 1:
                        scatter(b - 1, 1 - par)

                block_loop(pool, step)

        @block.scalar
        def _(act):
            for L in range(2):
                s, f = lay[L], FFN[L]

                def stds(var, done, eps):
                    for g in range(3):
                        act.wait_ge(var, 4 * (g + 1))
                        nc.scalar.activation(std[:, 4 * g:4 * g + 4], mean_var[:, 4 * g:4 * g + 4, 1], ACT.Sqrt
                                             ).then_inc(done, 1)

                stds(s.var, s.std, LN_EPS[0])
                for j in range(6):
                    act.wait_ge(s.xnT_mm, j + 1)
                    nc.scalar.copy(xnT[:, :, 2 * j * P:2 * (j + 1) * P].rearrange("p k (i t) -> p i k t", i=2),
                                   bank[j % 4][:, :].rearrange("p (i k t) -> p i k t", i=2, k=KC)).then_inc(s.xnT, 1)
                for j in range(8):
                    act.wait_ge(s.v_mm, j + 1)
                    if L == 1 and j == 0:
                        act.wait_ge(lay[0].store, 96)
                    nc.scalar.copy(v_sb[:, 2 * j:2 * j + 2, :],
                                   bank[6 + j % 2][0:BN, :].rearrange("p (q c) -> p q c", q=2)).then_inc(s.v, 1)
                    if j % 2 == 1:
                        g = j // 2
                        act.wait_ge(s.sub, g + 1)
                        nc.scalar.activation(probs[:, GROUP * g:GROUP * g + GROUP, :],
                                             probs[:, GROUP * g:GROUP * g + GROUP, :], ACT.Exp).then_inc(s.expd, 1)
                for g in range(HGROUPS):
                    act.wait_ge(s.aT_mm, g + 1)
                    if L == 0 and g == 0:
                        act.wait_ge(s.bias_ready, 1)
                    nc.scalar.copy(attnT[:, GROUP * g:GROUP * g + GROUP, :],
                                   bank[4 + g % 2][0:BN, 0:GROUP * BN].rearrange("p (h n) -> p h n", h=GROUP)
                                   ).then_inc(s.aT, 1)
                for j in range(0, 8, 2):
                    act.wait_ge(s.av_mm, j + 1)
                    if j == 0:
                        act.wait_ge(s.aT_mm, HGROUPS)
                    nc.scalar.copy(o_sb[:, :, 2 * HD * j:2 * HD * (j + 1)].rearrange("p q (h d) -> p h q d", h=2),
                                   bank[j % 4][0:BN, :].rearrange("p (h q d) -> p h q d", h=2, q=PIX)
                                   ).then_inc(s.o_act, 1)
                for j in range(0, 8, 2):
                    act.wait_ge(s.oT_mm, j + 1)
                    nc.scalar.copy(outT[:, j // 4, :, 4 * (j % 4):4 * (j % 4) + 4].rearrange("p n q -> p q n"),
                                   bank[4 + j % 4][:, 0:4 * BN].rearrange("p (q n) -> p q n", q=4)).then_inc(s.oT_act, 1)
                stds(s.var2, s.std2, LN_EPS[1])
                for j in range(6):
                    act.wait_ge(s.xn2T_mm, j + 1)
                    nc.scalar.copy(xn2T[:, j % 4, :, :, :],
                                   bank[4 + j % 4][:, :].rearrange("p (i k t) -> p i k t", i=2, k=KC)
                                   ).then_inc(s.xn2T, 1)
                act.wait_ge(s.mtop, 1)
                if L == 0:
                    nc.scalar.activation(prob8[:, :, :], prob8[:, :, :], ACT.Exp).then_inc(s.exp8, 1)
                nc.scalar.activation(small[:, 0, :], small[:, 0, :], ACT.Exp).then_inc(s.exp8, 1)

                def step(b, par):
                    if register(b) or b >= 1:
                        act.wait_ge(s.hT_mm, 2 * b - 1)
                        if register(b) or b >= 2:
                            act.wait_ge(s.e_mm, b - 1)
                        half = f.kt // 2
                        nc.scalar.copy(hT[0:f.kh, 0:half, :],
                                       bank[4][0:f.kh, 0:half * P].rearrange("p (k s) -> p k s", s=P)
                                       ).then_inc(s.hTa, 1)
                    if register(b) or b < NB:
                        for j in range(2):
                            act.wait_ge(s.h_mm, f.chunks * b + j + 1)
                            if L == 0:
                                if register(b) or b >= 1:
                                    act.wait_ge(s.hT_mm, 2 * b)
                                nc.scalar.activation(h_sb[:, f.chunk * j:f.chunk * (j + 1)], bank[j][:, 0:f.chunk],
                                                     ACT.Silu).then_inc(s.h, 1)
                            else:
                                if register(b) or b >= 1:
                                    act.wait_ge(s.h, 2 * b)
                                nc.scalar.activation(silu_g[:, f.chunk * j:f.chunk * (j + 1)], bank[j][:, 0:f.chunk],
                                                     ACT.Silu).then_inc(s.silu, 1)

                block_loop(act, step)

        @block.vector
        def _(dve):
            for L in range(2):
                s, f = lay[L], FFN[L]
                nchain = [0]

                def chain(ins):
                    nchain[0] += 1
                    ins.then_inc(s.chain, 1)
                    dve.wait_ge(s.chain, nchain[0])

                def stats_of(tiles, done, eps):
                    for i in tiles:
                        nc.vector.bn_stats(stats[:, i, :], xres[:, i, :]).then_inc(s.stat, 1)
                    dve.wait_ge(s.stat, nstat[0] + len(tiles))
                    nstat[0] += len(tiles)
                    for i in tiles:
                        nc.vector.bn_aggr(mean_var[:, i, :], stats[:, i, :]).then_inc(s.stat, 1)
                    nstat[0] += len(tiles)
                    dve.wait_ge(s.stat, nstat[0])
                    a, b = tiles[0], tiles[-1] + 1
                    nc.vector.tensor_scalar(mean_var[:, a:b, 1], mean_var[:, a:b, 1], eps, None,
                                            ALU.add).then_inc(done, len(tiles))

                def normalise(tiles, std_done, dst, done):
                    g = tiles[0] // 4
                    dve.wait_ge(std_done, g + 1)
                    chain(nc.vector.reciprocal(rstd[:, tiles[0]:tiles[-1] + 1], std[:, tiles[0]:tiles[-1] + 1]))
                    for i in tiles:
                        nc.vector.tensor_scalar(dst[:, i, :], xres[:, i, :], mean_var[:, i, 0:1], rstd[:, i:i + 1],
                                                ALU.subtract, ALU.mult).then_inc(done, 1)

                nstat = [0]
                for g in range(3):
                    dve.wait_ge((s.x_in0, s.x_in1, s.x_in2)[g], 16)
                    if L == 1 and g == 0:
                        dve.wait_ge(lay[0].std2, 3)
                    stats_of(range(4 * g, 4 * g + 4), s.var, LN_EPS[0])
                if L == 1:
                    dve.wait_ge(lay[0].added, 16 * NB)
                    dve.wait_ge(lay[0].e_mm, NB)
                for g in range(3):
                    normalise(range(4 * g, 4 * g + 4), s.std, xn, s.xn)
                if L == 0:
                    dve.wait_ge(const_done, 1)
                dve.wait_ge(s.pool_mm, 1)
                nc.vector.tensor_copy(xm[:, :, :], bank[4][:, 0:KC * BN].rearrange("p (k n) -> p k n", k=KC)
                                      ).then_inc(s.xm, 1)
                dve.wait_ge(s.qk_mm, 1)
                qk = bank[5][:, 0:4 * BN].rearrange("p (v k n) -> p v k n", v=2, k=KC)
                nc.vector.tensor_copy(kT[:, :, :], qk[:, 1, :, :]).then_inc(s.k_sb, 1)
                for k in range(KC):
                    nc.vector.tensor_tensor(qmask[:, HPH * k:HPH * (k + 1), :],
                                            qk[:, 0, k, :].unsqueeze(1).to_broadcast([P, HPH, BN]),
                                            q_mask[:, :].unsqueeze(2).to_broadcast([P, HPH, BN]),
                                            ALU.mult).then_inc(s.qm, 1)
                def heads(g):
                    return slice(GROUP * g, GROUP * (g + 1))

                def sm_front(g):
                    dve.wait_ge(s.s_mm, g + 1)
                    chain(nc.vector.tensor_tensor(probs[:, heads(g), :],
                                                  bank[g][0:BN, 0:GROUP * BN].rearrange("p (h m) -> p h m", h=GROUP),
                                                  batch_mask[:, :, :].rearrange("p b n -> p (b n)").unsqueeze(1)
                                                  .to_broadcast([BN, GROUP, BN]), ALU.add))
                    chain(nc.vector.tensor_reduce(row_max[:, heads(g)], probs[:, heads(g), :], AX.X, ALU.max))
                    nc.vector.tensor_tensor(probs[:, heads(g), :], probs[:, heads(g), :],
                                            row_max[:, heads(g)].unsqueeze(2).to_broadcast([BN, GROUP, BN]),
                                            ALU.subtract).then_inc(s.sub, 1)

                def sm_back(g):
                    dve.wait_ge(s.expd, g + 1)
                    chain(nc.vector.tensor_reduce(row_sum[:, heads(g)], probs[:, heads(g), :], AX.X, ALU.add))
                    chain(nc.vector.reciprocal(row_sum[:, heads(g)], row_sum[:, heads(g)]))
                    nc.vector.tensor_tensor(probs[:, heads(g), :], probs[:, heads(g), :],
                                            row_sum[:, heads(g)].unsqueeze(2).to_broadcast([BN, GROUP, BN]),
                                            ALU.mult).then_inc(s.attn, 1)

                for g in range(HGROUPS + 1):
                    if g < HGROUPS:
                        sm_front(g)
                    if g >= 1:
                        sm_back(g - 1)
                for j in range(1, 8, 2):
                    dve.wait_ge(s.av_mm, j + 1)
                    if j == 1:
                        dve.wait_ge(s.aT_mm, HGROUPS)
                    nc.vector.tensor_copy(o_sb[:, :, 2 * HD * j:2 * HD * (j + 1)].rearrange("p q (h d) -> p h q d", h=2),
                                          bank[j % 4][0:BN, :].rearrange("p (h q d) -> p h q d", h=2, q=PIX)
                                          ).then_inc(s.o_dve, 1)
                for j in range(1, 8, 2):
                    dve.wait_ge(s.oT_mm, j + 1)
                    nc.vector.tensor_copy(outT[:, j // 4, :, 4 * (j % 4):4 * (j % 4) + 4].rearrange("p n q -> p q n"),
                                          bank[4 + j % 4][:, 0:4 * BN].rearrange("p (q n) -> p q n", q=4)
                                          ).then_inc(s.oT_dve, 1)
                dve.wait_ge(s.bias_added, 1)
                nlast = [0]
                for g in range(3):
                    for j in (2 * g, 2 * g + 1):
                        dve.wait_ge(s.y_mm, j + 1)
                        nc.vector.tensor_tensor(xres[:, 2 * j:2 * j + 2, :], xres[:, 2 * j:2 * j + 2, :],
                                                bank[j % 3][:, :].rearrange("p (i c) -> p i c", i=2), ALU.add
                                                ).then_inc(s.x1, 1)
                    dve.wait_ge(s.x1, 2 * g + 2)
                    if g == 0:
                        dve.wait_ge(s.std, 3)
                        dve.wait_ge(s.xn, TILES)
                    stats_of(range(4 * g, 4 * g + 4), s.var2, LN_EPS[1])
                for g in range(3):
                    if g == 0:
                        dve.wait_ge(s.av_mm, 8)
                    normalise(range(4 * g, 4 * g + 4), s.std2, xn2, s.xn2)
                dve.wait_ge(s.lg_mm, 1)
                lgp = bank[3][:, 0:TILES * E].rearrange("p (i e) -> p i e", i=TILES)

                def tiles_bc(a):
                    return a.unsqueeze(2).to_broadcast([P, TILES, E])

                def experts_bc(a):
                    return a.unsqueeze(1).to_broadcast([P, TILES, E])

                if L == 0:
                    dve.wait_ge(const_done, 2)
                    dve.wait_ge(s.route_in, 32)
                    nc.vector.tensor_tensor(logits[:, :, :], lgp, experts_bc(broute[:, :]), ALU.add).then_inc(s.lg, 1)
                else:
                    nc.vector.tensor_copy(logits[:, :, :], lgp).then_inc(s.lg, 1)
                dve.wait_ge(s.lg, 1)
                cur = logits
                for k in range(TOPK):
                    chain(nc.vector.tensor_reduce(m_top[:, k, :], cur[:, :, :], AX.X, ALU.max))
                    chain(nc.vector.tensor_tensor(cand[:, :, :], cur[:, :, :], tiles_bc(m_top[:, k, :]), ALU.is_equal))
                    chain(nc.vector.tensor_tensor(cand[:, :, :], cand[:, :, :], experts_bc(expert_m8[:, :]), ALU.mult))
                    chain(nc.vector.tensor_reduce(i_top[:, k, :], cand[:, :, :], AX.X, ALU.min))
                    chain(nc.vector.tensor_tensor(pick[:, k, :, :].rearrange("p e i -> p i e"),
                                                  experts_bc(expert_m8[:, :]), tiles_bc(i_top[:, k, :]), ALU.is_equal))
                    if k == 0:
                        chain(nc.vector.scalar_tensor_tensor(out=lg2[:, :, :],
                                                             in0=pick[:, 0, :, :].rearrange("p e i -> p i e"),
                                                             scalar=NEG, in1=logits[:, :, :],
                                                             op0=ALU.mult, op1=ALU.add))
                        cur = lg2
                if L == 0:
                    chain(nc.vector.tensor_tensor(prob8[:, :, :], logits[:, :, :], tiles_bc(m_top[:, 0, :]),
                                                  ALU.subtract))
                nc.vector.tensor_tensor(small[:, 0, :], m_top[:, 1, :], m_top[:, 0, :], ALU.subtract).then_inc(s.mtop, 1)
                nc.vector.tensor_tensor(picked[:, :, :], pick[:, 0, :, :], pick[:, 1, :, :], ALU.add
                                        ).then_inc(s.picked, 1)
                if L == 0:
                    dve.wait_ge(s.exp8, 2)
                    chain(nc.vector.tensor_reduce(small[:, 1, :], prob8[:, :, :], AX.X, ALU.add))
                else:
                    dve.wait_ge(s.exp8, 1)
                    chain(nc.vector.tensor_scalar(small[:, 1, :], small[:, 0, :], 1.0, None, ALU.add))
                chain(nc.vector.reciprocal(gate[:, 0, :], small[:, 1, :]))
                chain(nc.vector.tensor_tensor(gate[:, 1, :], small[:, 0, :], gate[:, 0, :], ALU.mult))
                dve.wait_ge(s.cnt_mm, 2)
                before = bank[4][:, 0:E * TILES].rearrange("p (e i) -> p e i", e=E)
                total = bank[4][:, E * TILES:2 * E * TILES].rearrange("p (e i) -> p e i", e=E)
                flat = "p e i -> p (e i)"
                chain(nc.vector.tensor_tensor_scan(incl[:, :, :].rearrange(flat), scan_keep[:, :, :].rearrange(flat),
                                                   total.rearrange(flat), 0.0, ALU.mult, ALU.add))
                chain(nc.vector.tensor_tensor(place[:, :, :], incl[:, :, :], total, ALU.subtract))
                chain(nc.vector.tensor_tensor(place[:, :, :], place[:, :, :], before, ALU.add))
                chain(nc.vector.tensor_scalar(cnt_i[:, 0, :], incl[:, :, TILES - 1], float(P - 1), None, ALU.add))
                chain(nc.vector.tensor_scalar(cnt_i[:, 1, :], cnt_i[:, 0, :], 7, None, ALU.arith_shift_right))
                chain(nc.vector.tensor_copy(nblk[:, :], cnt_i[:, 1, :]))
                chain(nc.vector.tensor_tensor_scan(endblk[:, :], scan_keep[:, 0, 1:1 + E], nblk[:, :], 0.0, ALU.mult, ALU.add))
                chain(nc.vector.tensor_tensor(base[:, :], endblk[:, :], nblk[:, :], ALU.subtract))
                chain(nc.vector.scalar_tensor_tensor(out=place[:, :, :], in0=base[:, :].unsqueeze(2)
                                                     .to_broadcast([P, E, TILES]), scalar=float(P),
                                                     in1=place[:, :, :], op0=ALU.mult, op1=ALU.add))
                for k in range(TOPK):
                    chain(nc.vector.tensor_tensor(term[:, :, :], place[:, :, :], pick[:, k, :, :], ALU.mult))
                    chain(nc.vector.tensor_reduce(slot_f[:, k, :], term[:, :, :].rearrange("p e i -> p i e"), AX.X, ALU.add))
                chain(nc.vector.tensor_copy(slot_i[:, 0, :, :], slot_f[:, :, :]))
                chain(nc.vector.tensor_scalar(slot_i[:, 1, :, :], slot_i[:, 0, :, :], P - 1, None, ALU.bitwise_and))
                chain(nc.vector.tensor_scalar(slot_i[:, 2, :, :], slot_i[:, 0, :, :], 7, None, ALU.arith_shift_right))
                chain(nc.vector.tensor_copy(rowblk[:, :, :], slot_i[:, 1:3, :, :].rearrange("p v k i -> p v (k i)")))
                dve.wait_ge(s.y_mm, 6)
                nc.vector.tensor_tensor(onehot_row, iota[:, :].unsqueeze(1).to_broadcast([P, PAIRS, P]),
                                        rowblk[:, 0, :].unsqueeze(2).to_broadcast([P, PAIRS, P]),
                                        ALU.is_equal).then_inc(s.hot, 1)
                dve.wait_ge(s.xn2T, 6)
                for v in range(2):
                    chain(nc.vector.tensor_tensor(onehot_blk[:, :, v, :],
                                                  iota[:, 0:TABLE].unsqueeze(1).to_broadcast([P, PAIRS, TABLE]),
                                                  rowblk[:, 1, :].unsqueeze(2).to_broadcast([P, PAIRS, TABLE]),
                                                  ALU.is_equal))
                for k in range(TOPK):
                    pairs = slice(k * TILES, (k + 1) * TILES)
                    for v, value in ((0, token_id[:, :]), (1, gate[:, k, :])):
                        nc.vector.tensor_tensor(onehot_blk[:, pairs, v, :], onehot_blk[:, pairs, v, :],
                                                value.unsqueeze(2).to_broadcast([P, TILES, TABLE]), ALU.mult
                                                ).then_inc(s.hot, 1)
                chain(nc.vector.tensor_tensor(blk_cmp[:, :, :], iota[0:1, 0:TABLE].unsqueeze(2).to_broadcast([1, TABLE, E]),
                                              endblk[0:1, :].unsqueeze(1).to_broadcast([1, TABLE, E]), ALU.is_ge))
                chain(nc.vector.tensor_reduce(blk_e[:, 0, :], blk_cmp[:, :, :], AX.X, ALU.add))
                chain(nc.vector.tensor_scalar(blk_e[:, 0, :], blk_e[:, 0, :], float(E - 1), None, ALU.min))
                first = (L * E) % SLOTS
                chain(nc.vector.tensor_scalar(blk_e[:, 1, :], blk_e[:, 0, :], float(first), None, ALU.add))
                chain(nc.vector.tensor_scalar(blk_e[:, 2, :], blk_e[:, 1, :], float(SLOTS), -float(SLOTS),
                                              ALU.is_ge, ALU.mult))
                chain(nc.vector.tensor_tensor(blk_e[:, 1, :], blk_e[:, 1, :], blk_e[:, 2, :], ALU.add))
                if L == 1:
                    dve.wait_ge(lay[0].h_mm, FFN[0].chunks * NB)
                chain(nc.vector.tensor_copy(tab_e[:, :, :], blk_e[:, 0:2, :]))
                chain(nc.vector.tensor_scalar(tab_end[L][:, :], endblk[0:1, :], 1.0, None, ALU.max))
                chain(nc.vector.memset(tab_end[L][:, E - 1:E], NB))
                dve.wait_ge(s.tab_mm, 1)
                if L == 1:
                    dve.wait_ge(lay[0].added, 16 * NB)
                tabp = bank[5][:, 0:2 * TABLE].rearrange("p (v b) -> p v b", v=2)
                chain(nc.vector.tensor_copy(gate_tab[:, :], tabp[:, 1, :]))
                chain(nc.vector.tensor_scalar(gather_tab[:, :], tabp[:, 0, :], -1.0, 0.0, ALU.add, ALU.max))
                chain(nc.vector.tensor_scalar(id_sb[:, 0, :], tabp[:, 0, :], 0.0, float(BIG_ROW), ALU.is_equal, ALU.mult))
                chain(nc.vector.tensor_scalar(id_sb[:, 1, :], tabp[:, 0, :], -1.0, None, ALU.add))
                nc.vector.tensor_tensor(scatter_tab[:, :], id_sb[:, 0, :], id_sb[:, 1, :], ALU.add).then_inc(s.tab, 1)
                dve.wait_ge(s.tab, 1)

                def xT_copy(b, par):
                    dve.wait_ge(s.xT_mm, b + 1)
                    if register(b) or b >= 2:
                        dve.wait_ge(s.h_mm, f.chunks * (b - 1))
                    nc.vector.tensor_copy(xT[:, par, :, :], bank[7][:, 0:C].rearrange("p (k s) -> p k s", k=KC)
                                          ).then_inc(s.xT, 1)

                xT_copy(0, 0)

                def step(b, par):
                    half = f.kt // 2
                    if register(b) or b >= 1:
                        dve.wait_ge(s.hT_mm, 2 * b)
                        if register(b) or b >= 2:
                            dve.wait_ge(s.e_mm, b - 1)
                        nc.vector.tensor_copy(hT[0:f.kh, half:f.kt, :],
                                              bank[5][0:f.kh, 0:half * P].rearrange("p (k s) -> p k s", s=P)
                                              ).then_inc(s.hTb, 1)
                    if register(b) or b + 1 < NB:
                        xT_copy(b + 1, 1 - par)
                    if L == 1 and (register(b) or b < NB):
                        for j in range(2):
                            dve.wait_ge(s.silu, 2 * b + j + 1)
                            dve.wait_ge(s.h_mm, f.chunks * b + 3 + j)
                            nc.vector.tensor_tensor(h_sb[:, f.chunk * j:f.chunk * (j + 1)], bank[2 + j][:, 0:f.chunk],
                                                    silu_g[:, f.chunk * j:f.chunk * (j + 1)], ALU.mult
                                                    ).then_inc(s.h, 1)
                    if register(b) or b >= 1:
                        dve.wait_ge(s.e_mm, b)
                        if register(b) or b >= 3:
                            dve.wait_ge(s.added, 16 * (b - 2))
                        nc.vector.tensor_scalar(y_sb[:, 1 - par, :], bank[6][:, 0:C], col(gate_tab, b - 1), None,
                                                ALU.mult).then_inc(s.e_sb, 1)

                block_loop(dve, step)

        @block.tensor
        def _(pe):
            pe.wait_ge(const_done, 1)
            for L in range(2):
                s, f = lay[L], FFN[L]
                for j in range(6):
                    pe.wait_ge(s.xn, 2 * j + 2)
                    if j >= 4:
                        pe.wait_ge(s.xnT, j - 3)
                    if L == 1 and j == 0:
                        pe.wait_ge(lay[0].h, 2 * NB)
                    for i in range(2):
                        for k in range(KC):
                            mm = pe.transpose(bank[j % 4][:, (2 * i + k) * P:(2 * i + k + 1) * P],
                                              xn[:, 2 * j + i, k * P:(k + 1) * P], ident[:, :])
                    mm.then_inc(s.xnT_mm, 1)
                    for i in range(2):
                        for k in range(KC):
                            n = NPT * (2 * j + i)
                            mm = pe.matmul(bank[4][:, k * BN + n:k * BN + n + NPT], xn[:, 2 * j + i, k * P:(k + 1) * P],
                                           head_mask[:, :], start=True, stop=True)
                mm.then_inc(s.pool_mm, 1)
                pe.wait_ge(s.xm, 1)
                pe.wait_ge(s.conv_in, 48)
                for v in range(2):
                    for m in range(KC):
                        for k in range(KC):
                            o = (KC * v + m) * BN
                            mm = pe.matmul(bank[5][:, o:o + BN], wqkv[:, k, v * C + m * P:v * C + (m + 1) * P],
                                           xm[:, k, :], start=(k == 0), stop=(k == KC - 1))
                mm.then_inc(s.qk_mm, 1)

                def values(j):
                    if j >= 2:
                        pe.wait_ge(s.v, j - 1)
                    for q in range(2):
                        for k in range(KC):
                            toks = xnT[:, k, :].rearrange("p (n q) -> p q n", q=PIX)[:, 2 * j + q, :]
                            mm = pe.matmul(bank[6 + j % 2][0:BN, q * C:(q + 1) * C], toks, wqkv[:, k, 2 * C:3 * C],
                                           start=(k == 0), stop=(k == KC - 1))
                    mm.then_inc(s.v_mm, 1)

                pe.wait_ge(s.xnT, 6)
                if L == 1:
                    pe.wait_ge(lay[0].e_sb, NB)
                values(0)
                pe.wait_ge(s.k_sb, 1)
                for g in range(HGROUPS):
                    pe.wait_ge(s.qm, g // 2 + 1)
                    for h in range(GROUP * g, GROUP * (g + 1)):
                        o = (h - GROUP * g) * BN
                        mm = pe.matmul(bank[g][0:BN, o:o + BN], qmask[:, h, :], kT[:, h // HPH, :],
                                       start=True, stop=True)
                    mm.then_inc(s.s_mm, 1)
                for j in range(1, 8):
                    values(j)
                for g in range(HGROUPS):
                    pe.wait_ge(s.attn, g + 1)
                    if g >= 2:
                        pe.wait_ge(s.aT, g - 1)
                    for h in range(GROUP * g, GROUP * (g + 1)):
                        o = (h - GROUP * g) * BN
                        mm = pe.transpose(bank[4 + g % 2][0:BN, o:o + BN], probs[:, h, :], ident[0:BN, 0:BN])
                    mm.then_inc(s.aT_mm, 1)
                pe.wait_ge(s.v, 8)
                for j in range(8):
                    pe.wait_ge(s.aT, j // 2 + 1)
                    if j >= 4:
                        pe.wait_ge((s.o_act, s.o_dve)[j % 2], (j - 4) // 2 + 1)
                    for h in (2 * j, 2 * j + 1):
                        o = (h - 2 * j) * C
                        mm = pe.matmul(bank[j % 4][0:BN, o:o + C], attnT[:, h, :], v_sb[:, :, h * HD:(h + 1) * HD],
                                       start=True, stop=True)
                    mm.then_inc(s.av_mm, 1)
                pe.wait_ge(s.o_act, 4)
                pe.wait_ge(s.o_dve, 4)
                for j in range(8):
                    k, q0 = j // 4, 4 * (j % 4)
                    if j >= 4:
                        pe.wait_ge((s.oT_act, s.oT_dve)[j % 2], (j - 4) // 2 + 1)
                    for q in range(4):
                        mm = pe.transpose(bank[4 + j % 4][:, q * BN:(q + 1) * BN], o_sb[:, q0 + q, k * P:(k + 1) * P],
                                          ident[0:BN, 0:BN])
                    mm.then_inc(s.oT_mm, 1)
                pe.wait_ge(s.oT_act, 4)
                pe.wait_ge(s.oT_dve, 4)
                for j in range(6):
                    if j >= 3:
                        pe.wait_ge(s.x1, j - 2)
                    for i in range(2):
                        n = NPT * (2 * j + i)
                        for k in range(KC):
                            mm = pe.matmul(bank[j % 3][:, i * C:(i + 1) * C], outT[:, k, n:n + NPT, :], wproj[:, k, :],
                                           start=(k == 0), stop=(k == KC - 1))
                    mm.then_inc(s.y_mm, 1)
                pe.wait_ge(s.route_in, 32 if L == 0 else 16)

                def route(j):
                    pe.wait_ge(s.xn2T, j + 1)
                    for i in range(2):
                        for k in range(KC):
                            o = (2 * j + i) * E
                            mm = pe.matmul(bank[3][:, o:o + E], xn2T[:, j % 4, i, k, :], wroute[:, k, :],
                                           start=(k == 0), stop=(k == KC - 1))
                    return mm

                for j in range(6):
                    pe.wait_ge(s.xn2, 2 * j + 2)
                    if j >= 4:
                        pe.wait_ge(s.xn2T, j - 3)
                    for i in range(2):
                        for k in range(KC):
                            mm = pe.transpose(bank[4 + j % 4][:, (2 * i + k) * P:(2 * i + k + 1) * P],
                                              xn2[:, 2 * j + i, k * P:(k + 1) * P], ident[:, :])
                    mm.then_inc(s.xn2T_mm, 1)
                    if j >= 1:
                        route(j - 1)
                route(5).then_inc(s.lg_mm, 1)
                pe.wait_ge(s.picked, 1)
                if L == 0:
                    pe.wait_ge(const_done, 2)
                for n, m in ((0, tri), (1, ones)):
                    pe.matmul(bank[4][:, n * E * TILES:(n + 1) * E * TILES], m[:, :],
                              picked[:, :, :].rearrange("p e i -> p (e i)"), start=True, stop=True
                              ).then_inc(s.cnt_mm, 1)
                pe.wait_ge(s.hot, 1 + 2 * TOPK)
                for j in range(PAIRS):
                    mm = pe.matmul(bank[5][:, 0:2 * TABLE], onehot_row[:, j, :],
                                   onehot_blk[:, j, :, :].rearrange("p v b -> p (v b)"),
                                   start=(j == 0), stop=(j == PAIRS - 1))
                mm.then_inc(s.tab_mm, 1)
                pe.wait_ge(s.bias_ready, 1)
                pe.wait_ge(s.tab, 1)

                def x_transpose(b, par):
                    pe.wait_ge((s.gathered0, s.gathered1)[par], 16 * (b // 2 + 1))
                    if register(b) or b >= 1:
                        pe.wait_ge(s.xT, b)
                    for k in range(KC):
                        mm = pe.transpose(bank[7][:, k * P:(k + 1) * P], xg[:, par, k * P:(k + 1) * P], ident[:, :])
                    mm.then_inc(s.xT_mm, 1)

                x_transpose(0, 0)
                half = f.kt // 2
                order = (0, 1) if L == 0 else (2, 3, 0, 1)

                def expert_of(b):
                    e = pe.value_load(tab_e[0:1, 0, bass.ds(b, 1)] if register(b) else tab_e[0:1, 0, b:b + 1],
                                      min_val=0, max_val=E - 1)
                    slot = pe.value_load(tab_e[0:1, 1, bass.ds(b, 1)] if register(b) else tab_e[0:1, 1, b:b + 1],
                                         min_val=0, max_val=SLOTS - 1)
                    return e, slot

                def step(b, par):
                    if register(b) or b < NB:
                        e, slot = expert_of(b)
                    if register(b) or b >= 1:
                        e_old, slot_old = expert_of(b - 1)
                    if register(b) or b >= 1:
                        for j in range(2):
                            pe.wait_ge(s.h, 2 * b - 1 + j)
                            if register(b) or b >= 2:
                                pe.wait_ge((s.hTa, s.hTb)[j], b - 1)
                            for k in range(half):
                                o = (j * half + k) * f.kh
                                mm = pe.transpose(bank[4 + j][0:f.kh, k * P:(k + 1) * P], h_sb[:, o:o + f.kh],
                                                  ident[:, :])
                            mm.then_inc(s.hT_mm, 1)
                    if register(b) or b + 1 < NB:
                        x_transpose(b + 1, 1 - par)
                    if register(b) or b < NB:
                        pe.wait_ge(w_ready, e + (L * E + 1))
                        pe.wait_ge(s.xT, b + 1)
                        w1, _ = weight_views(L, slot)
                        for n, c in enumerate(order):
                            cs = slice(c * f.chunk, (c + 1) * f.chunk)
                            pe.matmul(bank[n][:, 0:f.chunk], expert_sel[:, e, :], bias_rows[:, cs],
                                      start=True, stop=False)
                            for k in range(KC):
                                mm = pe.matmul(bank[n][:, 0:f.chunk], xT[:, par, k, :], w1[:, k, cs],
                                               start=False, stop=(k == KC - 1))
                            mm.then_inc(s.h_mm, 1)
                    if register(b) or b >= 1:
                        pe.wait_ge(s.hTa, b)
                        if register(b) or b >= 2:
                            pe.wait_ge(s.e_sb, b - 1)
                        _, w2 = weight_views(L, slot_old)
                        pe.matmul(bank[6][:, 0:C], expert_sel[:, e_old, :], bias_rows[:, f.wide:f.wide + C],
                                  start=True, stop=False)
                        for k in range(f.kt):
                            if k == half:
                                pe.wait_ge(s.hTb, b)
                            mm = pe.matmul(bank[6][:, 0:C], hT[0:f.kh, k, :], w2[:, k, :],
                                           start=False, stop=(k == f.kt - 1))
                        mm.then_inc(s.e_mm, 1)

                block_loop(pe, step)


_INS = ['x', 'L0_conv_W_qkv', 'L0_conv_W_proj', 'L0_conv_b_proj', 'L0_ffn_gate_w', 'L0_ffn_gate_b', 'L0_ffn_w1',
        'L0_ffn_b1', 'L0_ffn_w2', 'L0_ffn_b2', 'L1_conv_W_qkv', 'L1_conv_W_proj', 'L1_conv_b_proj',
        'L1_ffn_router_w', 'L1_ffn_W1', 'L1_ffn_b1', 'L1_ffn_W2', 'L1_ffn_b2']


def kernel(**inputs):
    import numpy as _np
    import concourse.bacc as _bacc
    from concourse import mybir as _mybir
    from concourse.bass_utils import run_bass_kernel_spmd as _run

    nc = _bacc.Bacc("TRN2", target_bir_lowering=False, num_devices=1)
    arrays, d = {}, {}
    for name in _INS:
        a = _np.ascontiguousarray(inputs[name])
        arrays[f"in_{name}_dram"] = a
        d[name] = nc.dram_tensor(f"in_{name}_dram", a.shape, _mybir.dt.from_np(a.dtype), kind="ExternalInput").ap()
    out = nc.dram_tensor("out_0_dram", (B, N, PIX, C), _mybir.dt.float32, kind="ExternalOutput").ap()
    conv_w = [(d[f'L{n}_conv_W_qkv'], d[f'L{n}_conv_W_proj'], d[f'L{n}_conv_b_proj']) for n in range(2)]
    ffn_w = [(d['L0_ffn_gate_w'], d['L0_ffn_gate_b'], d['L0_ffn_w1'], d['L0_ffn_b1'], d['L0_ffn_w2'], d['L0_ffn_b2']),
             (d['L1_ffn_router_w'], None, d['L1_ffn_W1'], d['L1_ffn_b1'], d['L1_ffn_W2'], d['L1_ffn_b2'])]
    metaformer(nc, d['x'], conv_w, ffn_w, out)
    r = _run(nc, [arrays], core_ids=[0])
    return r.results[0]["out_0_dram"]
```

```python
from contextlib import ExitStack

import concourse.bass as bass
from concourse import mybir

F32 = mybir.dt.float32
F32R = mybir.dt.float32r
BF16 = mybir.dt.bfloat16
I32 = mybir.dt.int32
ALU = mybir.AluOpType
ACT = mybir.ActivationFunctionType
AX = mybir.AxisListType

P = 128
B, N, PIX, C = 4, 24, 16, 256
BN = B * N
TOKENS = B * N * PIX
TILES = TOKENS // P
KC = C // P
HEADS, HD = 16, 16
HPH = P // HD
GROUP = 4
HGROUPS = HEADS // GROUP
NPT = P // PIX
E, TOPK = 8, 2
PAIRS = TILES * TOPK
MAX_BLOCKS = (TOKENS * TOPK + E * (P - 1)) // P
MIN_BLOCKS = TOKENS * TOPK // P
TABLE = MAX_BLOCKS + 3
TAB = MAX_BLOCKS + MAX_BLOCKS % 2
SLOTS = 3
PIECES = 4
NEG = -1.0e30
BIG_ROW = 4096

class Ffn:
    def __init__(self, wide, kt, kh, chunk):
        self.wide, self.kt, self.kh, self.chunk, self.chunks = wide, kt, kh, chunk, wide // chunk


FFN = [Ffn(wide=1024, kt=8, kh=128, chunk=512), Ffn(wide=1344, kt=6, kh=112, chunk=336)]
WORDS = [KC * f.wide + f.kt * C for f in FFN]
SLOT_WORDS = max(WORDS)
BIAS_WIDE = max(f.wide for f in FFN) + C
LN_EPS = (1e-6, 1e-5)


class LayerSems:

    def __init__(self, sem, L):
        self.x_in0 = sem(f"x_in0_{L}")
        self.x_in1 = sem(f"x_in1_{L}")
        self.x_in2 = sem(f"x_in2_{L}")
        self.conv_in = sem(f"conv_in_{L}")
        self.bias_in = sem(f"bias_in_{L}")
        self.route_in = sem(f"route_in_{L}")
        self.stat = sem(f"stat_{L}")
        self.var = sem(f"var_{L}")
        self.std = sem(f"std_{L}")
        self.xn = sem(f"xn_{L}")
        self.xnT_mm = sem(f"xnT_mm_{L}")
        self.xnT = sem(f"xnT_{L}")
        self.xm = sem(f"xm_{L}")
        self.qk_mm = sem(f"qk_mm_{L}")
        self.k_sb = sem(f"k_sb_{L}")
        self.qm = sem(f"qm_{L}")
        self.s_mm = sem(f"s_mm_{L}")
        self.sub = sem(f"sub_{L}")
        self.expd = sem(f"expd_{L}")
        self.attn = sem(f"attn_{L}")
        self.bias_added = sem(f"bias_added_{L}")
        self.v_mm = sem(f"v_mm_{L}")
        self.v = sem(f"v_{L}")
        self.aT_mm = sem(f"aT_mm_{L}")
        self.aT = sem(f"aT_{L}")
        self.av_mm = sem(f"av_mm_{L}")
        self.o_act = sem(f"o_act_{L}")
        self.o_dve = sem(f"o_dve_{L}")
        self.oT_mm = sem(f"oT_mm_{L}")
        self.oT_act = sem(f"oT_act_{L}")
        self.oT_dve = sem(f"oT_dve_{L}")
        self.y_mm = sem(f"y_mm_{L}")
        self.x1 = sem(f"x1_{L}")
        self.var2 = sem(f"var2_{L}")
        self.std2 = sem(f"std2_{L}")
        self.xn2 = sem(f"xn2_{L}")
        self.xn2T_mm = sem(f"xn2T_mm_{L}")
        self.xn2T = sem(f"xn2T_{L}")
        self.lg_mm = sem(f"lg_mm_{L}")
        self.lg = sem(f"lg_{L}")
        self.chain = sem(f"chain_{L}")
        self.top2 = sem(f"top2_{L}")
        self.exp8 = sem(f"exp8_{L}")
        self.cnt_mm = sem(f"cnt_mm_{L}")
        self.blk_hot = sem(f"blk_hot_{L}")
        self.hot_rows = sem(f"hot_rows_{L}")
        self.hot_blk = sem(f"hot_blk_{L}")
        self.tab_mm = sem(f"tab_mm_{L}")
        self.tab = sem(f"tab_{L}")
        self.bias_cast = sem(f"bias_cast_{L}")
        self.bias_sub = sem(f"bias_sub_{L}")
        self.store = sem(f"store_{L}")
        self.gathered = sem(f"gathered_{L}")
        self.gcol = sem(f"gcol_{L}")
        self.scol = sem(f"scol_{L}")
        self.xT_mm = sem(f"xT_mm_{L}")
        self.xT_hi = sem(f"xT_hi_{L}")
        self.xT_lo = sem(f"xT_lo_{L}")
        self.h_mm = sem(f"h_mm_{L}")
        self.silu = sem(f"silu_{L}")
        self.h = sem(f"h_{L}")
        self.hT_mm = sem(f"hT_mm_{L}")
        self.hT_hi = sem(f"hT_hi_{L}")
        self.hT_lo = sem(f"hT_lo_{L}")
        self.e_mm = sem(f"e_mm_{L}")
        self.e_sb = sem(f"e_sb_{L}")
        self.added = sem(f"added_{L}")
        self.raw_ready = sem(f"raw_ready_{L}")
        self.first_hi = sem(f"first_hi_{L}")
        self.pool_split = sem(f"pool_split_{L}")
        self.w_hi = sem(f"w_hi_{L}")
        self.w_lo = sem(f"w_lo_{L}")
        self.moe_done = sem(f"moe_done_{L}")
        self.rows_go = sem(f"rows_go_{L}")


def metaformer(nc, x, conv_w, ffn_w, out):
    with ExitStack() as ctx:
        def sb(name, shape, dt=F32):
            return ctx.enter_context(nc.sbuf_tensor(name, shape, dt))

        def sem(name):
            return ctx.enter_context(nc.semaphore(name))

        bank = [ctx.enter_context(nc.psum_tensor(f"bank{i}", [P, 512], F32)) for i in range(8)]

        w_hi = sb("w_hi", [P, SLOTS, SLOT_WORDS], F32R)
        w_lo = sb("w_lo", [P, SLOTS, SLOT_WORDS], F32R)
        raw = sb("raw", [P, 2, SLOT_WORDS])
        xres = sb("xres", [P, TILES, C])
        with nc.sbuf_tensor("region_a", [P, 4096], F32) as region_a:
            pass
        with nc.sbuf_tensor("onehot_blk", [P, PAIRS, 3, TAB], F32R) as onehot_blk:
            pass
        hT_hi = sb("hT_hi", [P, 8, P], F32R)
        hT_lo = sb("hT_lo", [P, 8, P], F32R)
        xT_hi = sb("xT_hi", [P, KC, P], F32R)
        xT_lo = sb("xT_lo", [P, KC, P], F32R)
        h_sb = sb("h_sb", [P, 1024])
        region_a_rest = sb("region_a_rest", [P, 4096 - 2 * 1024 - 2 * C - 1024])
        with nc.sbuf_tensor("region_b", [P, KC * TOKENS], F32) as region_b:
            pass
        onehot_row = sb("onehot_row", [P, PAIRS, P], F32R)
        region_d = sb("region_d", [P, BIAS_WIDE])
        wqkv = sb("wqkv", [P, KC, 3 * C])
        wproj = sb("wproj", [P, KC, C])
        bproj = sb("bproj", [P, C])
        bias_rows = sb("bias_rows", [96, BIAS_WIDE], BF16)
        expert_sel = sb("expert_sel", [96, E, P], BF16)
        wroute = sb("wroute", [P, KC, E])
        broute = sb("broute", [P, E])

        xn = region_a[:, 0:TILES * C].rearrange("p (i c) -> p i c", i=TILES)
        probs = region_a[0:BN, 0:HEADS * BN].rearrange("p (h m) -> p h m", h=HEADS)
        qmask = region_a[:, 1536:1536 + HEADS * BN].rearrange("p (h n) -> p h n", h=HEADS)
        o_sb = region_a[0:BN, :].rearrange("p (q c) -> p q c", q=PIX)
        xnT = region_b[:, :].rearrange("p (k t) -> p k t", k=KC)
        outT = region_b[:, :].rearrange("p (k n q) -> p k n q", k=KC, q=PIX)
        v_sb = raw[0:BN, 1, 0:4096].rearrange("p (q c) -> p q c", q=PIX)
        attnT = region_d[0:BN, 0:HEADS * BN].rearrange("p (h n) -> p h n", h=HEADS)
        bias_raw = region_d[0:96, :]
        kT = sb("kT", [P, KC, BN])
        xm = sb("xm", [P, KC, BN])
        row_max = sb("row_max", [BN, HEADS])
        row_sum = sb("row_sum", [BN, HEADS])
        stats = sb("stats", [P, TILES, 6])
        mean_var = sb("mean_var", [P, TILES, 2])
        std = sb("std", [P, TILES])
        rstd = sb("rstd", [P, TILES])
        xn2T = region_a[:, 0:4 * 512].rearrange("p (r i k t) -> p r i k t", r=4, i=2, k=KC)
        xn2 = raw[:, 1, 0:TILES * C].rearrange("p (i c) -> p i c", i=TILES)
        logits = sb("logits", [P, TILES, E])
        lg2 = sb("lg2", [P, TILES, E])
        prob8 = sb("prob8", [P, TILES, E])
        cand = sb("cand", [P, TILES, E])
        m_top = sb("m_top", [P, TOPK, TILES])
        i_top = sb("i_top", [P, TOPK, TILES])
        pick = sb("pick", [P, TOPK, E, TILES])
        picked = sb("picked", [P, E, TILES], BF16)
        gate = sb("gate", [P, TOPK, TILES])
        gate_hi = sb("gate_hi", [P, TOPK, TILES], F32R)
        small = sb("small", [P, 4, TILES])
        incl = sb("incl", [P, E, TILES])
        place = sb("place", [P, E, TILES])
        term = sb("term", [P, TOPK, E, TILES])
        blk_hot = region_a[:, 3 * PAIRS * TAB:4 * PAIRS * TAB].rearrange("p (j b) -> p j b", j=PAIRS)
        cnt_i = sb("cnt_i", [P, 2, E], I32)
        nblk = sb("nblk", [P, E])
        endblk = sb("endblk", [P, E])
        base = sb("base", [P, E])
        slot_f = sb("slot_f", [P, TOPK, TILES])
        slot_i = sb("slot_i", [P, 3, TOPK, TILES], I32)
        rowblk = sb("rowblk", [P, 2, PAIRS])
        blk_cmp = sb("blk_cmp", [1, 3, TABLE, E])
        blk_e = sb("blk_e", [1, 4, TABLE])
        tab_e = sb("tab_e", [1, TABLE], I32)
        tab_pieces = sb("tab_pieces", [1, TABLE], I32)
        tab_blocks = sb("tab_blocks", [1, 1], I32)
        id_sb = sb("id_sb", [P, 2, TAB])
        gather_tab = sb("gather_tab", [P, TABLE], I32)
        scatter_tab = sb("scatter_tab", [P, TABLE], I32)
        gate_tab = sb("gate_tab", [P, TABLE])
        xg = region_b[:, 0:C]
        y_sb = region_b[:, C:2 * C]
        silu_g = region_b[:, 2 * C:2 * C + FFN[1].chunk * 2]
        gcol = sb("gcol", [P, 1], I32)
        scol = sb("scol", [P, 1], I32)
        ident = sb("ident", [P, P])
        q_mask = sb("q_mask", [P, HPH])
        batch_mask = sb("batch_mask", [BN, B, N])
        after_or_at = sb("after_or_at", [P, P], BF16)
        ones = sb("ones", [P, P], BF16)
        iota_i = sb("iota_i", [P, P], I32)
        iota = sb("iota", [P, P])
        expert_m8 = sb("expert_m8", [P, E])
        token_i = sb("token_i", [P, TILES], I32)
        token_id = sb("token_id", [P, TILES])
        scan_keep = sb("scan_keep", [P, E, TILES])

        xn_dram = nc.dram_tensor("xn_dram", [TOKENS, C], F32).ap()
        mid_dram = nc.dram_tensor("mid_dram", [TOKENS, C], F32).ap()
        x_rows = x.rearrange("b n p c -> (b n p) c")
        out_rows = out.rearrange("b n p c -> (b n p) c")

        lay = [LayerSems(sem, L) for L in range(2)]
        made_seq = sem("made_seq")
        const_done = sem("const_done")
        raw_dma = [sem(f"raw_dma{i}") for i in range(2)]

        block = ctx.enter_context(nc.Block())

        def register(b):
            return not isinstance(b, int)

        def after(b, n):
            return register(b) or b >= n

        def col(tab, b):
            return tab[:, bass.ds(b, 1)] if register(b) else tab[:, b:b + 1]

        def block_count(eng):
            return eng.value_load(tab_blocks[0:1, 0:1], min_val=0, max_val=MAX_BLOCKS - MIN_BLOCKS) + MIN_BLOCKS

        def steps(eng, begin, end_less, blocks, step):
            with eng.Fori(begin, MIN_BLOCKS - end_less) as b:
                step(b)
            with eng.Fori(MIN_BLOCKS - end_less, MAX_BLOCKS - end_less) as b:
                with eng.If(b + end_less < blocks):
                    step(b)
                with eng.Else():
                    eng.nop()

        def block_loop(eng, step):
            blocks = block_count(eng)
            step(0)
            step(1)
            steps(eng, 2, 0, blocks, step)
            step(blocks, last=True)

        def piece_range(eng, b):
            if not after(b, 2):
                return None
            first = eng.value_load(col(tab_pieces, b - 2), min_val=0, max_val=PIECES * (E - SLOTS))
            end = eng.value_load(col(tab_pieces, b - 1), min_val=0, max_val=PIECES * (E - SLOTS))
            return first, end

        def for_pieces(eng, pieces, split):
            if pieces is None:
                return
            first, end = pieces

            def piece(i):
                with eng.If(first + i < end):
                    split(first + i)
                    if i + 1 < PIECES:
                        piece(i + 1)
                with eng.Else():
                    eng.nop()

            piece(0)

        def expert_views(w, L, slot):
            f = FFN[L]
            w1 = w[:, slot, 0:KC * f.wide].rearrange("p (k n) -> p k n", k=KC)
            w2 = w[0:f.kh, slot, KC * f.wide:KC * f.wide + f.kt * C].rearrange("p (k n) -> p k n", k=f.kt)
            return w1, w2

        @block.sync
        def _(sp):
            def load_x(L, src):
                v = src.rearrange("(i p) c -> p i c", p=P)
                for g, done in enumerate((lay[L].x_in0, lay[L].x_in1, lay[L].x_in2)):
                    sp.dma_start(xres[:, 4 * g:4 * g + 4, :], v[:, 4 * g:4 * g + 4, :]).then_inc(done, 16)

            def load_conv(L):
                w_qkv, w_proj, b_proj = conv_w[L]
                sp.dma_start(wqkv[:, :, :], w_qkv.rearrange("(k p) n -> p k n", p=P)).then_inc(lay[L].conv_in, 16)
                sp.dma_start(wproj[:, :, :], w_proj.rearrange("(k p) n -> p k n", p=P)).then_inc(lay[L].conv_in, 16)
                sp.dma_start(bproj[:, :], b_proj.partition_broadcast(P)).then_inc(lay[L].conv_in, 16)

            def load_route(L):
                router, router_b = ffn_w[L][0:2]
                sp.dma_start(wroute[:, :, :], router.rearrange("(k p) n -> p k n", p=P)).then_inc(lay[L].route_in, 16)
                if router_b is not None:
                    sp.dma_start(broute[:, :], router_b.partition_broadcast(P)).then_inc(lay[L].route_in, 16)

            def load_biases(L):
                f = FFN[L]
                for q in range(3):
                    for src, to in ((ffn_w[L][3], slice(0, f.wide)), (ffn_w[L][5], slice(f.wide, f.wide + C))):
                        sp.dma_start(bias_raw[32 * q:32 * q + E, to], src).then_inc(lay[L].bias_in, 16)

            def load_expert(L, e, half):
                f = FFN[L]
                w1, w2 = expert_views(raw, L, half)
                sp.dma_start(w1, ffn_w[L][2][e].rearrange("(k p) n -> p k n", p=P)).then_inc(raw_dma[half], 16)
                sp.dma_start(w2, ffn_w[L][4][e].rearrange("(k p) n -> p k n", p=f.kh)).then_inc(raw_dma[half], 16)
                loads[half] += 2

            def expert_loaded(L, half):
                sp.wait_ge(raw_dma[half], 16 * loads[half])
                sp.sem_inc(lay[L].raw_ready, 1)

            loads = [0, 0]
            load_x(0, x_rows)
            load_conv(0)
            load_route(0)
            for L in range(2):
                s = lay[L]
                for e in range(SLOTS + 1):
                    if e == SLOTS:
                        sp.wait_ge(s.av_mm, 8)
                        if L == 0:
                            sp.wait_ge(const_done, 2)
                        load_biases(L)
                    if e >= 1:
                        sp.wait_ge(s.pool_split, e)
                    if (L, e) != (1, 0):
                        load_expert(L, e, 0)
                    if e < SLOTS:
                        expert_loaded(L, 0)
                dst = (mid_dram, out_rows)[L].rearrange("(i p) c -> p i c", p=P)
                xn_v = xn_dram.rearrange("(i p) c -> p i c", p=P)
                for g in range(3):
                    sp.wait_ge(s.xn2, 4 * (g + 1))
                    sp.dma_start(xn_v[:, 4 * g:4 * g + 4, :], xn2[:, 4 * g:4 * g + 4, :]).then_inc(s.store, 16)
                    sp.dma_start(dst[:, 4 * g:4 * g + 4, :], xres[:, 4 * g:4 * g + 4, :]).then_inc(s.store, 16)
                sp.wait_ge(s.store, 6 * 16)
                sp.wait_ge(s.xn2T_mm, 6)
                expert_loaded(L, 0)
                load_expert(L, SLOTS + 1, 1)
                if L == 0:
                    load_conv(1)
                    sp.wait_ge(s.lg, 1)
                    load_route(1)
                expert_loaded(L, 1)
                for e in range(SLOTS + 2, E):
                    sp.wait_ge(s.w_lo, PIECES * (e - 1))
                    load_expert(L, e, (e - SLOTS) % 2)
                    expert_loaded(L, (e - SLOTS) % 2)
                if L == 0:
                    sp.wait_ge(s.w_lo, PIECES * E)
                    load_expert(1, 0, 0)
                    sp.wait_ge(s.moe_done, 1)
                    load_x(1, mid_dram)
            sp.wait_ge(lay[1].moe_done, 1)

        @block.gpsimd
        def _(pool):
            cc = [0]

            def made(ins):
                cc[0] += 1
                ins.then_inc(made_seq, 1)
                pool.wait_ge(made_seq, cc[0])

            made(pool.memset(ident[:, :], 0.0))
            made(pool.affine_select(out=ident[:, :], in_=ident[:, :], compare_op=ALU.not_equal, fill=1.0, base=0,
                                    pattern=[[-1, P]], channel_multiplier=1))
            made(pool.memset(q_mask[:, :], float(HD) ** -0.5 / PIX ** 2))
            made(pool.affine_select(out=q_mask[:, :], in_=q_mask[:, :], compare_op=ALU.is_ge, fill=0.0, base=0,
                                    pattern=[[-HD, HPH]], channel_multiplier=1))
            made(pool.affine_select(out=q_mask[:, :], in_=q_mask[:, :], compare_op=ALU.is_ge, fill=0.0, base=HD - 1,
                                    pattern=[[HD, HPH]], channel_multiplier=-1))
            made(pool.memset(batch_mask[:, :, :], 0.0))
            made(pool.affine_select(out=batch_mask[:, :, :], in_=batch_mask[:, :, :], compare_op=ALU.is_ge, fill=NEG,
                                    base=0, pattern=[[-N, B], [0, N]], channel_multiplier=1))
            made(pool.affine_select(out=batch_mask[:, :, :], in_=batch_mask[:, :, :], compare_op=ALU.is_ge, fill=NEG,
                                    base=N - 1, pattern=[[N, B], [0, N]], channel_multiplier=-1))
            pool.sem_inc(const_done, 1)

            def biases(L):
                s = lay[L]
                pool.wait_ge(s.bias_cast, 1)
                pool.tensor_tensor(bias_raw[:, :], bias_raw[:, :], bias_rows[:, :], ALU.subtract).then_inc(s.bias_sub, 1)
                pool.wait_ge(s.bias_cast, 3)
                pool.tensor_tensor(bias_raw[64:96, :], bias_raw[64:96, :], bias_rows[64:96, :], ALU.subtract
                                   ).then_inc(s.bias_sub, 1)
                pool.wait_ge(s.bias_sub, 2)

            made(pool.memset(region_d[:, HEADS * BN:BIAS_WIDE], 0.0))
            made(pool.memset(after_or_at[:, :], -1.0))
            made(pool.affine_select(out=after_or_at[:, :], in_=after_or_at[:, :], compare_op=ALU.is_ge, fill=0.0,
                                    base=0, pattern=[[-1, P]], channel_multiplier=1))
            made(pool.memset(ones[:, :], 1.0))
            made(pool.iota(iota_i[:, :], pattern=[[1, P]], base=0, channel_multiplier=0))
            made(pool.tensor_copy(iota[:, :], iota_i[:, :]))
            made(pool.tensor_scalar(expert_m8[:, :], iota[:, 0:E], float(E), None, ALU.subtract))
            made(pool.iota(token_i[:, :], pattern=[[P, TILES]], base=1, channel_multiplier=1))
            made(pool.tensor_copy(token_id[:, :], token_i[:, :]))
            if SLOT_WORDS > WORDS[0]:
                made(pool.memset(raw[:, :, WORDS[0]:SLOT_WORDS], 0.0))
            made(pool.memset(gather_tab[:, TAB:TABLE], 0))
            made(pool.memset(scan_keep[:, :, :], 1.0))
            made(pool.memset(scan_keep[:, :, 0:1], 0.0))
            made(pool.memset(expert_sel[:, :, :], 0.0))
            for q in range(3):
                made(pool.affine_select(out=expert_sel[:, :, :], in_=expert_sel[:, :, :], compare_op=ALU.not_equal,
                                        fill=1.0, base=-32 * q, pattern=[[-1, E], [0, P]], channel_multiplier=1))
            pool.sem_inc(const_done, 1)

            for L in range(2):
                s = lay[L]
                pool.wait_ge(s.conv_in, 48)
                pool.wait_ge(s.xn, TILES)
                pool.tensor_tensor(xres[:, :, :], xres[:, :, :], bproj[:, :].unsqueeze(1).to_broadcast([P, TILES, C]),
                                   ALU.add).then_inc(s.bias_added, 1)
                for e in range(SLOTS):
                    pool.wait_ge(s.first_hi, e + 1 if e < SLOTS - 1 else SLOTS + 1)
                    pool.tensor_tensor(w_lo[:, e, 0:WORDS[L]], raw[:, 0, 0:WORDS[L]],
                                       w_hi[:, e, 0:WORDS[L]].bitcast(F32), ALU.subtract).then_inc(s.pool_split, 1)
                biases(L)
                for v, value in ((0, token_id[:, :].unsqueeze(1).to_broadcast([P, TOPK, TILES])),
                                 (1, gate_hi[:, :, :].bitcast(F32)), (2, gate[:, :, :])):
                    pool.wait_ge(s.blk_hot, 1 if v == 0 else 2)
                    pool.tensor_tensor(onehot_blk[:, :, v, :].rearrange("p (k i) b -> p k i b", k=TOPK),
                                       blk_hot[:, :, :].rearrange("p (k i) b -> p k i b", k=TOPK),
                                       value.unsqueeze(3).to_broadcast([P, TOPK, TILES, TAB]), ALU.mult
                                       ).then_inc(s.hot_blk, 1)
                    pool.wait_ge(s.hot_blk, v + 1)
                acc = (mid_dram, out_rows)[L]
                pool.wait_ge(s.store, 6 * 16)
                pool.wait_ge(s.tab, 2)

                def gather(b):
                    if after(b, 1):
                        pool.wait_ge(s.xT_mm, b)
                        pool.wait_ge(s.gathered, 16 * b)
                    pool.tensor_copy(gcol[:, :], col(gather_tab, b)).then_inc(s.gcol, 1)
                    pool.wait_ge(s.gcol, b + 1)
                    pool.sem_inc(s.rows_go, 1)
                    pool.indirect_dma_start(out=xg, out_offset=None, in_=xn_dram,
                                            in_offset=bass.IndirectOffsetOnAxis(ap=gcol[:, :], axis=0)
                                            ).then_inc(s.gathered, 16)

                def scatter(b):
                    if after(b, 1):
                        pool.wait_ge(s.added, 16 * b)
                    pool.tensor_copy(scol[:, :], col(scatter_tab, b)).then_inc(s.scol, 1)
                    pool.wait_ge(s.scol, b + 1)
                    pool.wait_ge(s.e_sb, b + 1)
                    pool.sem_inc(s.rows_go, 1)
                    pool.indirect_dma_start(out=acc, out_offset=bass.IndirectOffsetOnAxis(ap=scol[:, :], axis=0),
                                            in_=y_sb, in_offset=None, bounds_check=TOKENS - 1,
                                            oob_is_err=False, compute_op=ALU.add).then_inc(s.added, 16)

                gather(0)
                pool.wait_ge(s.tab, 3)
                gather(1)

                def step(b, last=False):
                    if not last:
                        gather(b + 2)
                    if after(b, 1):
                        scatter(b - 1)
                    if last:
                        pool.wait_ge(s.added, 16 * b)
                        pool.wait_ge(s.gathered, 16 * b + 32)
                        pool.sem_inc(s.moe_done, 1)

                block_loop(pool, step)

        @block.scalar
        def _(act):
            for L in range(2):
                s, f = lay[L], FFN[L]

                def stds(var, done, eps):
                    for g in range(3):
                        act.wait_ge(var, 4 * (g + 1))
                        nc.scalar.activation(std[:, 4 * g:4 * g + 4], mean_var[:, 4 * g:4 * g + 4, 1], ACT.Sqrt
                                             ).then_inc(done, 1)

                def first_high(e):
                    act.wait_ge(s.raw_ready, e + 1)
                    nc.scalar.copy(w_hi[:, e, 0:WORDS[L]], raw[:, 0, 0:WORDS[L]]).then_inc(s.first_hi, 1)

                stds(s.var, s.std, LN_EPS[0])
                for j in range(6):
                    act.wait_ge(s.xnT_mm, j + 1)
                    nc.scalar.copy(xnT[:, :, 2 * j * P:2 * (j + 1) * P].rearrange("p k (i t) -> p i k t", i=2),
                                   bank[j % 4][:, :].rearrange("p (i k t) -> p i k t", i=2, k=KC)).then_inc(s.xnT, 1)
                first_high(0)
                for j in range(8):
                    act.wait_ge(s.v_mm, j + 1)
                    if L == 1 and j == 0:
                        act.wait_ge(lay[0].store, 96)
                    nc.scalar.copy(v_sb[:, 2 * j:2 * j + 2, :],
                                   bank[6 + j % 2][0:BN, :].rearrange("p (q c) -> p q c", q=2)).then_inc(s.v, 1)
                    if j % 2 == 1:
                        g = j // 2
                        act.wait_ge(s.sub, g + 1)
                        nc.scalar.activation(probs[:, GROUP * g:GROUP * g + GROUP, :],
                                             probs[:, GROUP * g:GROUP * g + GROUP, :], ACT.Exp).then_inc(s.expd, 1)
                for g in range(HGROUPS):
                    act.wait_ge(s.aT_mm, g + 1)
                    nc.scalar.copy(attnT[:, GROUP * g:GROUP * g + GROUP, :],
                                   bank[4 + g % 2][0:BN, 0:GROUP * BN].rearrange("p (h n) -> p h n", h=GROUP)
                                   ).then_inc(s.aT, 1)
                first_high(1)
                for j in range(0, 8, 2):
                    act.wait_ge(s.av_mm, j + 1)
                    if j == 0:
                        act.wait_ge(s.aT_mm, HGROUPS)
                    nc.scalar.copy(o_sb[:, :, 2 * HD * j:2 * HD * (j + 1)].rearrange("p q (h d) -> p h q d", h=2),
                                   bank[j % 4][0:BN, :].rearrange("p (h q d) -> p h q d", h=2, q=PIX)
                                   ).then_inc(s.o_act, 1)
                for j in range(0, 8, 2):
                    act.wait_ge(s.oT_mm, j + 1)
                    nc.scalar.copy(outT[:, j // 4, :, 4 * (j % 4):4 * (j % 4) + 4].rearrange("p n q -> p q n"),
                                   bank[4 + j % 4][:, 0:4 * BN].rearrange("p (q n) -> p q n", q=4)).then_inc(s.oT_act, 1)
                stds(s.var2, s.std2, LN_EPS[1])
                for j in range(6):
                    act.wait_ge(s.xn2T_mm, j + 1)
                    if j >= 4:
                        act.wait_ge(s.lg_mm, j - 3)
                    nc.scalar.copy(xn2T[:, j % 4, :, :, :],
                                   bank[4 + j % 4][:, :].rearrange("p (i k t) -> p i k t", i=2, k=KC)
                                   ).then_inc(s.xn2T, 1)
                    if j < 2:
                        cols = slice(j * WORDS[L] // 2, (j + 1) * WORDS[L] // 2)
                        act.wait_ge(s.raw_ready, SLOTS)
                        nc.scalar.copy(w_hi[:, 2, cols], raw[:, 0, cols]).then_inc(s.first_hi, 1)
                    elif j == 2:
                        act.wait_ge(s.bias_in, 6 * 16)
                        if L == 1:
                            act.wait_ge(lay[0].moe_done, 1)
                        nc.scalar.copy(bias_rows[:, :], bias_raw[:, :]).then_inc(s.bias_cast, 1)
                act.wait_ge(s.bias_sub, 1)
                nc.scalar.copy(bias_rows[32:64, :], bias_raw[32:64, :]).then_inc(s.bias_cast, 1)
                nc.scalar.copy(bias_rows[64:96, :], bias_raw[64:96, :]).then_inc(s.bias_cast, 1)
                act.wait_ge(s.top2, 1)
                if L == 0:
                    nc.scalar.activation(prob8[:, :, :], prob8[:, :, :], ACT.Exp).then_inc(s.exp8, 1)
                nc.scalar.activation(small[:, 0, :], small[:, 0, :], ACT.Exp).then_inc(s.exp8, 1)

                act.wait_ge(s.bias_sub, 2)
                nc.scalar.copy(bias_rows[64:96, :], bias_raw[64:96, :]).then_inc(s.bias_cast, 1)
                act.wait_ge(s.tab, 1)
                half = f.kt // 2

                def xT_high(b):
                    act.wait_ge(s.xT_mm, b + 1)
                    if after(b, 1):
                        act.wait_ge(s.h_mm, f.chunks * b)
                    nc.scalar.copy(xT_hi[:, :, :], bank[7][:, 0:C].rearrange("p (k s) -> p k s", k=KC)
                                   ).then_inc(s.xT_hi, 1)

                def split(q, b):
                    act.wait_ge(s.e_mm, b - 1)
                    act.wait_ge(s.raw_ready, q // PIECES + SLOTS + 1)
                    w = WORDS[L] // PIECES
                    at = bass.ds((q % PIECES) * w, w)
                    nc.scalar.copy(w_hi[:, (q // PIECES) % SLOTS, at], raw[:, (q // PIECES) % 2, at]
                                   ).then_inc(s.w_hi, 1)

                def step(b, last=False):
                    if not last:
                        pieces = piece_range(act, b)
                    if after(b, 1):
                        for j in range(2):
                            act.wait_ge(s.hT_mm, 2 * b - 1 + j)
                            if after(b, 2):
                                act.wait_ge(s.e_mm, b - 1)
                            nc.scalar.copy(hT_hi[0:f.kh, half * j:half * (j + 1), :],
                                           bank[4 + j][0:f.kh, 0:half * P].rearrange("p (k s) -> p k s", s=P)
                                           ).then_inc(s.hT_hi, 1)
                    if last:
                        return
                    for j in range(2):
                        act.wait_ge(s.h_mm, f.chunks * b + j + 1)
                        if L == 0:
                            if after(b, 1):
                                act.wait_ge(s.hT_mm, 2 * b)
                            nc.scalar.activation(h_sb[:, f.chunk * j:f.chunk * (j + 1)], bank[j][:, 0:f.chunk],
                                                 ACT.Silu).then_inc(s.h, 1)
                        else:
                            if after(b, 1):
                                act.wait_ge(s.h, 2 * b)
                            nc.scalar.activation(silu_g[:, f.chunk * j:f.chunk * (j + 1)], bank[j][:, 0:f.chunk],
                                                 ACT.Silu).then_inc(s.silu, 1)
                    xT_high(b + 1)
                    for_pieces(act, pieces, lambda q: split(q, b))

                xT_high(0)
                block_loop(act, step)

        @block.vector
        def _(dve):
            for L in range(2):
                s, f = lay[L], FFN[L]
                nchain = [0]

                def chain(ins):
                    nchain[0] += 1
                    ins.then_inc(s.chain, 1)
                    dve.wait_ge(s.chain, nchain[0])

                def stats_of(tiles, done, eps):
                    for i in tiles:
                        nc.vector.bn_stats(stats[:, i, :], xres[:, i, :]).then_inc(s.stat, 1)
                    dve.wait_ge(s.stat, nstat[0] + len(tiles))
                    nstat[0] += len(tiles)
                    for i in tiles:
                        nc.vector.bn_aggr(mean_var[:, i, :], stats[:, i, :]).then_inc(s.stat, 1)
                    nstat[0] += len(tiles)
                    dve.wait_ge(s.stat, nstat[0])
                    a, b = tiles[0], tiles[-1] + 1
                    nc.vector.tensor_scalar(mean_var[:, a:b, 1], mean_var[:, a:b, 1], eps, None,
                                            ALU.add).then_inc(done, len(tiles))

                def normalise(tiles, std_done, dst, done):
                    g = tiles[0] // 4
                    dve.wait_ge(std_done, g + 1)
                    chain(nc.vector.reciprocal(rstd[:, tiles[0]:tiles[-1] + 1], std[:, tiles[0]:tiles[-1] + 1]))
                    for i in tiles:
                        nc.vector.tensor_scalar(dst[:, i, :], xres[:, i, :], mean_var[:, i, 0:1], rstd[:, i:i + 1],
                                                ALU.subtract, ALU.mult).then_inc(done, 1)

                nstat = [0]
                if L == 1:
                    dve.wait_ge(lay[0].std2, 3)
                    dve.wait_ge(lay[0].moe_done, 1)
                for g in range(4):
                    if g < 3:
                        dve.wait_ge((s.x_in0, s.x_in1, s.x_in2)[g], 16)
                        stats_of(range(4 * g, 4 * g + 4), s.var, LN_EPS[0])
                    if g >= 1:
                        normalise(range(4 * g - 4, 4 * g), s.std, xn, s.xn)
                if L == 0:
                    dve.wait_ge(const_done, 1)
                for j in range(6):
                    dve.wait_ge(s.xnT, j + 1)
                    nc.vector.tensor_reduce(xm[:, :, 2 * NPT * j:2 * NPT * (j + 1)],
                                            xnT[:, :, 2 * P * j:2 * P * (j + 1)]
                                            .rearrange("p k (n q) -> p k n q", q=PIX), AX.X, ALU.add
                                            ).then_inc(s.xm, 1)
                dve.wait_ge(s.qk_mm, 1)
                qk = bank[5][:, 0:4 * BN].rearrange("p (v k n) -> p v k n", v=2, k=KC)
                nc.vector.tensor_copy(kT[:, :, :], qk[:, 1, :, :]).then_inc(s.k_sb, 1)
                for k in range(KC):
                    nc.vector.tensor_tensor(qmask[:, HPH * k:HPH * (k + 1), :],
                                            qk[:, 0, k, :].unsqueeze(1).to_broadcast([P, HPH, BN]),
                                            q_mask[:, :].unsqueeze(2).to_broadcast([P, HPH, BN]),
                                            ALU.mult).then_inc(s.qm, 1)
                def heads(g):
                    return slice(GROUP * g, GROUP * (g + 1))

                def sm_front(g):
                    dve.wait_ge(s.s_mm, g + 1)
                    chain(nc.vector.tensor_tensor(probs[:, heads(g), :],
                                                  bank[g][0:BN, 0:GROUP * BN].rearrange("p (h m) -> p h m", h=GROUP),
                                                  batch_mask[:, :, :].rearrange("p b n -> p (b n)").unsqueeze(1)
                                                  .to_broadcast([BN, GROUP, BN]), ALU.add))
                    chain(nc.vector.tensor_reduce(row_max[:, heads(g)], probs[:, heads(g), :], AX.X, ALU.max))
                    nc.vector.tensor_tensor(probs[:, heads(g), :], probs[:, heads(g), :],
                                            row_max[:, heads(g)].unsqueeze(2).to_broadcast([BN, GROUP, BN]),
                                            ALU.subtract).then_inc(s.sub, 1)

                def sm_back(g):
                    dve.wait_ge(s.expd, g + 1)
                    chain(nc.vector.tensor_reduce(row_sum[:, heads(g)], probs[:, heads(g), :], AX.X, ALU.add))
                    chain(nc.vector.reciprocal(row_sum[:, heads(g)], row_sum[:, heads(g)]))
                    nc.vector.tensor_tensor(probs[:, heads(g), :], probs[:, heads(g), :],
                                            row_sum[:, heads(g)].unsqueeze(2).to_broadcast([BN, GROUP, BN]),
                                            ALU.mult).then_inc(s.attn, 1)

                for g in range(HGROUPS + 1):
                    if g < HGROUPS:
                        sm_front(g)
                    if g >= 1:
                        sm_back(g - 1)
                for j in range(1, 8, 2):
                    dve.wait_ge(s.av_mm, j + 1)
                    if j == 1:
                        dve.wait_ge(s.aT_mm, HGROUPS)
                    nc.vector.tensor_copy(o_sb[:, :, 2 * HD * j:2 * HD * (j + 1)].rearrange("p q (h d) -> p h q d", h=2),
                                          bank[j % 4][0:BN, :].rearrange("p (h q d) -> p h q d", h=2, q=PIX)
                                          ).then_inc(s.o_dve, 1)
                for j in range(1, 8, 2):
                    dve.wait_ge(s.oT_mm, j + 1)
                    nc.vector.tensor_copy(outT[:, j // 4, :, 4 * (j % 4):4 * (j % 4) + 4].rearrange("p n q -> p q n"),
                                          bank[4 + j % 4][:, 0:4 * BN].rearrange("p (q n) -> p q n", q=4)
                                          ).then_inc(s.oT_dve, 1)
                dve.wait_ge(s.bias_added, 1)
                for g in range(4):
                    for j in (2 * g, 2 * g + 1) if g < 3 else ():
                        dve.wait_ge(s.y_mm, j + 1)
                        nc.vector.tensor_tensor(xres[:, 2 * j:2 * j + 2, :], xres[:, 2 * j:2 * j + 2, :],
                                                bank[j % 3][:, :].rearrange("p (i c) -> p i c", i=2), ALU.add
                                                ).then_inc(s.x1, 1)
                    if g == 0:
                        dve.wait_ge(s.std, 3)
                        dve.wait_ge(s.xn, TILES)
                        dve.wait_ge(s.av_mm, 8)
                    if g < 3:
                        dve.wait_ge(s.x1, 2 * g + 2)
                        stats_of(range(4 * g, 4 * g + 4), s.var2, LN_EPS[1])
                    if g >= 1:
                        normalise(range(4 * g - 4, 4 * g), s.std2, xn2, s.xn2)
                dve.wait_ge(s.lg_mm, 6)
                lgp = bank[3][:, 0:TILES * E].rearrange("p (i e) -> p i e", i=TILES)

                def tiles_bc(a):
                    return a.unsqueeze(2).to_broadcast([P, TILES, E])

                def experts_bc(a):
                    return a.unsqueeze(1).to_broadcast([P, TILES, E])

                if L == 0:
                    dve.wait_ge(const_done, 2)
                    nc.vector.tensor_tensor(logits[:, :, :], lgp, experts_bc(broute[:, :]), ALU.add).then_inc(s.lg, 1)
                else:
                    nc.vector.tensor_copy(logits[:, :, :], lgp).then_inc(s.lg, 1)
                dve.wait_ge(s.lg, 1)
                cur = logits
                for k in range(TOPK):
                    chain(nc.vector.tensor_reduce(m_top[:, k, :], cur[:, :, :], AX.X, ALU.max))
                    chain(nc.vector.tensor_tensor(cand[:, :, :], cur[:, :, :], tiles_bc(m_top[:, k, :]), ALU.is_equal))
                    chain(nc.vector.tensor_tensor(cand[:, :, :], cand[:, :, :], experts_bc(expert_m8[:, :]), ALU.mult))
                    chain(nc.vector.tensor_reduce(i_top[:, k, :], cand[:, :, :], AX.X, ALU.min))
                    chain(nc.vector.tensor_tensor(pick[:, k, :, :].rearrange("p e i -> p i e"),
                                                  experts_bc(expert_m8[:, :]), tiles_bc(i_top[:, k, :]), ALU.is_equal))
                    if k == 0:
                        chain(nc.vector.scalar_tensor_tensor(out=lg2[:, :, :],
                                                             in0=pick[:, 0, :, :].rearrange("p e i -> p i e"),
                                                             scalar=NEG, in1=logits[:, :, :],
                                                             op0=ALU.mult, op1=ALU.add))
                        cur = lg2
                if L == 0:
                    chain(nc.vector.tensor_tensor(prob8[:, :, :], logits[:, :, :], tiles_bc(m_top[:, 0, :]),
                                                  ALU.subtract))
                nc.vector.tensor_tensor(small[:, 0, :], m_top[:, 1, :], m_top[:, 0, :], ALU.subtract).then_inc(s.top2, 1)
                nc.vector.tensor_tensor(picked[:, :, :], pick[:, 0, :, :], pick[:, 1, :, :], ALU.add
                                        ).then_inc(s.top2, 1)
                dve.wait_ge(s.cnt_mm, 2)
                from_here = bank[4][:, 0:E * TILES].rearrange("p (e i) -> p e i", e=E)
                total = bank[4][:, E * TILES:2 * E * TILES].rearrange("p (e i) -> p e i", e=E)
                flat = "p e i -> p (e i)"
                chain(nc.vector.tensor_tensor_scan(incl[:, :, :].rearrange(flat), scan_keep[:, :, :].rearrange(flat),
                                                   total.rearrange(flat), 0.0, ALU.mult, ALU.add))
                chain(nc.vector.tensor_tensor(place[:, :, :], incl[:, :, :], from_here, ALU.add))
                chain(nc.vector.tensor_scalar(cnt_i[:, 0, :], incl[:, :, TILES - 1], float(P - 1), None, ALU.add))
                chain(nc.vector.tensor_scalar(cnt_i[:, 1, :], cnt_i[:, 0, :], 7, None, ALU.arith_shift_right))
                chain(nc.vector.tensor_scalar(nblk[:, :], cnt_i[:, 1, :], 1.0, None, ALU.max))
                chain(nc.vector.tensor_tensor_scan(endblk[:, :], scan_keep[:, 0, 1:1 + E], nblk[:, :], 0.0, ALU.mult, ALU.add))
                chain(nc.vector.tensor_tensor(base[:, :], endblk[:, :], nblk[:, :], ALU.subtract))
                chain(nc.vector.scalar_tensor_tensor(out=place[:, :, :], in0=base[:, :].unsqueeze(2)
                                                     .to_broadcast([P, E, TILES]), scalar=float(P),
                                                     in1=place[:, :, :], op0=ALU.mult, op1=ALU.add))
                chain(nc.vector.tensor_tensor(term[:, :, :, :], place[:, :, :].unsqueeze(1)
                                              .to_broadcast([P, TOPK, E, TILES]), pick[:, :, :, :], ALU.mult))
                chain(nc.vector.tensor_reduce(slot_f[:, :, :], term[:, :, :, :].rearrange("p k e i -> p k i e"),
                                              AX.X, ALU.add))
                chain(nc.vector.tensor_copy(slot_i[:, 0, :, :], slot_f[:, :, :]))
                chain(nc.vector.tensor_scalar(slot_i[:, 1, :, :], slot_i[:, 0, :, :], P - 1, None, ALU.bitwise_and))
                chain(nc.vector.tensor_scalar(slot_i[:, 2, :, :], slot_i[:, 0, :, :], 7, None, ALU.arith_shift_right))
                chain(nc.vector.tensor_copy(rowblk[:, :, :], slot_i[:, 1:3, :, :].rearrange("p v k i -> p v (k i)")))
                nc.vector.tensor_tensor(blk_hot[:, :, :],
                                        iota[:, 0:TAB].unsqueeze(1).to_broadcast([P, PAIRS, TAB]),
                                        rowblk[:, 1, :].unsqueeze(2).to_broadcast([P, PAIRS, TAB]),
                                        ALU.is_equal).then_inc(s.blk_hot, 1)
                if L == 0:
                    dve.wait_ge(s.exp8, 2)
                    chain(nc.vector.tensor_reduce(small[:, 1, :], prob8[:, :, :], AX.X, ALU.add))
                else:
                    dve.wait_ge(s.exp8, 1)
                    chain(nc.vector.tensor_scalar(small[:, 1, :], small[:, 0, :], 1.0, None, ALU.add))
                chain(nc.vector.reciprocal(gate[:, 0, :], small[:, 1, :]))
                chain(nc.vector.tensor_tensor(gate[:, 1, :], small[:, 0, :], gate[:, 0, :], ALU.mult))
                chain(nc.vector.tensor_copy(gate_hi[:, :, :], gate[:, :, :]))
                nc.vector.tensor_tensor(gate[:, :, :], gate[:, :, :], gate_hi[:, :, :].bitcast(F32), ALU.subtract
                                        ).then_inc(s.blk_hot, 1)
                dve.wait_ge(s.y_mm, 6)
                nc.vector.tensor_tensor(onehot_row[:, :, :], iota[:, :].unsqueeze(1).to_broadcast([P, PAIRS, P]),
                                        rowblk[:, 0, :].unsqueeze(2).to_broadcast([P, PAIRS, P]),
                                        ALU.is_equal).then_inc(s.hot_rows, 1)
                by_block = iota[0:1, 0:TABLE].unsqueeze(2).to_broadcast([1, TABLE, E])
                chain(nc.vector.tensor_tensor(blk_cmp[:, 0, :, :], by_block,
                                              endblk[0:1, :].unsqueeze(1).to_broadcast([1, TABLE, E]), ALU.is_ge))
                chain(nc.vector.tensor_reduce(blk_e[:, 0, :], blk_cmp[:, 0, :, :], AX.X, ALU.add))
                chain(nc.vector.tensor_scalar(tab_e[:, :], blk_e[:, 0, :], float(E - 1), None, ALU.min))
                chain(nc.vector.tensor_scalar(tab_blocks[:, :], endblk[0:1, E - 1:E], -float(MIN_BLOCKS), None, ALU.add))
                chain(nc.vector.tensor_tensor(blk_cmp[:, 1, :, :], blk_cmp[:, 0, :, :],
                                              nblk[0:1, :].unsqueeze(1).to_broadcast([1, TABLE, E]), ALU.mult))
                chain(nc.vector.tensor_reduce(blk_e[:, 1, :], blk_cmp[:, 1, :, :], AX.X, ALU.add))
                chain(nc.vector.tensor_tensor(blk_e[:, 1, :], iota[0:1, 0:TABLE], blk_e[:, 1, :], ALU.subtract))
                chain(nc.vector.tensor_scalar(blk_e[:, 1, :], blk_e[:, 1, :], 1.0, float(PIECES), ALU.add, ALU.min))
                chain(nc.vector.tensor_scalar(nblk[0:1, :], endblk[0:1, :], 1.0, None, ALU.subtract))
                chain(nc.vector.tensor_tensor(blk_cmp[:, 2, :, :], by_block,
                                              nblk[0:1, :].unsqueeze(1).to_broadcast([1, TABLE, E]), ALU.is_equal))
                chain(nc.vector.tensor_reduce(blk_e[:, 2, :], blk_cmp[:, 2, :, :], AX.X, ALU.add))
                chain(nc.vector.scalar_tensor_tensor(out=blk_e[:, 1, :], in0=blk_e[:, 2, :], scalar=float(PIECES),
                                                     in1=blk_e[:, 1, :], op0=ALU.mult, op1=ALU.max))
                chain(nc.vector.scalar_tensor_tensor(out=blk_e[:, 1, :], in0=blk_e[:, 0, :], scalar=float(PIECES),
                                                     in1=blk_e[:, 1, :], op0=ALU.mult, op1=ALU.add))
                chain(nc.vector.tensor_scalar(blk_e[:, 1, :], blk_e[:, 1, :], -float(PIECES), 0.0, ALU.add, ALU.max))
                nc.vector.tensor_scalar(tab_pieces[:, :], blk_e[:, 1, :], float(PIECES * (E - SLOTS)), None,
                                        ALU.min).then_inc(s.tab, 1)
                dve.wait_ge(s.tab, 1)
                dve.wait_ge(s.tab_mm, 1)
                tabp = bank[5][:, 0:3 * TAB].rearrange("p (v b) -> p v b", v=3)
                nc.vector.tensor_scalar(gather_tab[:, 0:TAB], tabp[:, 0, :], -1.0, 0.0, ALU.add, ALU.max
                                        ).then_inc(s.tab, 1)
                chain(nc.vector.tensor_scalar(id_sb[:, 0, :], tabp[:, 0, :], 0.0, float(BIG_ROW), ALU.is_equal, ALU.mult))
                chain(nc.vector.scalar_tensor_tensor(out=scatter_tab[:, 0:TAB], in0=tabp[:, 0, :], scalar=-1.0,
                                                     in1=id_sb[:, 0, :], op0=ALU.add, op1=ALU.add))
                chain(nc.vector.tensor_copy(id_sb[:, 1, :], tabp[:, 2, :]))
                nc.vector.tensor_tensor(gate_tab[:, 0:TAB], tabp[:, 1, :], id_sb[:, 1, :], ALU.add
                                        ).then_inc(s.tab, 1)
                dve.wait_ge(s.tab, 3)

                dve.wait_ge(s.pool_split, SLOTS)
                dve.sem_inc(s.w_lo, PIECES * SLOTS)
                half = f.kt // 2

                def xT_low(b):
                    dve.wait_ge(s.xT_hi, b + 1)
                    nc.vector.tensor_tensor(xT_lo[:, :, :], bank[7][:, 0:C].rearrange("p (k s) -> p k s", k=KC),
                                            xT_hi[:, :, :].bitcast(F32), ALU.subtract).then_inc(s.xT_lo, 1)

                def split(q):
                    dve.wait_ge(s.w_hi, q + 1)
                    w = WORDS[L] // PIECES
                    at = bass.ds((q % PIECES) * w, w)
                    slot = (q // PIECES) % SLOTS
                    nc.vector.tensor_tensor(w_lo[:, slot, at], raw[:, (q // PIECES) % 2, at],
                                            w_hi[:, slot, at].bitcast(F32), ALU.subtract).then_inc(s.w_lo, 1)

                xT_low(0)

                def step(b, last=False):
                    if not last:
                        pieces = piece_range(dve, b)
                    if after(b, 1):
                        for j in range(2):
                            dve.wait_ge(s.hT_hi, 2 * b - 1 + j)
                            part = slice(half * j, half * (j + 1))
                            nc.vector.tensor_tensor(hT_lo[0:f.kh, part, :],
                                                    bank[4 + j][0:f.kh, 0:half * P].rearrange("p (k s) -> p k s", s=P),
                                                    hT_hi[0:f.kh, part, :].bitcast(F32), ALU.subtract
                                                    ).then_inc(s.hT_lo, 1)
                    if L == 1 and not last:
                        for j in range(2):
                            dve.wait_ge(s.silu, 2 * b + j + 1)
                            dve.wait_ge(s.h_mm, f.chunks * b + 3 + j)
                            nc.vector.tensor_tensor(h_sb[:, f.chunk * j:f.chunk * (j + 1)], bank[2 + j][:, 0:f.chunk],
                                                    silu_g[:, f.chunk * j:f.chunk * (j + 1)], ALU.mult
                                                    ).then_inc(s.h, 1)
                    if not last:
                        xT_low(b + 1)
                        for_pieces(dve, pieces, split)
                    if after(b, 1):
                        dve.wait_ge(s.e_mm, b)
                        if after(b, 2):
                            dve.wait_ge(s.added, 16 * (b - 1))
                        nc.vector.tensor_scalar(y_sb, bank[6][:, 0:C], col(gate_tab, b - 1), None,
                                                ALU.mult).then_inc(s.e_sb, 1)

                block_loop(dve, step)

        @block.tensor
        def _(pe):
            def product(out, hi, lo, w_high, w_low, first, last):
                pe.matmul(out, hi, w_high, start=first, stop=False)
                pe.matmul(out, hi, w_low, start=False, stop=False)
                return pe.matmul(out, lo, w_high, start=False, stop=last)

            pe.wait_ge(const_done, 1)
            for L in range(2):
                s, f = lay[L], FFN[L]
                for j in range(6):
                    pe.wait_ge(s.xn, 2 * j + 2)
                    if j >= 4:
                        pe.wait_ge(s.xnT, j - 3)
                    for i in range(2):
                        for k in range(KC):
                            mm = pe.transpose(bank[j % 4][:, (2 * i + k) * P:(2 * i + k + 1) * P],
                                              xn[:, 2 * j + i, k * P:(k + 1) * P], ident[:, :])
                    mm.then_inc(s.xnT_mm, 1)
                pe.wait_ge(s.xm, 6)
                pe.wait_ge(s.conv_in, 48)
                for v in range(2):
                    for m in range(KC):
                        for k in range(KC):
                            o = (KC * v + m) * BN
                            mm = pe.matmul(bank[5][:, o:o + BN], wqkv[:, k, v * C + m * P:v * C + (m + 1) * P],
                                           xm[:, k, :], start=(k == 0), stop=(k == KC - 1))
                mm.then_inc(s.qk_mm, 1)

                def values(j):
                    if j >= 2:
                        pe.wait_ge(s.v, j - 1)
                    for q in range(2):
                        for k in range(KC):
                            toks = xnT[:, k, :].rearrange("p (n q) -> p q n", q=PIX)[:, 2 * j + q, :]
                            mm = pe.matmul(bank[6 + j % 2][0:BN, q * C:(q + 1) * C], toks, wqkv[:, k, 2 * C:3 * C],
                                           start=(k == 0), stop=(k == KC - 1))
                    mm.then_inc(s.v_mm, 1)

                pe.wait_ge(s.xnT, 6)
                values(0)
                pe.wait_ge(s.k_sb, 1)
                for g in range(HGROUPS):
                    pe.wait_ge(s.qm, g // 2 + 1)
                    for h in range(GROUP * g, GROUP * (g + 1)):
                        o = (h - GROUP * g) * BN
                        mm = pe.matmul(bank[g][0:BN, o:o + BN], qmask[:, h, :], kT[:, h // HPH, :],
                                       start=True, stop=True)
                    mm.then_inc(s.s_mm, 1)
                for j in range(1, 8):
                    values(j)
                for g in range(HGROUPS):
                    pe.wait_ge(s.attn, g + 1)
                    if g >= 2:
                        pe.wait_ge(s.aT, g - 1)
                    for h in range(GROUP * g, GROUP * (g + 1)):
                        o = (h - GROUP * g) * BN
                        mm = pe.transpose(bank[4 + g % 2][0:BN, o:o + BN], probs[:, h, :], ident[0:BN, 0:BN])
                    mm.then_inc(s.aT_mm, 1)
                pe.wait_ge(s.v, 8)
                for j in range(8):
                    pe.wait_ge(s.aT, j // 2 + 1)
                    if j >= 4:
                        pe.wait_ge((s.o_act, s.o_dve)[j % 2], (j - 4) // 2 + 1)
                    for h in (2 * j, 2 * j + 1):
                        o = (h - 2 * j) * C
                        mm = pe.matmul(bank[j % 4][0:BN, o:o + C], attnT[:, h, :], v_sb[:, :, h * HD:(h + 1) * HD],
                                       start=True, stop=True)
                    mm.then_inc(s.av_mm, 1)
                pe.wait_ge(s.o_act, 4)
                pe.wait_ge(s.o_dve, 4)
                for j in range(8):
                    k, q0 = j // 4, 4 * (j % 4)
                    if j >= 4:
                        pe.wait_ge((s.oT_act, s.oT_dve)[j % 2], (j - 4) // 2 + 1)
                    for q in range(4):
                        mm = pe.transpose(bank[4 + j % 4][:, q * BN:(q + 1) * BN], o_sb[:, q0 + q, k * P:(k + 1) * P],
                                          ident[0:BN, 0:BN])
                    mm.then_inc(s.oT_mm, 1)
                pe.wait_ge(s.oT_act, 4)
                pe.wait_ge(s.oT_dve, 4)
                for j in range(6):
                    if j >= 3:
                        pe.wait_ge(s.x1, j - 2)
                    for i in range(2):
                        n = NPT * (2 * j + i)
                        for k in range(KC):
                            mm = pe.matmul(bank[j % 3][:, i * C:(i + 1) * C], outT[:, k, n:n + NPT, :], wproj[:, k, :],
                                           start=(k == 0), stop=(k == KC - 1))
                    mm.then_inc(s.y_mm, 1)
                pe.wait_ge(s.route_in, 32 if L == 0 else 16)

                def route(j):
                    pe.wait_ge(s.xn2T, j + 1)
                    for i in range(2):
                        for k in range(KC):
                            o = (2 * j + i) * E
                            mm = pe.matmul(bank[3][:, o:o + E], xn2T[:, j % 4, i, k, :], wroute[:, k, :],
                                           start=(k == 0), stop=(k == KC - 1))
                    mm.then_inc(s.lg_mm, 1)

                for j in range(6):
                    pe.wait_ge(s.xn2, 2 * j + 2)
                    if j >= 4:
                        pe.wait_ge(s.xn2T, j - 3)
                    for i in range(2):
                        for k in range(KC):
                            mm = pe.transpose(bank[4 + j % 4][:, (2 * i + k) * P:(2 * i + k + 1) * P],
                                              xn2[:, 2 * j + i, k * P:(k + 1) * P], ident[:, :])
                    mm.then_inc(s.xn2T_mm, 1)
                    if j >= 1:
                        route(j - 1)
                route(5)
                pe.wait_ge(s.top2, 2)
                if L == 0:
                    pe.wait_ge(const_done, 2)
                for n, m in ((0, after_or_at), (1, ones)):
                    pe.matmul(bank[4][:, n * E * TILES:(n + 1) * E * TILES], m[:, :],
                              picked[:, :, :].rearrange("p e i -> p (e i)"), start=True, stop=True
                              ).then_inc(s.cnt_mm, 1)
                pe.wait_ge(s.hot_rows, 1)
                pe.wait_ge(s.hot_blk, 3)
                for j in range(PAIRS):
                    mm = pe.matmul(bank[5][:, 0:3 * TAB], onehot_row[:, j, :],
                                   onehot_blk[:, j, :, :].rearrange("p v b -> p (v b)"),
                                   start=(j == 0), stop=(j == PAIRS - 1))
                mm.then_inc(s.tab_mm, 1)
                pe.wait_ge(s.bias_cast, 4)
                pe.wait_ge(s.tab, 1)

                def x_transpose(b):
                    pe.wait_ge(s.gathered, 16 * b + 16)
                    if after(b, 1):
                        pe.wait_ge(s.xT_lo, b)
                    for k in range(KC):
                        mm = pe.transpose(bank[7][:, k * P:(k + 1) * P], xg[:, k * P:(k + 1) * P], ident[:, :])
                    mm.then_inc(s.xT_mm, 1)

                half = f.kt // 2
                order = (0, 1) if L == 0 else (2, 3, 0, 1)

                def expert_of(b):
                    return pe.value_load(col(tab_e, b), min_val=0, max_val=E - 1)

                def first_product(b, e):
                    pe.wait_ge(s.xT_lo, b + 1)
                    pe.wait_ge(s.w_lo, e * PIECES + PIECES)
                    high, _ = expert_views(w_hi, L, e % SLOTS)
                    low, _ = expert_views(w_lo, L, e % SLOTS)
                    for n, c in enumerate(order):
                        cs = slice(c * f.chunk, (c + 1) * f.chunk)
                        pe.matmul(bank[n][:, 0:f.chunk], expert_sel[:, e, :], bias_rows[:, cs],
                                  start=True, stop=False)
                        for k in range(KC):
                            mm = product(bank[n][:, 0:f.chunk], xT_hi[:, k, :], xT_lo[:, k, :], high[:, k, cs],
                                         low[:, k, cs], False, k == KC - 1)
                        mm.then_inc(s.h_mm, 1)

                def h_transpose(b):
                    for j in range(2):
                        pe.wait_ge(s.h, 2 * b + 1 + j)
                        if after(b, 1):
                            pe.wait_ge(s.hT_lo, 2 * b - 1 + j)
                        for k in range(half):
                            o = (j * half + k) * f.kh
                            mm = pe.transpose(bank[4 + j][0:f.kh, k * P:(k + 1) * P], h_sb[:, o:o + f.kh],
                                              ident[:, :])
                        mm.then_inc(s.hT_mm, 1)

                def second_product(b, e):
                    _, high = expert_views(w_hi, L, e % SLOTS)
                    _, low = expert_views(w_lo, L, e % SLOTS)
                    if after(b, 1):
                        pe.wait_ge(s.e_sb, b)
                    pe.matmul(bank[6][:, 0:C], expert_sel[:, e, :], bias_rows[:, f.wide:f.wide + C],
                              start=True, stop=False)
                    for k in range(f.kt):
                        if k % half == 0:
                            pe.wait_ge(s.hT_lo, 2 * b + 1 + k // half)
                        mm = product(bank[6][:, 0:C], hT_hi[0:f.kh, k, :], hT_lo[0:f.kh, k, :], high[:, k, :],
                                     low[:, k, :], False, k == f.kt - 1)
                    mm.then_inc(s.e_mm, 1)

                def step(b):
                    if after(b, 1):
                        e_old = expert_of(b - 1)
                    e_new = expert_of(b + 1)
                    x_transpose(b + 1)
                    if after(b, 1):
                        second_product(b - 1, e_old)
                    h_transpose(b)
                    first_product(b + 1, e_new)

                blocks = block_count(pe)
                x_transpose(0)
                first_product(0, expert_of(0))
                step(0)
                step(1)
                steps(pe, 2, 1, blocks, step)
                e_old, e_last = expert_of(blocks - 2), expert_of(blocks - 1)
                x_transpose(blocks)
                second_product(blocks - 2, e_old)
                h_transpose(blocks - 1)
                second_product(blocks - 1, e_last)


_INS = ['x', 'L0_conv_W_qkv', 'L0_conv_W_proj', 'L0_conv_b_proj', 'L0_ffn_gate_w', 'L0_ffn_gate_b', 'L0_ffn_w1',
        'L0_ffn_b1', 'L0_ffn_w2', 'L0_ffn_b2', 'L1_conv_W_qkv', 'L1_conv_W_proj', 'L1_conv_b_proj',
        'L1_ffn_router_w', 'L1_ffn_W1', 'L1_ffn_b1', 'L1_ffn_W2', 'L1_ffn_b2']


def kernel(**inputs):
    import numpy as _np
    import concourse.bacc as _bacc
    from concourse import mybir as _mybir
    from concourse.bass_utils import run_bass_kernel_spmd as _run

    nc = _bacc.Bacc("TRN2", target_bir_lowering=False, num_devices=1)
    arrays, d = {}, {}
    for name in _INS:
        a = _np.ascontiguousarray(inputs[name])
        arrays[f"in_{name}_dram"] = a
        d[name] = nc.dram_tensor(f"in_{name}_dram", a.shape, _mybir.dt.from_np(a.dtype), kind="ExternalInput").ap()
    out = nc.dram_tensor("out_0_dram", (B, N, PIX, C), _mybir.dt.float32, kind="ExternalOutput").ap()
    conv_w = [(d[f'L{n}_conv_W_qkv'], d[f'L{n}_conv_W_proj'], d[f'L{n}_conv_b_proj']) for n in range(2)]
    ffn_w = [(d['L0_ffn_gate_w'], d['L0_ffn_gate_b'], d['L0_ffn_w1'], d['L0_ffn_b1'], d['L0_ffn_w2'], d['L0_ffn_b2']),
             (d['L1_ffn_router_w'], None, d['L1_ffn_W1'], d['L1_ffn_b1'], d['L1_ffn_W2'], d['L1_ffn_b2'])]
    metaformer(nc, d['x'], conv_w, ffn_w, out)
    r = _run(nc, [arrays], core_ids=[0])
    return r.results[0]["out_0_dram"]
```

```python
from contextlib import ExitStack

import concourse.bass as bass
from concourse import mybir

F32 = mybir.dt.float32
F32R = mybir.dt.float32r
BF16 = mybir.dt.bfloat16
I32 = mybir.dt.int32
ALU = mybir.AluOpType
ACT = mybir.ActivationFunctionType
AX = mybir.AxisListType

P = 128
B, N, PIX, C = 4, 24, 16, 256
BN = B * N
TOKENS = B * N * PIX
TILES = TOKENS // P
KC = C // P
HEADS, HD = 16, 16
HPH = P // HD
GROUP = 4
HGROUPS = HEADS // GROUP
NPT = P // PIX
E, TOPK = 8, 2
PAIRS = TILES * TOPK
ACT_TILES = 8
MAX_BLOCKS = (TOKENS * TOPK + E * (P - 1)) // P
MIN_BLOCKS = TOKENS * TOPK // P
TABLE = MAX_BLOCKS + 3
TAB = MAX_BLOCKS + MAX_BLOCKS % 2
ROW_CHUNKS = 4
BUSY_LOAD, BUSY_POOL, BUSY_NORM, BUSY_TOP, BUSY_LIST, BUSY_GATHER, BUSY_LAYER = 32, 8, 10, 4, 16, 12, 50
XT_BANKS = (0, 1, 2, 3, 4, 6)
SLOTS = 3
EARLY_LOW = 3
Y_BANKS = (4, 5, 0, 1, 2, 0)
PIECES = 4
NEG = -1.0e30
BIG_ROW = 4096

class Ffn:
    def __init__(self, wide, kt, kh, chunk):
        self.wide, self.kt, self.kh, self.chunk, self.chunks = wide, kt, kh, chunk, wide // chunk


FFN = [Ffn(wide=1024, kt=8, kh=128, chunk=512), Ffn(wide=1344, kt=6, kh=112, chunk=336)]
WORDS = [KC * f.wide + f.kt * C for f in FFN]
SLOT_WORDS = max(WORDS)
BIAS_WIDE = max(f.wide for f in FFN) + C
LN_EPS = (1e-6, 1e-5)


class LayerSems:

    def __init__(self, sem, L):
        self.x_in0 = sem(f"x_in0_{L}")
        self.x_in1 = sem(f"x_in1_{L}")
        self.x_in2 = sem(f"x_in2_{L}")
        self.conv_in = sem(f"conv_in_{L}")
        self.bias_in = sem(f"bias_in_{L}")
        self.route_in = sem(f"route_in_{L}")
        self.stat = sem(f"stat_{L}")
        self.var = sem(f"var_{L}")
        self.std = sem(f"std_{L}")
        self.rstd = sem(f"rstd_{L}")
        self.xn = sem(f"xn_{L}")
        self.xn_dve = sem(f"xn_dve_{L}")
        self.xnT_mm = sem(f"xnT_mm_{L}")
        self.xnT = sem(f"xnT_{L}")
        self.xnT_lo = sem(f"xnT_lo_{L}")
        self.xm = sem(f"xm_{L}")
        self.qk_mm = sem(f"qk_mm_{L}")
        self.k_sb = sem(f"k_sb_{L}")
        self.qm = sem(f"qm_{L}")
        self.s_mm = sem(f"s_mm_{L}")
        self.sub = sem(f"sub_{L}")
        self.expd = sem(f"expd_{L}")
        self.attn = sem(f"attn_{L}")
        self.v_mm = sem(f"v_mm_{L}")
        self.v = sem(f"v_{L}")
        self.aT_mm = sem(f"aT_mm_{L}")
        self.aT = sem(f"aT_{L}")
        self.av_mm = sem(f"av_mm_{L}")
        self.o_act = sem(f"o_act_{L}")
        self.o_dve = sem(f"o_dve_{L}")
        self.oT_mm = sem(f"oT_mm_{L}")
        self.y_mm = sem(f"y_mm_{L}")
        self.b_added = sem(f"b_added_{L}")
        self.var2 = sem(f"var2_{L}")
        self.std2 = sem(f"std2_{L}")
        self.xn2 = sem(f"xn2_{L}")
        self.xn2T_mm = sem(f"xn2T_mm_{L}")
        self.xn2T = sem(f"xn2T_{L}")
        self.lg_mm = sem(f"lg_mm_{L}")
        self.lg = sem(f"lg_{L}")
        self.chain = sem(f"chain_{L}")
        self.top2 = sem(f"top2_{L}")
        self.exp8 = sem(f"exp8_{L}")
        self.cnt_mm = sem(f"cnt_mm_{L}")
        self.blk_hot = sem(f"blk_hot_{L}")
        self.hot_rows = sem(f"hot_rows_{L}")
        self.hot_blk = sem(f"hot_blk_{L}")
        self.tab_mm = sem(f"tab_mm_{L}")
        self.tab = sem(f"tab_{L}")
        self.bias_cast = sem(f"bias_cast_{L}")
        self.bias_sub = sem(f"bias_sub_{L}")
        self.store = sem(f"store_{L}")
        self.gathered = sem(f"gathered_{L}")
        self.gcol = sem(f"gcol_{L}")
        self.scol = sem(f"scol_{L}")
        self.xT_mm = sem(f"xT_mm_{L}")
        self.xT_hi = sem(f"xT_hi_{L}")
        self.xT_lo = sem(f"xT_lo_{L}")
        self.h_mm = sem(f"h_mm_{L}")
        self.silu = sem(f"silu_{L}")
        self.h = sem(f"h_{L}")
        self.hT_mm = sem(f"hT_mm_{L}")
        self.hT_hi = sem(f"hT_hi_{L}")
        self.hT_lo = sem(f"hT_lo_{L}")
        self.e_mm = sem(f"e_mm_{L}")
        self.e_sb = sem(f"e_sb_{L}")
        self.added = sem(f"added_{L}")
        self.raw_ready = sem(f"raw_ready_{L}")
        self.first_in = sem(f"first_in_{L}")
        self.first_hi = sem(f"first_hi_{L}")
        self.pool_split = sem(f"pool_split_{L}")
        self.w_hi = sem(f"w_hi_{L}")
        self.w_lo = sem(f"w_lo_{L}")
        self.moe_done = sem(f"moe_done_{L}")
        self.rows_go = sem(f"rows_go_{L}")


def metaformer(nc, x, conv_w, ffn_w, out):
    with ExitStack() as ctx:
        def sb(name, shape, dt=F32):
            return ctx.enter_context(nc.sbuf_tensor(name, shape, dt))

        def sem(name):
            return ctx.enter_context(nc.semaphore(name))

        bank = [ctx.enter_context(nc.psum_tensor(f"bank{i}", [P, 512], F32)) for i in range(8)]

        w_hi = sb("w_hi", [P, SLOTS, SLOT_WORDS], F32R)
        w_lo = sb("w_lo", [P, SLOTS, SLOT_WORDS], F32R)
        raw = sb("raw", [P, 2, SLOT_WORDS])
        xres = sb("xres", [P, TILES, C])
        with nc.sbuf_tensor("region_a", [P, 4096], F32) as region_a:
            pass
        with nc.sbuf_tensor("onehot_blk", [P, PAIRS, 5, TAB], BF16) as onehot_blk:
            pass
        hT_hi = sb("hT_hi", [P, 8, P], F32R)
        hT_lo = sb("hT_lo", [P, 8, P], F32R)
        xT_hi = sb("xT_hi", [P, KC, P], F32R)
        xT_lo = sb("xT_lo", [P, KC, P], F32R)
        h_sb = sb("h_sb", [P, 1024])
        blk_hot = sb("blk_hot", [P, PAIRS, TAB], BF16)
        region_a_rest = sb("region_a_rest", [P, 4096 - 2 * 1024 - 2 * C - 1024 - PAIRS * TAB // 2])
        with nc.sbuf_tensor("region_b", [P, KC * TOKENS], F32) as region_b:
            pass
        expert_io = sb("expert_io", [P, KC * TOKENS - PAIRS * P // 2])
        onehot_row = sb("onehot_row", [P, PAIRS, P], BF16)
        with nc.sbuf_tensor("wv", [P, 2, KC, C], F32R) as wv:
            pass
        region_d = sb("region_d", [P, BIAS_WIDE])
        wqkv = sb("wqkv", [P, KC, 3 * C])
        wproj = sb("wproj", [P, KC, C])
        bproj = sb("bproj", [P, C])
        bias_rows = sb("bias_rows", [96, BIAS_WIDE], BF16)
        expert_sel = sb("expert_sel", [96, E, P], BF16)
        wroute = sb("wroute", [P, KC, E])
        broute = sb("broute", [P, E])

        xn = region_a[:, 0:TILES * C].rearrange("p (i c) -> p i c", i=TILES)
        probs = region_a[0:BN, 0:HEADS * BN].rearrange("p (h m) -> p h m", h=HEADS)
        qmask = region_a[:, 1536:1536 + HEADS * BN].rearrange("p (h n) -> p h n", h=HEADS)
        o_sb = region_a[0:BN, :].rearrange("p (q c) -> p q c", q=PIX)
        xnT_hi = w_hi[:, SLOTS - 1, 0:KC * TOKENS].rearrange("p (k t) -> p k t", k=KC)
        xnT_lo = w_lo[:, SLOTS - 1, 0:KC * TOKENS].rearrange("p (k t) -> p k t", k=KC)
        outT = region_b[:, :].rearrange("p (k n q) -> p k n q", k=KC, q=PIX)
        v_sb = raw[0:BN, 1, 0:4096].rearrange("p (q c) -> p q c", q=PIX)
        attnT = region_d[0:BN, 0:HEADS * BN].rearrange("p (h n) -> p h n", h=HEADS)
        bias_raw = region_d[0:96, :]
        kT = sb("kT", [P, KC, BN])
        xm = sb("xm", [P, TILES, KC, NPT])
        row_max = sb("row_max", [BN, HEADS])
        less_max = sb("less_max", [BN, HEADS])
        row_sum = sb("row_sum", [BN, HEADS])
        stats = sb("stats", [P, TILES, 6])
        mean_var = sb("mean_var", [P, TILES, 2])
        table_out = sb("table_out", [P, 4])
        std = sb("std", [P, TILES])
        rstd = sb("rstd", [P, TILES])
        less_mean = sb("less_mean", [P, TILES])
        xn2T = region_a[:, 0:4 * 512].rearrange("p (r i k t) -> p r i k t", r=4, i=2, k=KC)
        xn2 = raw[:, 1, 0:TILES * C].rearrange("p (i c) -> p i c", i=TILES)
        logits = sb("logits", [P, TILES, E])
        lg2 = sb("lg2", [P, TILES, E])
        prob8 = sb("prob8", [P, TILES, E])
        past_io = expert_io[:, 2 * C + FFN[1].chunk * 2:]
        cand = past_io[:, 0:TILES * E].rearrange("p (i e) -> p i e", i=TILES)
        m_top = sb("m_top", [P, TOPK, TILES])
        i_top = sb("i_top", [P, TOPK, TILES])
        pick = sb("pick", [P, TOPK, E, TILES])
        picked = sb("picked", [P, E, TILES], BF16)
        gate = sb("gate", [P, TOPK, TILES])
        gate_part = sb("gate_part", [P, 3, TOPK, TILES], BF16)
        small = sb("small", [P, 4, TILES])
        incl = sb("incl", [P, E, TILES])
        place = sb("place", [P, E, TILES])
        term = past_io[:, TILES * E:3 * TILES * E].rearrange("p (k e i) -> p k e i", k=TOPK, e=E)
        cnt_i = sb("cnt_i", [P, 2, E], I32)
        nblk = sb("nblk", [P, E])
        endblk = sb("endblk", [P, E])
        base = sb("base", [P, E])
        slot_f = sb("slot_f", [P, TOPK, TILES])
        slot_i = sb("slot_i", [P, 3, TOPK, TILES], I32)
        rowblk = sb("rowblk", [P, 2, PAIRS])
        blk_cmp = sb("blk_cmp", [1, 3, TABLE, E])
        blk_e = sb("blk_e", [1, 4, TABLE])
        tab_e = sb("tab_e", [1, TABLE], I32)
        tab_pieces = sb("tab_pieces", [1, TABLE], I32)
        tab_blocks = sb("tab_blocks", [1, 1], I32)
        id_sb = sb("id_sb", [P, 2, TAB])
        gather_tab = sb("gather_tab", [P, TABLE], I32)
        scatter_tab = sb("scatter_tab", [P, TABLE], I32)
        gate_tab = sb("gate_tab", [P, TABLE])
        xg = expert_io[:, 0:C]
        y_sb = expert_io[:, C:2 * C]
        silu_g = expert_io[:, 2 * C:2 * C + FFN[1].chunk * 2]
        gcol = sb("gcol", [P, 1], I32)
        scol = sb("scol", [P, 1], I32)
        ident = sb("ident", [P, P])
        q_mask = sb("q_mask", [P, HPH])
        in_batch = sb("in_batch", [B, BN], BF16)
        other_batch = sb("other_batch", [B, GROUP, BN], BF16)
        after_or_at = sb("after_or_at", [P, P], BF16)
        ones = sb("ones", [P, P], BF16)
        iota_i = sb("iota_i", [P, P], I32)
        iota = sb("iota", [P, P])
        expert_m8 = sb("expert_m8", [P, E])
        token_i = sb("token_i", [P, TILES], I32)
        token_id = sb("token_id", [P, 1])
        tile_first = sb("tile_first", [P, TILES])
        iota_bf = sb("iota_bf", [P, P], BF16)
        scan_keep = sb("scan_keep", [P, E, TILES])
        busy_in = sb("busy_in", [P, P], BF16)

        xn_dram = nc.dram_tensor("xn_dram", [TOKENS, C], F32).ap()
        mid_dram = nc.dram_tensor("mid_dram", [TOKENS, C], F32).ap()
        x_rows = x.rearrange("b n p c -> (b n p) c")
        out_rows = out.rearrange("b n p c -> (b n p) c")

        lay = [LayerSems(sem, L) for L in range(2)]
        made_seq = sem("made_seq")
        const_done = sem("const_done")
        busy_ready = sem("busy_ready")
        raw_dma = [sem(f"raw_dma{i}") for i in range(2)]

        block = ctx.enter_context(nc.Block())

        def pair_of(xT, j):
            return xT[:, :, 2 * j * P:2 * (j + 1) * P].rearrange("p k (i t) -> p i k t", i=2)

        def wait_xn(eng, s, tiles):
            eng.wait_ge(s.xn, min(tiles, ACT_TILES))
            if tiles > ACT_TILES:
                eng.wait_ge(s.xn_dve, tiles - ACT_TILES)

        def register(b):
            return not isinstance(b, int)

        def after(b, n):
            return register(b) or b >= n

        def col(tab, b):
            return tab[:, bass.ds(b, 1)] if register(b) else tab[:, b:b + 1]

        def blk_value(eng, v, value):
            return eng.tensor_tensor(onehot_blk[:, :, v, :].rearrange("p (k i) b -> p k i b", k=TOPK),
                                     blk_hot[:, :, :].rearrange("p (k i) b -> p k i b", k=TOPK),
                                     value.unsqueeze(3).to_broadcast([P, TOPK, TILES, TAB]), ALU.mult)

        def block_count(eng):
            return eng.value_load(tab_blocks[0:1, 0:1], min_val=0, max_val=MAX_BLOCKS - MIN_BLOCKS) + MIN_BLOCKS

        def steps(eng, begin, end_less, blocks, step):
            with eng.Fori(begin, MIN_BLOCKS - end_less) as b:
                step(b)
            with eng.Fori(MIN_BLOCKS - end_less, MAX_BLOCKS - end_less) as b:
                with eng.If(b + end_less < blocks):
                    step(b)
                with eng.Else():
                    eng.nop()

        def block_loop(eng, step, tab=None):
            blocks = block_count(eng)
            step(0)
            step(1)
            if tab is not None:
                eng.wait_ge(tab, 3)
            steps(eng, 2, 0, blocks, step)
            step(blocks, last=True)

        def piece_range(eng, b):
            if not after(b, 2):
                return None
            first = eng.value_load(col(tab_pieces, b - 2), min_val=0, max_val=PIECES * (E - SLOTS))
            end = eng.value_load(col(tab_pieces, b - 1), min_val=0, max_val=PIECES * (E - SLOTS))
            return first, end

        def for_pieces(eng, pieces, split):
            if pieces is None:
                return
            first, end = pieces

            def piece(i):
                with eng.If(first + i < end):
                    split(first + i)
                    if i + 1 < PIECES:
                        piece(i + 1)
                with eng.Else():
                    eng.nop()

            piece(0)

        def expert_views(w, L, slot):
            f = FFN[L]
            w1 = w[:, slot, 0:KC * f.wide].rearrange("p (k n) -> p k n", k=KC)
            w2 = w[0:f.kh, slot, KC * f.wide:KC * f.wide + f.kt * C].rearrange("p (k n) -> p k n", k=f.kt)
            return w1, w2

        @block.sync
        def _(sp):
            def load_x(L, src):
                v = src.rearrange("(i p) c -> p i c", p=P)
                for g, done in enumerate((lay[L].x_in0, lay[L].x_in1, lay[L].x_in2)):
                    sp.dma_start(xres[:, 4 * g:4 * g + 4, :], v[:, 4 * g:4 * g + 4, :]).then_inc(done, 16)

            def load_conv(L):
                w_qkv, w_proj, b_proj = conv_w[L]
                sp.dma_start(wqkv[:, :, :], w_qkv.rearrange("(k p) n -> p k n", p=P)).then_inc(lay[L].conv_in, 16)
                sp.dma_start(wproj[:, :, :], w_proj.rearrange("(k p) n -> p k n", p=P)).then_inc(lay[L].conv_in, 16)
                sp.dma_start(bproj[:, :], b_proj.partition_broadcast(P)).then_inc(lay[L].conv_in, 16)

            def load_route(L):
                router, router_b = ffn_w[L][0:2]
                sp.dma_start(wroute[:, :, :], router.rearrange("(k p) n -> p k n", p=P)).then_inc(lay[L].route_in, 16)
                if router_b is not None:
                    sp.dma_start(broute[:, :], router_b.partition_broadcast(P)).then_inc(lay[L].route_in, 16)

            def load_biases(L):
                f = FFN[L]
                for q in range(3):
                    for src, to in ((ffn_w[L][3], slice(0, f.wide)), (ffn_w[L][5], slice(f.wide, f.wide + C))):
                        sp.dma_start(bias_raw[32 * q:32 * q + E, to], src).then_inc(lay[L].bias_in, 16)

            def load_expert(L, e, half):
                f = FFN[L]
                w1, w2 = expert_views(raw, L, half)
                src1 = ffn_w[L][2][e].rearrange("(k p) n -> p k n", p=P)
                src2 = ffn_w[L][4][e].rearrange("(k p) n -> p k n", p=f.kh)
                kt2 = f.kt // 2
                for to, src, end in ((w1[:, 0, :], src1[:, 0, :], f.wide), (w1[:, 1, :], src1[:, 1, :], KC * f.wide),
                                     (w2[:, 0:kt2, :], src2[:, 0:kt2, :], KC * f.wide + kt2 * C),
                                     (w2[:, kt2:, :], src2[:, kt2:, :], WORDS[L])):
                    pieces = -(-end // (WORDS[L] // PIECES))
                    if e >= SLOTS + 2:
                        sp.wait_ge(lay[L].w_lo, PIECES * (e - 2) + pieces)
                    elif 1 <= e <= SLOTS:
                        sp.wait_ge(lay[L].pool_split, PIECES * (e - 1) + pieces)
                    sp.dma_start(to, src).then_inc(raw_dma[half], 16)
                    loads[half] += 1
                    if e < SLOTS:
                        sp.wait_ge(raw_dma[half], 16 * loads[half])
                        there = end // (WORDS[L] // PIECES)
                        for _ in range(there - handed[0]):
                            sp.sem_inc(lay[L].first_in, 1)
                        handed[0] = there % PIECES

            def expert_loaded(L, half):
                sp.wait_ge(raw_dma[half], 16 * loads[half])
                sp.sem_inc(lay[L].raw_ready, 1)

            loads = [0, 0]
            handed = [0]
            load_x(0, x_rows)
            load_conv(0)
            load_route(0)
            for L in range(2):
                s = lay[L]
                for e in range(SLOTS):
                    if e == SLOTS - 1:
                        sp.wait_ge(s.av_mm, 8)
                        if L == 0:
                            sp.wait_ge(const_done, 2)
                        load_biases(L)
                    if (L, e) != (1, 0):
                        load_expert(L, e, 0)
                dst = (mid_dram, out_rows)[L].rearrange("(i p) c -> p i c", p=P)
                xn_v = xn_dram.rearrange("(i p) c -> p i c", p=P)
                for g in range(3):
                    sp.wait_ge(s.xn2, 4 * (g + 1))
                    sp.dma_start(xn_v[:, 4 * g:4 * g + 4, :], xn2[:, 4 * g:4 * g + 4, :]).then_inc(s.store, 16)
                    sp.dma_start(dst[:, 4 * g:4 * g + 4, :], xres[:, 4 * g:4 * g + 4, :]).then_inc(s.store, 16)
                load_expert(L, SLOTS, 0)
                sp.wait_ge(s.store, 6 * 16)
                sp.wait_ge(s.xn2T_mm, 6)
                load_expert(L, SLOTS + 1, 1)
                expert_loaded(L, 0)
                if L == 0:
                    load_conv(1)
                    sp.wait_ge(s.lg, 1)
                    load_route(1)
                expert_loaded(L, 1)
                for e in range(SLOTS + 2, E):
                    load_expert(L, e, (e - SLOTS) % 2)
                    expert_loaded(L, (e - SLOTS) % 2)
                if L == 0:
                    sp.wait_ge(s.w_lo, PIECES * E)
                    load_expert(1, 0, 0)
                    sp.wait_ge(s.moe_done, 1)
                    load_x(1, mid_dram)
            sp.wait_ge(lay[1].moe_done, 1)

        @block.gpsimd
        def _(pool):
            cc = [0]

            def made(ins):
                cc[0] += 1
                ins.then_inc(made_seq, 1)
                pool.wait_ge(made_seq, cc[0])

            made(pool.memset(ident[:, :], 0.0))
            made(pool.affine_select(out=ident[:, :], in_=ident[:, :], compare_op=ALU.not_equal, fill=1.0, base=0,
                                    pattern=[[-1, P]], channel_multiplier=1))
            made(pool.memset(q_mask[:, :], float(HD) ** -0.5 / PIX ** 2))
            made(pool.affine_select(out=q_mask[:, :], in_=q_mask[:, :], compare_op=ALU.is_ge, fill=0.0, base=0,
                                    pattern=[[-HD, HPH]], channel_multiplier=1))
            made(pool.affine_select(out=q_mask[:, :], in_=q_mask[:, :], compare_op=ALU.is_ge, fill=0.0, base=HD - 1,
                                    pattern=[[HD, HPH]], channel_multiplier=-1))
            made(pool.memset(in_batch[:, :], 1.0))
            made(pool.affine_select(out=in_batch[:, :], in_=in_batch[:, :], compare_op=ALU.is_ge, fill=0.0,
                                    base=0, pattern=[[1, BN]], channel_multiplier=-N))
            made(pool.affine_select(out=in_batch[:, :], in_=in_batch[:, :], compare_op=ALU.is_ge, fill=0.0,
                                    base=N - 1, pattern=[[-1, BN]], channel_multiplier=N))
            made(pool.memset(other_batch[:, :, :], 0.0))
            made(pool.affine_select(out=other_batch[:, :, :], in_=other_batch[:, :, :], compare_op=ALU.is_ge, fill=NEG,
                                    base=0, pattern=[[0, GROUP], [1, BN]], channel_multiplier=-N))
            made(pool.affine_select(out=other_batch[:, :, :], in_=other_batch[:, :, :], compare_op=ALU.is_ge, fill=NEG,
                                    base=N - 1, pattern=[[0, GROUP], [-1, BN]], channel_multiplier=N))
            pool.sem_inc(const_done, 1)

            for L in range(2):
                s = lay[L]
                pool.wait_ge(s.conv_in, 48)
                if L == 1:
                    pool.wait_ge(lay[0].bias_cast, 4)
                pool.tensor_copy(wv[:, 0, :, :], wqkv[:, :, 2 * C:3 * C]).then_inc(s.b_added, 1)
                pool.wait_ge(s.b_added, 1)
                pool.tensor_tensor(wv[:, 1, :, :], wqkv[:, :, 2 * C:3 * C], wv[:, 0, :, :].bitcast(F32), ALU.subtract
                                   ).then_inc(s.b_added, 1)
                wait_xn(pool, s, TILES)
                for g in range(3):
                    tiles = slice(4 * g, 4 * g + 4)
                    pool.tensor_tensor(xres[:, tiles, :], xres[:, tiles, :],
                                       bproj[:, :].unsqueeze(1).to_broadcast([P, 4, C]), ALU.add).then_inc(s.b_added, 1)
                w = WORDS[L] // PIECES
                for q in range(PIECES * SLOTS):
                    if L == 0 and q == PIECES:
                        made(pool.memset(region_d[:, HEADS * BN:BIAS_WIDE], 0.0))
                        made(pool.memset(after_or_at[:, :], -1.0))
                        made(pool.affine_select(out=after_or_at[:, :], in_=after_or_at[:, :], compare_op=ALU.is_ge, fill=0.0,
                                                base=0, pattern=[[-1, P]], channel_multiplier=1))
                        made(pool.memset(ones[:, :], 1.0))
                        made(pool.iota(iota_i[:, :], pattern=[[1, P]], base=0, channel_multiplier=0))
                        made(pool.tensor_copy(iota[:, :], iota_i[:, :]))
                        made(pool.tensor_scalar(expert_m8[:, :], iota[:, 0:E], float(E), None, ALU.subtract))
                        made(pool.iota(token_i[:, :], pattern=[[P, TILES]], base=0, channel_multiplier=0))
                        made(pool.tensor_copy(tile_first[:, :], token_i[:, :]))
                        made(pool.iota(token_i[:, 0:1], pattern=[[0, 1]], base=1, channel_multiplier=1))
                        made(pool.tensor_copy(token_id[:, :], token_i[:, 0:1]))
                        made(pool.tensor_copy(iota_bf[:, :], iota_i[:, :]))
                        if SLOT_WORDS > WORDS[0]:
                            made(pool.memset(raw[:, :, WORDS[0]:SLOT_WORDS], 0.0))
                        made(pool.memset(gather_tab[:, TAB:TABLE], 0))
                        made(pool.memset(scan_keep[:, :, :], 1.0))
                        made(pool.memset(scan_keep[:, :, 0:1], 0.0))
                        made(pool.memset(expert_sel[:, :, :], 0.0))
                        for part in range(3):
                            made(pool.affine_select(out=expert_sel[:, :, :], in_=expert_sel[:, :, :], compare_op=ALU.not_equal,
                                                    fill=1.0, base=-32 * part, pattern=[[-1, E], [0, P]], channel_multiplier=1))
                        pool.sem_inc(const_done, 1)
                    if q == 2 * PIECES:
                        pool.wait_ge(s.bias_cast, 1)
                        pool.tensor_tensor(bias_raw[:, :], bias_raw[:, :], bias_rows[:, :], ALU.subtract).then_inc(s.bias_sub, 1)
                    e, at = q // PIECES, slice((q % PIECES) * w, (q % PIECES + 1) * w)
                    pool.wait_ge(s.first_hi, q + 1)
                    pool.tensor_tensor(w_lo[:, e, at], raw[:, 0, at], w_hi[:, e, at].bitcast(F32), ALU.subtract
                                       ).then_inc(s.pool_split, 1)
                pool.wait_ge(s.pool_split, PIECES * SLOTS)
                pool.wait_ge(s.bias_sub, 1)
                pool.wait_ge(s.bias_cast, 3)
                pool.tensor_tensor(bias_raw[64:96, :], bias_raw[64:96, :], bias_rows[64:96, :], ALU.subtract
                                   ).then_inc(s.bias_sub, 1)
                pool.wait_ge(s.bias_sub, 2)
                pool.wait_ge(s.blk_hot, 1)
                blk_value(nc.gpsimd, 1, tile_first[:, :].unsqueeze(1).to_broadcast([P, TOPK, TILES])
                          ).then_inc(s.hot_blk, 1)
                pool.wait_ge(s.hot_blk, 1)
                acc = (mid_dram, out_rows)[L]
                pool.wait_ge(s.store, 6 * 16)
                pool.wait_ge(s.tab, 1)

                def gather(b):
                    if after(b, 1):
                        pool.wait_ge(s.xT_mm, b)
                        pool.wait_ge(s.gathered, 16 * b)
                    if after(b, 1):
                        pool.tensor_copy(gcol[:, :], col(gather_tab, b)).then_inc(s.gcol, 1)
                        pool.wait_ge(s.gcol, b)
                        pool.sem_inc(s.rows_go, 1)
                    rows = gcol[:, :] if after(b, 1) else gather_tab[:, 0:1]
                    pool.indirect_dma_start(out=xg, out_offset=None, in_=xn_dram,
                                            in_offset=bass.IndirectOffsetOnAxis(ap=rows, axis=0)
                                            ).then_inc(s.gathered, 16)

                def scatter(b):
                    if after(b, 1):
                        pool.wait_ge(s.added, 16 * b)
                    pool.tensor_copy(scol[:, :], col(scatter_tab, b)).then_inc(s.scol, 1)
                    pool.wait_ge(s.scol, b + 1)
                    pool.wait_ge(s.e_sb, b + 1)
                    pool.sem_inc(s.rows_go, 1)
                    pool.indirect_dma_start(out=acc, out_offset=bass.IndirectOffsetOnAxis(ap=scol[:, :], axis=0),
                                            in_=y_sb, in_offset=None, bounds_check=TOKENS - 1,
                                            oob_is_err=False, compute_op=ALU.add).then_inc(s.added, 16)

                gather(0)
                pool.wait_ge(s.blk_hot, 2)
                for v in range(2):
                    blk_value(nc.gpsimd, 2 + v, gate_part[:, v, :, :]).then_inc(s.hot_blk, 1)
                    pool.wait_ge(s.hot_blk, v + 2)
                gather(1)
                pool.wait_ge(s.tab, 3)

                def step(b, last=False):
                    if not last:
                        gather(b + 2)
                    if after(b, 1):
                        scatter(b - 1)
                    if last:
                        pool.wait_ge(s.added, 16 * b)
                        pool.wait_ge(s.gathered, 16 * b + 32)
                        pool.sem_inc(s.moe_done, 1)

                block_loop(pool, step)

        @block.scalar
        def _(act):
            for L in range(2):
                s, f = lay[L], FFN[L]

                def deviations(var, g, done):
                    act.wait_ge(var, 4 * (g + 1))
                    nc.scalar.activation(std[:, 4 * g:4 * g + 4], mean_var[:, 4 * g:4 * g + 4, 1], ACT.Sqrt
                                         ).then_inc(done, 1)

                def first_high(p, end):
                    for q in range(p, end):
                        w = WORDS[L] // PIECES
                        at = slice((q % PIECES) * w, (q % PIECES + 1) * w)
                        act.wait_ge(s.first_in, q + 1)
                        nc.scalar.copy(w_hi[:, q // PIECES, at], raw[:, 0, at]).then_inc(s.first_hi, 1)

                for g in range(3):
                    deviations(s.var, g, s.std)
                    for i in range(4 * g - 4, 4 * g):
                        if 0 <= i < ACT_TILES:
                            act.wait_ge(s.rstd, g)
                            nc.scalar.activation(xn[:, i, :], xres[:, i, :], ACT.Identity,
                                                 bias=less_mean[:, i:i + 1], scale=rstd[:, i:i + 1]
                                                 ).then_inc(s.xn, 1)
                for j in range(6):
                    act.wait_ge(s.xnT_mm, j + 1)
                    nc.scalar.copy(pair_of(xnT_hi, j),
                                   bank[XT_BANKS[j]][:, :].rearrange("p (i k t) -> p i k t", i=2, k=KC)
                                   ).then_inc(s.xnT, 1)
                first_high(0, PIECES)
                for j in range(8):
                    if j in (1, 3, 5, 6):
                        g = (1, 3, 5, 6).index(j)
                        act.wait_ge(s.sub, g + 1)
                        for h in range(GROUP * g, GROUP * (g + 1)):
                            o = (h - GROUP * g) * BN
                            exps = nc.scalar.activation(probs[:, h, :], bank[g][0:BN, o:o + BN], ACT.Exp,
                                                        bias=less_max[:, h:h + 1], accum_out=row_sum[:, h:h + 1])
                        exps.then_inc(s.expd, 1)
                    act.wait_ge(s.v_mm, j + 1)
                    if L == 1 and j == 0:
                        act.wait_ge(lay[0].store, 96)
                    nc.scalar.copy(v_sb[:, 2 * j:2 * j + 2, :],
                                   bank[6 + j % 2][0:BN, :].rearrange("p (q c) -> p q c", q=2)).then_inc(s.v, 1)
                for g in range(HGROUPS):
                    act.wait_ge(s.aT_mm, g + 1)
                    nc.scalar.copy(attnT[:, GROUP * g:GROUP * g + GROUP, :],
                                   bank[4 + g % 2][0:BN, 0:GROUP * BN].rearrange("p (h n) -> p h n", h=GROUP)
                                   ).then_inc(s.aT, 1)
                first_high(PIECES, PIECES + 2)
                for j in range(0, 8, 2):
                    act.wait_ge(s.av_mm, j + 1)
                    if j == 0:
                        act.wait_ge(s.aT_mm, HGROUPS)
                    nc.scalar.copy(o_sb[:, :, 2 * HD * j:2 * HD * (j + 1)].rearrange("p q (h d) -> p h q d", h=2),
                                   bank[j % 4][0:BN, :].rearrange("p (h q d) -> p h q d", h=2, q=PIX)
                                   ).then_inc(s.o_act, 1)
                    if j < 4:
                        first_high(PIECES + 2 + j // 2, PIECES + 3 + j // 2)
                for j in range(0, 8, 2):
                    act.wait_ge(s.oT_mm, j + 1)
                    nc.scalar.copy(outT[:, j // 4, :, 4 * (j % 4):4 * (j % 4) + 4].rearrange("p n q -> p q n"),
                                   bank[4 + j % 4][:, 0:4 * BN].rearrange("p (q n) -> p q n", q=4)).then_inc(s.o_act, 1)
                act.wait_ge(s.bias_in, 6 * 16)
                if L == 1:
                    act.wait_ge(lay[0].moe_done, 1)
                nc.scalar.copy(bias_rows[:, :], bias_raw[:, :]).then_inc(s.bias_cast, 1)
                nc.scalar.activation(table_out[0:BN, 2 * L:2 * L + 1], row_sum[:, 0:1], ACT.Sqrt)
                first_high(2 * PIECES, 2 * PIECES + 1)
                deviations(s.var2, 0, s.std2)
                deviations(s.var2, 1, s.std2)
                for j in range(6):
                    if j == 2:
                        deviations(s.var2, 2, s.std2)
                    act.wait_ge(s.xn2T_mm, j + 1)
                    if j >= 4:
                        act.wait_ge(s.lg_mm, j - 3)
                    nc.scalar.copy(xn2T[:, j % 4, :, :, :],
                                   bank[4 + j % 4][:, :].rearrange("p (i k t) -> p i k t", i=2, k=KC)
                                   ).then_inc(s.xn2T, 1)
                    if j == 3:
                        first_high(2 * PIECES + 1, 2 * PIECES + 2)
                    if j == 5:
                        first_high(2 * PIECES + 2, 3 * PIECES)
                act.wait_ge(s.bias_sub, 1)
                nc.scalar.copy(bias_rows[32:64, :], bias_raw[32:64, :]).then_inc(s.bias_cast, 1)
                nc.scalar.copy(bias_rows[64:96, :], bias_raw[64:96, :]).then_inc(s.bias_cast, 1)
                act.wait_ge(s.xn2, TILES)
                nc.scalar.activation(table_out[:, 2 * L + 1:2 * L + 2], std[:, 0:1], ACT.Exp)
                act.wait_ge(s.top2, 1)
                if L == 0:
                    nc.scalar.activation(prob8[:, :, :], prob8[:, :, :], ACT.Exp).then_inc(s.exp8, 1)
                nc.scalar.activation(small[:, 0, :], small[:, 0, :], ACT.Exp).then_inc(s.exp8, 1)
                act.wait_ge(s.bias_sub, 2)
                nc.scalar.copy(bias_rows[64:96, :], bias_raw[64:96, :]).then_inc(s.bias_cast, 1)
                act.wait_ge(s.tab, 2)
                half = f.kt // 2

                def xT_high(b):
                    act.wait_ge(s.xT_mm, b + 1)
                    if after(b, 1):
                        act.wait_ge(s.h_mm, f.chunks * b)
                    nc.scalar.copy(xT_hi[:, :, :], bank[7][:, 0:C].rearrange("p (k s) -> p k s", k=KC)
                                   ).then_inc(s.xT_hi, 1)

                def split(q, b):
                    act.wait_ge(s.e_mm, b - 1)
                    act.wait_ge(s.raw_ready, q // PIECES + 1)
                    w = WORDS[L] // PIECES
                    at = bass.ds((q % PIECES) * w, w)
                    nc.scalar.copy(w_hi[:, (q // PIECES) % SLOTS, at], raw[:, (q // PIECES) % 2, at]
                                   ).then_inc(s.w_hi, 1)

                def step(b, last=False):
                    if not last:
                        pieces = piece_range(act, b)
                    if after(b, 1):
                        for j in range(2):
                            act.wait_ge(s.hT_mm, 2 * b - 1 + j)
                            if after(b, 2):
                                act.wait_ge(s.e_mm, b - 1)
                            nc.scalar.copy(hT_hi[0:f.kh, half * j:half * (j + 1), :],
                                           bank[4 + j][0:f.kh, 0:half * P].rearrange("p (k s) -> p k s", s=P)
                                           ).then_inc(s.hT_hi, 1)
                    if last:
                        return
                    for j in range(2):
                        act.wait_ge(s.h_mm, f.chunks * b + j + 1)
                        if L == 0:
                            if after(b, 1):
                                act.wait_ge(s.hT_mm, 2 * b)
                            nc.scalar.activation(h_sb[:, f.chunk * j:f.chunk * (j + 1)], bank[j][:, 0:f.chunk],
                                                 ACT.Silu).then_inc(s.h, 1)
                        else:
                            if after(b, 1):
                                act.wait_ge(s.h, 2 * b)
                            nc.scalar.activation(silu_g[:, f.chunk * j:f.chunk * (j + 1)], bank[j][:, 0:f.chunk],
                                                 ACT.Silu).then_inc(s.silu, 1)
                    xT_high(b + 1)
                    for_pieces(act, pieces, lambda q: split(q, b))

                xT_high(0)
                block_loop(act, step, s.tab)

        @block.vector
        def _(dve):
            nc.vector.memset(busy_in[:, :], 0.0).then_inc(busy_ready, 1)
            for L in range(2):
                s, f = lay[L], FFN[L]
                nchain = [0]

                def chain(ins):
                    nchain[0] += 1
                    ins.then_inc(s.chain, 1)
                    dve.wait_ge(s.chain, nchain[0])

                def stats_of(tiles, done, eps):
                    for i in tiles:
                        nc.vector.bn_stats(stats[:, i, :], xres[:, i, :]).then_inc(s.stat, 1)
                    dve.wait_ge(s.stat, nstat[0] + len(tiles))
                    nstat[0] += len(tiles)
                    for i in tiles:
                        nc.vector.bn_aggr(mean_var[:, i, :], stats[:, i, :]).then_inc(s.stat, 1)
                    nstat[0] += len(tiles)
                    dve.wait_ge(s.stat, nstat[0])
                    a, b = tiles[0], tiles[-1] + 1
                    nc.vector.tensor_scalar(mean_var[:, a:b, 1], mean_var[:, a:b, 1], eps, None,
                                            ALU.add).then_inc(done, len(tiles))

                def reciprocals(g, std_done):
                    dve.wait_ge(std_done, g + 1)
                    tiles = slice(4 * g, 4 * g + 4)
                    chain(nc.vector.reciprocal(rstd[:, tiles], std[:, tiles]))
                    nc.vector.scalar_tensor_tensor(out=less_mean[:, tiles], in0=mean_var[:, tiles, 0], scalar=-1.0,
                                                   in1=rstd[:, tiles], op0=ALU.mult, op1=ALU.mult).then_inc(s.rstd, 1)

                def normalise(i, dst, done):
                    nc.vector.tensor_scalar(dst[:, i, :], xres[:, i, :], mean_var[:, i, 0:1], rstd[:, i:i + 1],
                                            ALU.subtract, ALU.mult).then_inc(done, 1)

                nstat = [0]
                if L == 1:
                    dve.wait_ge(lay[0].std2, 3)
                    dve.wait_ge(lay[0].moe_done, 1)
                for g in range(4):
                    if g < 3:
                        dve.wait_ge((s.x_in0, s.x_in1, s.x_in2)[g], 16)
                        stats_of(range(4 * g, 4 * g + 4), s.var, LN_EPS[0])
                    if g >= 1:
                        reciprocals(g - 1, s.std)
                dve.wait_ge(s.rstd, 3)
                for i in range(ACT_TILES, TILES):
                    normalise(i, xn, s.xn_dve)
                if L == 0:
                    dve.wait_ge(const_done, 1)
                for j in range(6):
                    dve.wait_ge(s.xnT, j + 1)
                    nc.vector.tensor_reduce(xm[:, 2 * j:2 * j + 2, :, :].rearrange("p i k n -> p (i k n)"),
                                            bank[XT_BANKS[j]][:, :].rearrange("p (n q) -> p n q", q=PIX), AX.X, ALU.add
                                            ).then_inc(s.xm, 1)

                def low(j):
                    nc.vector.tensor_tensor(pair_of(xnT_lo, j),
                                            bank[XT_BANKS[j]][:, :].rearrange("p (i k t) -> p i k t", i=2, k=KC),
                                            pair_of(xnT_hi, j).bitcast(F32), ALU.subtract).then_inc(s.xnT_lo, 1)

                for j in range(EARLY_LOW):
                    low(j)
                dve.wait_ge(s.qk_mm, 1)
                qk = bank[5][:, 0:4 * BN].rearrange("p (v k n) -> p v k n", v=2, k=KC)
                nc.vector.tensor_copy(kT[:, :, :], qk[:, 1, :, :]).then_inc(s.k_sb, 1)
                for k in range(KC):
                    nc.vector.tensor_tensor(qmask[:, HPH * k:HPH * (k + 1), :],
                                            qk[:, 0, k, :].unsqueeze(1).to_broadcast([P, HPH, BN]),
                                            q_mask[:, :].unsqueeze(2).to_broadcast([P, HPH, BN]),
                                            ALU.mult).then_inc(s.qm, 1)
                for j in range(EARLY_LOW, 6):
                    low(j)
                def heads(g):
                    return slice(GROUP * g, GROUP * (g + 1))

                def sm_front(g):
                    dve.wait_ge(s.s_mm, g + 1)
                    chain(nc.vector.tensor_reduce(row_max[:, heads(g)], bank[g][0:BN, 0:GROUP * BN]
                                                  .rearrange("p (h m) -> p h m", h=GROUP), AX.X, ALU.max))
                    nc.vector.tensor_scalar(less_max[:, heads(g)], row_max[:, heads(g)], -1.0, None, ALU.mult
                                            ).then_inc(s.sub, 1)

                def sm_back(g):
                    dve.wait_ge(s.expd, g + 1)
                    chain(nc.vector.reciprocal(row_sum[:, heads(g)], row_sum[:, heads(g)]))
                    nc.vector.tensor_tensor(probs[:, heads(g), :], probs[:, heads(g), :],
                                            row_sum[:, heads(g)].unsqueeze(2).to_broadcast([BN, GROUP, BN]),
                                            ALU.mult).then_inc(s.attn, 1)

                dve.wait_ge(s.conv_in, 48)
                wait_xn(dve, s, TILES)
                for g in range(HGROUPS + 1):
                    if g < HGROUPS:
                        sm_front(g)
                    if g >= 1:
                        sm_back(g - 1)
                for j in range(1, 8, 2):
                    dve.wait_ge(s.av_mm, j + 1)
                    if j == 1:
                        dve.wait_ge(s.aT_mm, HGROUPS)
                    nc.vector.tensor_copy(o_sb[:, :, 2 * HD * j:2 * HD * (j + 1)].rearrange("p q (h d) -> p h q d", h=2),
                                          bank[j % 4][0:BN, :].rearrange("p (h q d) -> p h q d", h=2, q=PIX)
                                          ).then_inc(s.o_dve, 1)
                for j in range(1, 8, 2):
                    dve.wait_ge(s.oT_mm, j + 1)
                    nc.vector.tensor_copy(outT[:, j // 4, :, 4 * (j % 4):4 * (j % 4) + 4].rearrange("p n q -> p q n"),
                                          bank[4 + j % 4][:, 0:4 * BN].rearrange("p (q n) -> p q n", q=4)
                                          ).then_inc(s.o_dve, 1)
                dve.wait_ge(s.std, 3)
                wait_xn(dve, s, TILES)
                dve.wait_ge(s.av_mm, 8)
                dve.wait_ge(s.b_added, 2 + 3)

                def add_projected(j):
                    dve.wait_ge(s.y_mm, j + 1)
                    nc.vector.tensor_tensor(xres[:, 2 * j:2 * j + 2, :], xres[:, 2 * j:2 * j + 2, :],
                                            bank[Y_BANKS[j]][:, :].rearrange("p (i c) -> p i c", i=2), ALU.add
                                            ).then_inc(s.attn, 1)

                add_projected(0)
                for g in range(3):
                    tiles = slice(4 * g, 4 * g + 4)
                    add_projected(2 * g + 1)
                    dve.wait_ge(s.attn, HGROUPS + 2 * g + 2)
                    stats_of(range(4 * g, 4 * g + 4), s.var2, LN_EPS[1])
                    if g < 2:
                        add_projected(2 * g + 2)
                    dve.wait_ge(s.std2, g + 1)
                    chain(nc.vector.reciprocal(rstd[:, tiles], std[:, tiles]))
                    for i in range(4 * g, 4 * g + 4):
                        normalise(i, xn2, s.xn2)
                dve.wait_ge(s.lg_mm, 6)
                lgp = bank[3][:, 0:TILES * E].rearrange("p (i e) -> p i e", i=TILES)

                def tiles_bc(a):
                    return a.unsqueeze(2).to_broadcast([P, TILES, E])

                def experts_bc(a):
                    return a.unsqueeze(1).to_broadcast([P, TILES, E])

                if L == 0:
                    dve.wait_ge(const_done, 2)
                    nc.vector.tensor_tensor(logits[:, :, :], lgp, experts_bc(broute[:, :]), ALU.add).then_inc(s.lg, 1)
                else:
                    nc.vector.tensor_copy(logits[:, :, :], lgp).then_inc(s.lg, 1)
                dve.wait_ge(s.lg, 1)
                cur = logits
                for k in range(TOPK):
                    chain(nc.vector.tensor_reduce(m_top[:, k, :], cur[:, :, :], AX.X, ALU.max))
                    chain(nc.vector.tensor_tensor(cand[:, :, :], cur[:, :, :], tiles_bc(m_top[:, k, :]), ALU.is_equal))
                    chain(nc.vector.tensor_tensor(cand[:, :, :], cand[:, :, :], experts_bc(expert_m8[:, :]), ALU.mult))
                    chain(nc.vector.tensor_reduce(i_top[:, k, :], cand[:, :, :], AX.X, ALU.min))
                    chain(nc.vector.tensor_tensor(pick[:, k, :, :].rearrange("p e i -> p i e"),
                                                  experts_bc(expert_m8[:, :]), tiles_bc(i_top[:, k, :]), ALU.is_equal))
                    if k == 0:
                        chain(nc.vector.scalar_tensor_tensor(out=lg2[:, :, :],
                                                             in0=pick[:, 0, :, :].rearrange("p e i -> p i e"),
                                                             scalar=NEG, in1=logits[:, :, :],
                                                             op0=ALU.mult, op1=ALU.add))
                        cur = lg2
                if L == 0:
                    chain(nc.vector.tensor_tensor(prob8[:, :, :], logits[:, :, :], tiles_bc(m_top[:, 0, :]),
                                                  ALU.subtract))
                nc.vector.tensor_tensor(small[:, 0, :], m_top[:, 1, :], m_top[:, 0, :], ALU.subtract).then_inc(s.top2, 1)
                nc.vector.tensor_tensor(picked[:, :, :], pick[:, 0, :, :], pick[:, 1, :, :], ALU.add
                                        ).then_inc(s.top2, 1)
                dve.wait_ge(s.cnt_mm, 2)
                from_here = bank[4][:, 0:E * TILES].rearrange("p (e i) -> p e i", e=E)
                total = bank[4][:, E * TILES:2 * E * TILES].rearrange("p (e i) -> p e i", e=E)
                flat = "p e i -> p (e i)"
                chain(nc.vector.tensor_tensor_scan(incl[:, :, :].rearrange(flat), scan_keep[:, :, :].rearrange(flat),
                                                   total.rearrange(flat), 0.0, ALU.mult, ALU.add))
                chain(nc.vector.tensor_tensor(place[:, :, :], incl[:, :, :], from_here, ALU.add))
                chain(nc.vector.tensor_scalar(cnt_i[:, 0, :], incl[:, :, TILES - 1], float(P - 1), None, ALU.add))
                chain(nc.vector.tensor_scalar(cnt_i[:, 1, :], cnt_i[:, 0, :], 7, None, ALU.arith_shift_right))
                chain(nc.vector.tensor_scalar(nblk[:, :], cnt_i[:, 1, :], 1.0, None, ALU.max))
                chain(nc.vector.tensor_tensor_scan(endblk[:, :], scan_keep[:, 0, 1:1 + E], nblk[:, :], 0.0, ALU.mult, ALU.add))
                chain(nc.vector.tensor_tensor(base[:, :], endblk[:, :], nblk[:, :], ALU.subtract))
                chain(nc.vector.scalar_tensor_tensor(out=place[:, :, :], in0=base[:, :].unsqueeze(2)
                                                     .to_broadcast([P, E, TILES]), scalar=float(P),
                                                     in1=place[:, :, :], op0=ALU.mult, op1=ALU.add))
                chain(nc.vector.tensor_tensor(term[:, :, :, :], place[:, :, :].unsqueeze(1)
                                              .to_broadcast([P, TOPK, E, TILES]), pick[:, :, :, :], ALU.mult))
                chain(nc.vector.tensor_reduce(slot_f[:, :, :], term[:, :, :, :].rearrange("p k e i -> p k i e"),
                                              AX.X, ALU.add))
                chain(nc.vector.tensor_copy(slot_i[:, 0, :, :], slot_f[:, :, :]))
                chain(nc.vector.tensor_scalar(slot_i[:, 1, :, :], slot_i[:, 0, :, :], P - 1, None, ALU.bitwise_and))
                chain(nc.vector.tensor_scalar(slot_i[:, 2, :, :], slot_i[:, 0, :, :], 7, None, ALU.arith_shift_right))
                chain(nc.vector.tensor_copy(rowblk[:, :, :], slot_i[:, 1:3, :, :].rearrange("p v k i -> p v (k i)")))
                nc.vector.tensor_tensor(blk_hot[:, :, :],
                                        iota[:, 0:TAB].unsqueeze(1).to_broadcast([P, PAIRS, TAB]),
                                        rowblk[:, 1, :].unsqueeze(2).to_broadcast([P, PAIRS, TAB]),
                                        ALU.is_equal).then_inc(s.blk_hot, 1)
                dve.wait_ge(s.blk_hot, 1)
                nc.vector.tensor_scalar(onehot_blk[:, :, 0, :], blk_hot[:, :, :], token_id[:, :], None, ALU.mult
                                        ).then_inc(s.hot_rows, 1)
                dve.wait_ge(s.y_mm, 6)
                for j in range(PAIRS):
                    hot = nc.vector.tensor_scalar(onehot_row[:, j, :], iota_bf[:, :], rowblk[:, 0, j:j + 1], None,
                                                  ALU.is_equal)
                    if (j + 1) % (PAIRS // ROW_CHUNKS) == 0:
                        hot.then_inc(s.hot_rows, 1)
                dve.wait_ge(s.tab_mm, 1)
                tokp = bank[5][:, 0:2 * TAB].rearrange("p (v b) -> p v b", v=2)
                chain(nc.vector.tensor_scalar(id_sb[:, 0, :], tokp[:, 0, :], -1.0, None, ALU.add))
                chain(nc.vector.tensor_tensor(id_sb[:, 0, :], id_sb[:, 0, :], tokp[:, 1, :], ALU.add))
                nc.vector.tensor_scalar(gather_tab[:, 0:TAB], id_sb[:, 0, :], 0.0, None, ALU.max).then_inc(s.tab, 1)
                by_block = iota[0:1, 0:TABLE].unsqueeze(2).to_broadcast([1, TABLE, E])
                chain(nc.vector.tensor_tensor(blk_cmp[:, 0, :, :], by_block,
                                              endblk[0:1, :].unsqueeze(1).to_broadcast([1, TABLE, E]), ALU.is_ge))
                chain(nc.vector.tensor_reduce(blk_e[:, 0, :], blk_cmp[:, 0, :, :], AX.X, ALU.add))
                chain(nc.vector.tensor_scalar(tab_e[:, :], blk_e[:, 0, :], float(E - 1), None, ALU.min))
                nc.vector.tensor_scalar(tab_blocks[:, :], endblk[0:1, E - 1:E], -float(MIN_BLOCKS), None, ALU.add
                                        ).then_inc(s.tab, 1)
                if L == 0:
                    dve.wait_ge(s.exp8, 2)
                    chain(nc.vector.tensor_reduce(small[:, 1, :], prob8[:, :, :], AX.X, ALU.add))
                else:
                    dve.wait_ge(s.exp8, 1)
                    chain(nc.vector.tensor_scalar(small[:, 1, :], small[:, 0, :], 1.0, None, ALU.add))
                chain(nc.vector.reciprocal(gate[:, 0, :], small[:, 1, :]))
                chain(nc.vector.tensor_tensor(gate[:, 1, :], small[:, 0, :], gate[:, 0, :], ALU.mult))
                for v in range(2):
                    chain(nc.vector.tensor_copy(gate_part[:, v, :, :], gate[:, :, :]))
                    chain(nc.vector.tensor_tensor(gate[:, :, :], gate[:, :, :], gate_part[:, v, :, :], ALU.subtract))
                nc.vector.tensor_copy(gate_part[:, 2, :, :], gate[:, :, :]).then_inc(s.blk_hot, 1)

                dve.wait_ge(s.pool_split, PIECES * SLOTS)
                dve.sem_inc(s.w_lo, PIECES * SLOTS)
                half = f.kt // 2

                def xT_low(b):
                    dve.wait_ge(s.xT_hi, b + 1)
                    nc.vector.tensor_tensor(xT_lo[:, :, :], bank[7][:, 0:C].rearrange("p (k s) -> p k s", k=KC),
                                            xT_hi[:, :, :].bitcast(F32), ALU.subtract).then_inc(s.xT_lo, 1)

                def split(q):
                    dve.wait_ge(s.w_hi, q + 1)
                    w = WORDS[L] // PIECES
                    at = bass.ds((q % PIECES) * w, w)
                    slot = (q // PIECES) % SLOTS
                    nc.vector.tensor_tensor(w_lo[:, slot, at], raw[:, (q // PIECES) % 2, at],
                                            w_hi[:, slot, at].bitcast(F32), ALU.subtract).then_inc(s.w_lo, 1)

                xT_low(0)
                dve.wait_ge(s.blk_hot, 2)
                blk_value(nc.vector, 4, gate_part[:, 2, :, :]).then_inc(s.hot_rows, 1)
                chain(nc.vector.tensor_tensor(blk_cmp[:, 1, :, :], blk_cmp[:, 0, :, :],
                                              nblk[0:1, :].unsqueeze(1).to_broadcast([1, TABLE, E]), ALU.mult))
                chain(nc.vector.tensor_reduce(blk_e[:, 1, :], blk_cmp[:, 1, :, :], AX.X, ALU.add))
                chain(nc.vector.tensor_tensor(blk_e[:, 1, :], iota[0:1, 0:TABLE], blk_e[:, 1, :], ALU.subtract))
                chain(nc.vector.tensor_scalar(blk_e[:, 1, :], blk_e[:, 1, :], 1.0, float(PIECES), ALU.add, ALU.min))
                chain(nc.vector.tensor_scalar(nblk[0:1, :], endblk[0:1, :], 1.0, None, ALU.subtract))
                chain(nc.vector.tensor_tensor(blk_cmp[:, 2, :, :], by_block,
                                              nblk[0:1, :].unsqueeze(1).to_broadcast([1, TABLE, E]), ALU.is_equal))
                chain(nc.vector.tensor_reduce(blk_e[:, 2, :], blk_cmp[:, 2, :, :], AX.X, ALU.add))
                chain(nc.vector.scalar_tensor_tensor(out=blk_e[:, 1, :], in0=blk_e[:, 2, :], scalar=float(PIECES),
                                                     in1=blk_e[:, 1, :], op0=ALU.mult, op1=ALU.max))
                chain(nc.vector.scalar_tensor_tensor(out=blk_e[:, 1, :], in0=blk_e[:, 0, :], scalar=float(PIECES),
                                                     in1=blk_e[:, 1, :], op0=ALU.mult, op1=ALU.add))
                chain(nc.vector.tensor_scalar(blk_e[:, 1, :], blk_e[:, 1, :], -float(PIECES), 0.0, ALU.add, ALU.max))
                chain(nc.vector.tensor_scalar(tab_pieces[:, :], blk_e[:, 1, :], float(PIECES * (E - SLOTS)), None,
                                              ALU.min))
                chain(nc.vector.tensor_scalar(id_sb[:, 1, :], id_sb[:, 0, :], -1.0, float(BIG_ROW), ALU.is_equal, ALU.mult))
                chain(nc.vector.tensor_tensor(scatter_tab[:, 0:TAB], id_sb[:, 0, :], id_sb[:, 1, :], ALU.add))
                dve.wait_ge(s.tab_mm, 2)
                gatep = bank[6][:, 0:3 * TAB].rearrange("p (v b) -> p v b", v=3)
                chain(nc.vector.tensor_copy(id_sb[:, 1, :], gatep[:, 0, :]))
                chain(nc.vector.tensor_tensor(id_sb[:, 1, :], id_sb[:, 1, :], gatep[:, 1, :], ALU.add))
                nc.vector.tensor_tensor(gate_tab[:, 0:TAB], id_sb[:, 1, :], gatep[:, 2, :], ALU.add).then_inc(s.tab, 1)
                dve.wait_ge(s.tab, 3)

                def step(b, last=False):
                    if not last:
                        pieces = piece_range(dve, b)
                    if after(b, 1):
                        for j in range(2):
                            dve.wait_ge(s.hT_hi, 2 * b - 1 + j)
                            part = slice(half * j, half * (j + 1))
                            nc.vector.tensor_tensor(hT_lo[0:f.kh, part, :],
                                                    bank[4 + j][0:f.kh, 0:half * P].rearrange("p (k s) -> p k s", s=P),
                                                    hT_hi[0:f.kh, part, :].bitcast(F32), ALU.subtract
                                                    ).then_inc(s.hT_lo, 1)
                    if L == 1 and not last:
                        for j in range(2):
                            dve.wait_ge(s.silu, 2 * b + j + 1)
                            dve.wait_ge(s.h_mm, f.chunks * b + 3 + j)
                            nc.vector.tensor_tensor(h_sb[:, f.chunk * j:f.chunk * (j + 1)], bank[2 + j][:, 0:f.chunk],
                                                    silu_g[:, f.chunk * j:f.chunk * (j + 1)], ALU.mult
                                                    ).then_inc(s.h, 1)
                    if not last:
                        xT_low(b + 1)
                        for_pieces(dve, pieces, split)
                    if after(b, 1):
                        dve.wait_ge(s.e_mm, b)
                        if after(b, 2):
                            dve.wait_ge(s.added, 16 * (b - 1))
                        nc.vector.tensor_scalar(y_sb, bank[6][:, 0:C], col(gate_tab, b - 1), None,
                                                ALU.mult).then_inc(s.e_sb, 1)

                block_loop(dve, step)

        @block.tensor
        def _(pe):
            def product(out, hi, lo, w_high, w_low, first, last):
                pe.matmul(out, hi, w_high, start=first, stop=False)
                pe.matmul(out, hi, w_low, start=False, stop=False)
                return pe.matmul(out, lo, w_high, start=False, stop=last)

            def keep_busy(n, bank_no):
                for _ in range(n):
                    pe.matmul(bank[bank_no][:, :], busy_in[:, :],
                              busy_in[:, :].unsqueeze(1).to_broadcast([P, 512 // P, P]), start=True, stop=True)

            pe.wait_ge(busy_ready, 1)
            keep_busy(BUSY_LOAD, 7)
            pe.wait_ge(const_done, 1)
            for L in range(2):
                s, f = lay[L], FFN[L]
                for j in range(6):
                    wait_xn(pe, s, 2 * j + 2)
                    for i in range(2):
                        for k in range(KC):
                            mm = pe.transpose(bank[XT_BANKS[j]][:, (2 * i + k) * P:(2 * i + k + 1) * P],
                                              xn[:, 2 * j + i, k * P:(k + 1) * P], ident[:, :])
                    mm.then_inc(s.xnT_mm, 1)
                keep_busy(BUSY_POOL, 7)
                pe.wait_ge(s.xm, 6)
                pe.wait_ge(s.conv_in, 48)
                for v in range(2):
                    for m in range(KC):
                        for k in range(KC):
                            o = (KC * v + m) * BN
                            mm = pe.matmul(bank[5][:, o:o + BN], wqkv[:, k, v * C + m * P:v * C + (m + 1) * P],
                                           xm[:, :, k, :], start=(k == 0), stop=(k == KC - 1))
                mm.then_inc(s.qk_mm, 1)

                def values(j):
                    if j >= 2:
                        pe.wait_ge(s.v, j - 1)
                    for q in range(2):
                        for k in range(KC):
                            hi, lo = (xT[:, k, :].rearrange("p (n q) -> p q n", q=PIX)[:, 2 * j + q, :]
                                      for xT in (xnT_hi, xnT_lo))
                            mm = product(bank[6 + j % 2][0:BN, q * C:(q + 1) * C], hi, lo, wv[:, 0, k, :],
                                         wv[:, 1, k, :], k == 0, k == KC - 1)
                    mm.then_inc(s.v_mm, 1)

                pe.wait_ge(s.k_sb, 1)
                for g in range(HGROUPS):
                    pe.wait_ge(s.qm, g // 2 + 1)
                    pe.wait_ge(s.xnT_lo, g + 1)
                    pe.matmul(bank[g][0:BN, 0:GROUP * BN], in_batch[:, :],
                              other_batch[:, :, :].rearrange("p h m -> p (h m)"), start=True, stop=False)
                    for h in range(GROUP * g, GROUP * (g + 1)):
                        o = (h - GROUP * g) * BN
                        mm = pe.matmul(bank[g][0:BN, o:o + BN], qmask[:, h, :], kT[:, h // HPH, :],
                                       start=False, stop=(h % GROUP == GROUP - 1))
                    mm.then_inc(s.s_mm, 1)
                pe.wait_ge(s.xnT_lo, 6)
                pe.wait_ge(s.b_added, 2)
                for j in range(8):
                    values(j)
                for g in range(HGROUPS):
                    pe.wait_ge(s.attn, g + 1)
                    if g >= 2:
                        pe.wait_ge(s.aT, g - 1)
                    for h in range(GROUP * g, GROUP * (g + 1)):
                        o = (h - GROUP * g) * BN
                        mm = pe.transpose(bank[4 + g % 2][0:BN, o:o + BN], probs[:, h, :], ident[0:BN, 0:BN])
                    mm.then_inc(s.aT_mm, 1)
                pe.wait_ge(s.v, 8)
                for j in range(8):
                    pe.wait_ge(s.aT, j // 2 + 1)
                    if j >= 4:
                        pe.wait_ge((s.o_act, s.o_dve)[j % 2], (j - 4) // 2 + 1)
                    for h in (2 * j, 2 * j + 1):
                        o = (h - 2 * j) * C
                        mm = pe.matmul(bank[j % 4][0:BN, o:o + C], attnT[:, h, :], v_sb[:, :, h * HD:(h + 1) * HD],
                                       start=True, stop=True)
                    mm.then_inc(s.av_mm, 1)
                pe.wait_ge(s.o_act, 4)
                pe.wait_ge(s.o_dve, 4)
                for j in range(8):
                    k, q0 = j // 4, 4 * (j % 4)
                    if j >= 4:
                        pe.wait_ge((s.o_act, s.o_dve)[j % 2], 4 + (j - 4) // 2 + 1)
                    for q in range(4):
                        mm = pe.transpose(bank[4 + j % 4][:, q * BN:(q + 1) * BN], o_sb[:, q0 + q, k * P:(k + 1) * P],
                                          ident[0:BN, 0:BN])
                    mm.then_inc(s.oT_mm, 1)
                pe.wait_ge(s.o_act, 8)
                pe.wait_ge(s.o_dve, 8)
                for j in range(6):
                    if j == 5:
                        pe.wait_ge(s.attn, HGROUPS + 3)
                    for i in range(2):
                        n = NPT * (2 * j + i)
                        for k in range(KC):
                            mm = pe.matmul(bank[Y_BANKS[j]][:, i * C:(i + 1) * C], outT[:, k, n:n + NPT, :], wproj[:, k, :],
                                           start=(k == 0), stop=(k == KC - 1))
                    mm.then_inc(s.y_mm, 1)
                pe.wait_ge(s.route_in, 32 if L == 0 else 16)

                def route(j):
                    pe.wait_ge(s.xn2T, j + 1)
                    for i in range(2):
                        for k in range(KC):
                            o = (2 * j + i) * E
                            mm = pe.matmul(bank[3][:, o:o + E], xn2T[:, j % 4, i, k, :], wroute[:, k, :],
                                           start=(k == 0), stop=(k == KC - 1))
                    mm.then_inc(s.lg_mm, 1)

                for j in range(6):
                    if j == 2:
                        keep_busy(BUSY_NORM, 7)
                    pe.wait_ge(s.xn2, 2 * j + 2)
                    if j >= 4:
                        pe.wait_ge(s.xn2T, j - 3)
                    for i in range(2):
                        for k in range(KC):
                            mm = pe.transpose(bank[4 + j % 4][:, (2 * i + k) * P:(2 * i + k + 1) * P],
                                              xn2[:, 2 * j + i, k * P:(k + 1) * P], ident[:, :])
                    mm.then_inc(s.xn2T_mm, 1)
                    if j >= 1:
                        route(j - 1)
                route(5)
                keep_busy(BUSY_TOP, 0)
                pe.wait_ge(s.top2, 2)
                if L == 0:
                    pe.wait_ge(const_done, 2)
                for n, m in ((0, after_or_at), (1, ones)):
                    pe.matmul(bank[4][:, n * E * TILES:(n + 1) * E * TILES], m[:, :],
                              picked[:, :, :].rearrange("p e i -> p (e i)"), start=True, stop=True
                              ).then_inc(s.cnt_mm, 1)
                keep_busy(BUSY_LIST, 0)
                pe.wait_ge(s.hot_blk, 1)
                for j in range(PAIRS):
                    if j % (PAIRS // ROW_CHUNKS) == 0:
                        pe.wait_ge(s.hot_rows, j // (PAIRS // ROW_CHUNKS) + 2)
                    mm = pe.matmul(bank[5][:, 0:2 * TAB], onehot_row[:, j, :],
                                   onehot_blk[:, j, 0:2, :].rearrange("p v b -> p (v b)"),
                                   start=(j == 0), stop=(j == PAIRS - 1))
                mm.then_inc(s.tab_mm, 1)
                keep_busy(BUSY_GATHER, 0)
                pe.wait_ge(s.bias_cast, 4)
                pe.wait_ge(s.tab, 2)

                def x_transpose(b):
                    pe.wait_ge(s.gathered, 16 * b + 16)
                    if after(b, 1):
                        pe.wait_ge(s.xT_lo, b)
                    for k in range(KC):
                        mm = pe.transpose(bank[7][:, k * P:(k + 1) * P], xg[:, k * P:(k + 1) * P], ident[:, :])
                    mm.then_inc(s.xT_mm, 1)

                half = f.kt // 2
                order = (0, 1) if L == 0 else (2, 3, 0, 1)

                def expert_of(b):
                    return pe.value_load(col(tab_e, b), min_val=0, max_val=E - 1)

                def first_product(b, e):
                    pe.wait_ge(s.xT_lo, b + 1)
                    pe.wait_ge(s.w_lo, e * PIECES + PIECES)
                    high, _ = expert_views(w_hi, L, e % SLOTS)
                    low, _ = expert_views(w_lo, L, e % SLOTS)
                    for n, c in enumerate(order):
                        cs = slice(c * f.chunk, (c + 1) * f.chunk)
                        pe.matmul(bank[n][:, 0:f.chunk], expert_sel[:, e, :], bias_rows[:, cs],
                                  start=True, stop=False)
                        for k in range(KC):
                            mm = product(bank[n][:, 0:f.chunk], xT_hi[:, k, :], xT_lo[:, k, :], high[:, k, cs],
                                         low[:, k, cs], False, k == KC - 1)
                        mm.then_inc(s.h_mm, 1)

                def h_transpose(b):
                    for j in range(2):
                        pe.wait_ge(s.h, 2 * b + 1 + j)
                        if after(b, 1):
                            pe.wait_ge(s.hT_lo, 2 * b - 1 + j)
                        for k in range(half):
                            o = (j * half + k) * f.kh
                            mm = pe.transpose(bank[4 + j][0:f.kh, k * P:(k + 1) * P], h_sb[:, o:o + f.kh],
                                              ident[:, :])
                        mm.then_inc(s.hT_mm, 1)

                def second_product(b, e):
                    _, high = expert_views(w_hi, L, e % SLOTS)
                    _, low = expert_views(w_lo, L, e % SLOTS)
                    if after(b, 1):
                        pe.wait_ge(s.e_sb, b)
                    pe.matmul(bank[6][:, 0:C], expert_sel[:, e, :], bias_rows[:, f.wide:f.wide + C],
                              start=True, stop=False)
                    for k in range(f.kt):
                        if k % half == 0:
                            pe.wait_ge(s.hT_lo, 2 * b + 1 + k // half)
                        mm = product(bank[6][:, 0:C], hT_hi[0:f.kh, k, :], hT_lo[0:f.kh, k, :], high[:, k, :],
                                     low[:, k, :], False, k == f.kt - 1)
                    mm.then_inc(s.e_mm, 1)

                def step(b):
                    if after(b, 1):
                        e_old = expert_of(b - 1)
                    e_new = expert_of(b + 1)
                    x_transpose(b + 1)
                    if after(b, 1):
                        second_product(b - 1, e_old)
                    h_transpose(b)
                    first_product(b + 1, e_new)

                blocks = block_count(pe)
                x_transpose(0)
                first_product(0, expert_of(0))
                pe.wait_ge(s.hot_blk, 3)
                pe.wait_ge(s.hot_rows, ROW_CHUNKS + 2)
                for j in range(PAIRS):
                    mm = pe.matmul(bank[6][:, 0:3 * TAB], onehot_row[:, j, :],
                                   onehot_blk[:, j, 2:5, :].rearrange("p v b -> p (v b)"),
                                   start=(j == 0), stop=(j == PAIRS - 1))
                mm.then_inc(s.tab_mm, 1)
                step(0)
                pe.wait_ge(s.tab, 3)
                step(1)
                steps(pe, 2, 1, blocks, step)
                e_old, e_last = expert_of(blocks - 2), expert_of(blocks - 1)
                x_transpose(blocks)
                second_product(blocks - 2, e_old)
                h_transpose(blocks - 1)
                second_product(blocks - 1, e_last)
                if L == 0:
                    keep_busy(BUSY_LAYER, 3)


_INS = ['x', 'L0_conv_W_qkv', 'L0_conv_W_proj', 'L0_conv_b_proj', 'L0_ffn_gate_w', 'L0_ffn_gate_b', 'L0_ffn_w1',
        'L0_ffn_b1', 'L0_ffn_w2', 'L0_ffn_b2', 'L1_conv_W_qkv', 'L1_conv_W_proj', 'L1_conv_b_proj',
        'L1_ffn_router_w', 'L1_ffn_W1', 'L1_ffn_b1', 'L1_ffn_W2', 'L1_ffn_b2']


def kernel(**inputs):
    import numpy as _np
    import concourse.bacc as _bacc
    from concourse import mybir as _mybir
    from concourse.bass_utils import run_bass_kernel_spmd as _run

    nc = _bacc.Bacc("TRN2", target_bir_lowering=False, num_devices=1)
    arrays, d = {}, {}
    for name in _INS:
        a = _np.ascontiguousarray(inputs[name])
        arrays[f"in_{name}_dram"] = a
        d[name] = nc.dram_tensor(f"in_{name}_dram", a.shape, _mybir.dt.from_np(a.dtype), kind="ExternalInput").ap()
    out = nc.dram_tensor("out_0_dram", (B, N, PIX, C), _mybir.dt.float32, kind="ExternalOutput").ap()
    conv_w = [(d[f'L{n}_conv_W_qkv'], d[f'L{n}_conv_W_proj'], d[f'L{n}_conv_b_proj']) for n in range(2)]
    ffn_w = [(d['L0_ffn_gate_w'], d['L0_ffn_gate_b'], d['L0_ffn_w1'], d['L0_ffn_b1'], d['L0_ffn_w2'], d['L0_ffn_b2']),
             (d['L1_ffn_router_w'], None, d['L1_ffn_W1'], d['L1_ffn_b1'], d['L1_ffn_W2'], d['L1_ffn_b2'])]
    metaformer(nc, d['x'], conv_w, ffn_w, out)
    r = _run(nc, [arrays], core_ids=[0])
    return r.results[0]["out_0_dram"]
```
